# Optimizing a Trainium2 kernel written in Bass

```python
import numpy as np
import jax
import jax.numpy as jnp

def _softmax(x, axis=-1):
    return jax.nn.softmax(x, axis=axis)

def _gelu(x):
    return jax.nn.gelu(x, approximate=True)

def _silu(x):
    return jax.nn.silu(x)

def _sigmoid(x):
    return jax.nn.sigmoid(x)

def _layernorm(x, axis=-1, eps=1e-05):
    m = jnp.mean(x, axis=axis, keepdims=True)
    v = jnp.var(x, axis=axis, keepdims=True)
    return (x - m) / jnp.sqrt(v + eps)

def _scatter_add(tgt, idx, src, axis=0):
    return tgt.at[idx].add(src)

def _segment_sum(src, seg, n):
    return jax.ops.segment_sum(src, seg, n)
kernel_name = 'mk_xattn_ffn_d4_seqx_r4_36b206'

def setup_inputs(seed: int=0):
    np.random.seed(seed)
    _w = jnp.asarray

    def _rec_inputs():
        import jax
        import jax.numpy as jnp
        _rk = jax.random.key(seed)
        x = -0.0002928 + 1 * jax.random.normal(jax.random.fold_in(_rk, 1), (2, 512, 256), jnp.float32)
        _lenS = 512 - jax.random.randint(jax.random.fold_in(_rk, 7), (2,), 0, max(1, 512 // 4) + 1, jnp.int32)
        _lenS2 = 1024 - jax.random.randint(jax.random.fold_in(_rk, 8), (2,), 0, max(1, 1024 // 4) + 1, jnp.int32)
        _ctx_1024P = jax.random.normal(jax.random.fold_in(_rk, 11), (2, 16, 256), jnp.float32)
        _ctx_1024c = jax.random.dirichlet(jax.random.fold_in(_rk, 511), 0.3 * jnp.ones((16,), jnp.float32), (2, 1024))
        _ctx_1024t = jnp.einsum('bsk,bkd->bsd', _ctx_1024c, _ctx_1024P)
        _ctx_1024t = _ctx_1024t * jax.lax.rsqrt(jnp.mean(jnp.square(_ctx_1024t)) + 1e-12) * 0.953939
        ctx_1024 = -1.39393e-06 + 0.999914 * (_ctx_1024t + 0.3 * jax.random.normal(jax.random.fold_in(_rk, 611), (2, 1024, 256), jnp.float32))
        _validS = jnp.arange(512)[None, :] < _lenS[:, None]
        _validS2 = jnp.arange(1024)[None, :] < _lenS2[:, None]
        _causal = jnp.tril(jnp.ones((512, 512), dtype=bool))
        mask_BxSxS2_if1 = jnp.where(jnp.ones((2, 512, 1024), dtype=bool), 1, 0).astype(jnp.int32)
        mask_Bx1xSxS2_bk1 = jnp.broadcast_to(_validS2[:, None, None, :], (2, 1, 512, 1024))
        return (x, ctx_1024, mask_BxSxS2_if1, mask_Bx1xSxS2_bk1)
    x, ctx_1024, mask_BxSxS2_if1, mask_Bx1xSxS2_bk1 = _rec_inputs()

    def _L0_xattn_setup():
        import jax, jax.numpy as jnp
        import numpy as np
        B, M, N = (2, 512, 512)
        D_MODEL = 256
        H, DH = (16, 64)
        key = jax.random.key(seed)
        ks = jax.random.split(key, 12)
        s = D_MODEL ** (-0.5)
        return {'queries': jax.random.normal(ks[0], (B, M, D_MODEL), jnp.float32), 'keys': jax.random.normal(ks[1], (B, N, D_MODEL), jnp.float32), 'values': jax.random.normal(ks[2], (B, N, D_MODEL), jnp.float32), 'Wq': jax.random.normal(ks[3], (H * DH, D_MODEL), jnp.float32) * s, 'bq': jnp.zeros((H * DH,), jnp.float32), 'Wk': jax.random.normal(ks[4], (H * DH, D_MODEL), jnp.float32) * s, 'bk': jnp.zeros((H * DH,), jnp.float32), 'Wv': jax.random.normal(ks[5], (H * DH, D_MODEL), jnp.float32) * s, 'bv': jnp.zeros((H * DH,), jnp.float32), 'Wo': jax.random.normal(ks[6], (D_MODEL, H * DH), jnp.float32) * s, 'bo': jnp.zeros((D_MODEL,), jnp.float32)}
    _L0_xattn_all = _L0_xattn_setup()
    _L0_xattn_in = {k: v for k, v in _L0_xattn_all.items() if k in ('Wq', 'bq', 'Wk', 'bk', 'Wv', 'bv', 'Wo', 'bo')}
    del _L0_xattn_all

    def _L0_ffn_setup():
        import jax, jax.numpy as jnp
        import numpy as np
        TOP_K = 2
        EPS = 1e-09
        key = jax.random.key(seed)
        ks = jax.random.split(key, 6)
        B, T, D, H, E = (4, 512, 256, 512, 8)
        x = jax.random.normal(ks[0], (B, T, D), dtype=jnp.float32)
        Wg = jax.random.normal(ks[1], (E, D), dtype=jnp.float32) * 0.02
        W1 = jax.random.normal(ks[2], (E, 2 * H, D), dtype=jnp.float32) * 0.02
        b1 = jax.random.normal(ks[3], (E, 2 * H), dtype=jnp.float32) * 0.02
        Wo = jax.random.normal(ks[4], (D, H), dtype=jnp.float32) * 0.02
        bo = jax.random.normal(ks[5], (D,), dtype=jnp.float32) * 0.02
        return {'x': x, 'Wg': Wg, 'W1': W1, 'b1': b1, 'Wo': Wo, 'bo': bo}
    _L0_ffn_all = _L0_ffn_setup()
    _L0_ffn_in = {k: v for k, v in _L0_ffn_all.items() if k in ('Wg', 'W1', 'b1', 'Wo', 'bo')}
    del _L0_ffn_all

    def _L1_xattn_setup():
        import jax, jax.numpy as jnp
        import numpy as np
        B, S, H = (4, 512, 256)
        key = jax.random.key(seed)
        ks = jax.random.split(key, 12)
        scale = 1.0 / np.sqrt(H)
        inp = {'query': jax.random.normal(ks[0], (B, S, H), jnp.float32), 'key': jax.random.normal(ks[1], (B, S, H), jnp.float32), 'value': jax.random.normal(ks[2], (B, S, H), jnp.float32), 'mask': jnp.ones((B, S, S), jnp.int32), 'Wq': jax.random.normal(ks[3], (H, H), jnp.float32) * scale, 'bq': jnp.zeros((H,), jnp.float32), 'Wk': jax.random.normal(ks[4], (H, H), jnp.float32) * scale, 'bk': jnp.zeros((H,), jnp.float32), 'Wv': jax.random.normal(ks[5], (H, H), jnp.float32) * scale, 'bv': jnp.zeros((H,), jnp.float32), 'Wo': jax.random.normal(ks[6], (H, H), jnp.float32) * scale, 'bo': jnp.zeros((H,), jnp.float32)}
        return inp
    _L1_xattn_all = _L1_xattn_setup()
    _L1_xattn_in = {k: v for k, v in _L1_xattn_all.items() if k in ('Wq', 'bq', 'Wk', 'bk', 'Wv', 'bv', 'Wo', 'bo')}
    del _L1_xattn_all

    def _L1_ffn_setup():
        import jax, jax.numpy as jnp
        import numpy as np
        EMB = 256
        FF = 4 * EMB

        def _ternary(w):
            scale = jnp.maximum(jnp.mean(jnp.abs(w)), 1e-08)
            w_t = jnp.clip(jnp.round(w / scale), -1.0, 1.0)
            return w + jax.lax.stop_gradient(w_t - w)
        key = jax.random.key(seed)
        kx, k1, k2, kb1, kb2 = jax.random.split(key, 5)
        x = jax.random.normal(kx, (4, 512, EMB), dtype=jnp.float32)
        lim1 = 1.0 / np.sqrt(EMB)
        lim2 = 1.0 / np.sqrt(FF)
        W1 = jax.random.uniform(k1, (FF, EMB), jnp.float32, -lim1, lim1)
        b1 = jax.random.uniform(kb1, (FF,), jnp.float32, -lim1, lim1)
        W2 = jax.random.uniform(k2, (EMB, FF), jnp.float32, -lim2, lim2)
        b2 = jax.random.uniform(kb2, (EMB,), jnp.float32, -lim2, lim2)
        return {'x': x, 'W1': W1, 'b1': b1, 'W2': W2, 'b2': b2}
    _L1_ffn_all = _L1_ffn_setup()
    _L1_ffn_in = {k: v for k, v in _L1_ffn_all.items() if k in ('W1', 'b1', 'W2', 'b2')}
    del _L1_ffn_all

    def _L2_xattn_setup():
        import jax, jax.numpy as jnp
        import numpy as np
        B, S, D, H = (4, 512, 256, 16)
        HD = D // H
        key = jax.random.key(seed)
        ks = jax.random.split(key, 12)
        scale = 1.0 / np.sqrt(D)
        inp = {'queries': jax.random.normal(ks[0], (B, S, D), jnp.float32), 'keys': jax.random.normal(ks[1], (B, S, D), jnp.float32), 'values': jax.random.normal(ks[2], (B, S, D), jnp.float32), 'mask': jax.random.randint(ks[3], (B, 1, S, S), 0, 2).astype(bool), 'Wq': jax.random.normal(ks[4], (D, D), jnp.float32) * scale, 'bq': jnp.zeros((D,), jnp.float32), 'Wk': jax.random.normal(ks[5], (D, D), jnp.float32) * scale, 'bk': jnp.zeros((D,), jnp.float32), 'Wv': jax.random.normal(ks[6], (D, D), jnp.float32) * scale, 'bv': jnp.zeros((D,), jnp.float32), 'Wo': jax.random.normal(ks[7], (D, D), jnp.float32) * scale, 'bo': jnp.zeros((D,), jnp.float32)}
        return inp
    _L2_xattn_all = _L2_xattn_setup()
    _L2_xattn_in = {k: v for k, v in _L2_xattn_all.items() if k in ('Wq', 'bq', 'Wk', 'bk', 'Wv', 'bv', 'Wo', 'bo')}
    del _L2_xattn_all

    def _L2_ffn_setup():
        import jax, jax.numpy as jnp
        import numpy as np
        B, S, D, E = (2, 1024, 256, 8)
        key = jax.random.key(seed)
        ks = jax.random.split(key, 7)
        s = 1.0 / np.sqrt(D)
        return {'x': jax.random.normal(ks[0], (B, S, D), jnp.float32), 'Ws': jax.random.normal(ks[1], (E, D), jnp.float32) * s, 'bs': jax.random.normal(ks[2], (E,), jnp.float32) * s, 'W1': jax.random.normal(ks[3], (E, D, D), jnp.float32) * s, 'b1': jax.random.normal(ks[4], (E, D), jnp.float32) * s, 'W2': jax.random.normal(ks[5], (E, D, D), jnp.float32) * s, 'b2': jax.random.normal(ks[6], (E, D), jnp.float32) * s}
    _L2_ffn_all = _L2_ffn_setup()
    _L2_ffn_in = {k: v for k, v in _L2_ffn_all.items() if k in ('Ws', 'bs', 'W1', 'b1', 'W2', 'b2')}
    del _L2_ffn_all

    def _L3_xattn_setup():
        import jax, jax.numpy as jnp
        import numpy as np
        HEADS = 16
        DIM_HEAD = 64
        QUERY_DIM = 256
        INNER = HEADS * DIM_HEAD
        SCALE = DIM_HEAD ** (-0.5)
        key = jax.random.key(seed)
        ks = jax.random.split(key, 6)
        B, N, M = (2, 512, 512)
        x = jax.random.normal(ks[0], (B, N, QUERY_DIM), dtype=jnp.float32)
        context = jax.random.normal(ks[1], (B, M, QUERY_DIM), dtype=jnp.float32)
        s = QUERY_DIM ** (-0.5)
        Wq = jax.random.normal(ks[2], (QUERY_DIM, INNER), dtype=jnp.float32) * s
        Wk = jax.random.normal(ks[3], (QUERY_DIM, INNER), dtype=jnp.float32) * s
        Wv = jax.random.normal(ks[4], (QUERY_DIM, INNER), dtype=jnp.float32) * s
        Wo = jax.random.normal(ks[5], (INNER, QUERY_DIM), dtype=jnp.float32) * INNER ** (-0.5)
        return {'x': x, 'context': context, 'Wq': Wq, 'Wk': Wk, 'Wv': Wv, 'Wo': Wo}
    _L3_xattn_all = _L3_xattn_setup()
    _L3_xattn_in = {k: v for k, v in _L3_xattn_all.items() if k in ('Wq', 'Wk', 'Wv', 'Wo')}
    del _L3_xattn_all

    def _L3_ffn_setup():
        import jax, jax.numpy as jnp
        import numpy as np
        B, S, D = (4, 512, 256)
        E = 8
        TOPK = 2
        I = 938

        def _swiglu(x, gate_up, down):
            h = jnp.einsum('bsd,fd->bsf', x, gate_up)
            g, u = jnp.split(h, 2, axis=-1)
            return jnp.einsum('bsi,di->bsd', jax.nn.silu(g) * u, down)
        key = jax.random.key(seed)
        ks = jax.random.split(key, 6)
        scale = 1.0 / np.sqrt(D)
        return {'hidden_states': jax.random.normal(ks[0], (B, S, D), dtype=jnp.float32), 'gate_weight': jax.random.normal(ks[1], (E, D), dtype=jnp.float32) * scale, 'shared_gate_up': jax.random.normal(ks[2], (2 * I, D), dtype=jnp.float32) * scale, 'shared_down': jax.random.normal(ks[3], (D, I), dtype=jnp.float32) * (1.0 / np.sqrt(I)), 'experts_gate_up': jax.random.normal(ks[4], (E, 2 * I, D), dtype=jnp.float32) * scale, 'experts_down': jax.random.normal(ks[5], (E, D, I), dtype=jnp.float32) * (1.0 / np.sqrt(I))}
    _L3_ffn_all = _L3_ffn_setup()
    _L3_ffn_in = {k: v for k, v in _L3_ffn_all.items() if k in ('gate_weight', 'shared_gate_up', 'shared_down', 'experts_gate_up', 'experts_down')}
    del _L3_ffn_all
    return {'x': x, 'ctx_1024': ctx_1024, 'mask_BxSxS2_if1': mask_BxSxS2_if1, 'mask_Bx1xSxS2_bk1': mask_Bx1xSxS2_bk1, 'L0_xattn_Wq': _L0_xattn_in['Wq'], 'L0_xattn_bq': _L0_xattn_in['bq'], 'L0_xattn_Wk': _L0_xattn_in['Wk'], 'L0_xattn_bk': _L0_xattn_in['bk'], 'L0_xattn_Wv': _L0_xattn_in['Wv'], 'L0_xattn_bv': _L0_xattn_in['bv'], 'L0_xattn_Wo': _L0_xattn_in['Wo'], 'L0_xattn_bo': _L0_xattn_in['bo'], 'L0_ffn_Wg': _L0_ffn_in['Wg'], 'L0_ffn_W1': _L0_ffn_in['W1'], 'L0_ffn_b1': _L0_ffn_in['b1'], 'L0_ffn_Wo': _L0_ffn_in['Wo'], 'L0_ffn_bo': _L0_ffn_in['bo'], 'L1_xattn_Wq': _L1_xattn_in['Wq'], 'L1_xattn_bq': _L1_xattn_in['bq'], 'L1_xattn_Wk': _L1_xattn_in['Wk'], 'L1_xattn_bk': _L1_xattn_in['bk'], 'L1_xattn_Wv': _L1_xattn_in['Wv'], 'L1_xattn_bv': _L1_xattn_in['bv'], 'L1_xattn_Wo': _L1_xattn_in['Wo'], 'L1_xattn_bo': _L1_xattn_in['bo'], 'L1_ffn_W1': _L1_ffn_in['W1'], 'L1_ffn_b1': _L1_ffn_in['b1'], 'L1_ffn_W2': _L1_ffn_in['W2'], 'L1_ffn_b2': _L1_ffn_in['b2'], 'L2_xattn_Wq': _L2_xattn_in['Wq'], 'L2_xattn_bq': _L2_xattn_in['bq'], 'L2_xattn_Wk': _L2_xattn_in['Wk'], 'L2_xattn_bk': _L2_xattn_in['bk'], 'L2_xattn_Wv': _L2_xattn_in['Wv'], 'L2_xattn_bv': _L2_xattn_in['bv'], 'L2_xattn_Wo': _L2_xattn_in['Wo'], 'L2_xattn_bo': _L2_xattn_in['bo'], 'L2_ffn_Ws': _L2_ffn_in['Ws'], 'L2_ffn_bs': _L2_ffn_in['bs'], 'L2_ffn_W1': _L2_ffn_in['W1'], 'L2_ffn_b1': _L2_ffn_in['b1'], 'L2_ffn_W2': _L2_ffn_in['W2'], 'L2_ffn_b2': _L2_ffn_in['b2'], 'L3_xattn_Wq': _L3_xattn_in['Wq'], 'L3_xattn_Wk': _L3_xattn_in['Wk'], 'L3_xattn_Wv': _L3_xattn_in['Wv'], 'L3_xattn_Wo': _L3_xattn_in['Wo'], 'L3_ffn_gate_weight': _L3_ffn_in['gate_weight'], 'L3_ffn_shared_gate_up': _L3_ffn_in['shared_gate_up'], 'L3_ffn_shared_down': _L3_ffn_in['shared_down'], 'L3_ffn_experts_gate_up': _L3_ffn_in['experts_gate_up'], 'L3_ffn_experts_down': _L3_ffn_in['experts_down']}

def reference(x, ctx_1024, mask_BxSxS2_if1, mask_Bx1xSxS2_bk1, L0_xattn_Wq, L0_xattn_bq, L0_xattn_Wk, L0_xattn_bk, L0_xattn_Wv, L0_xattn_bv, L0_xattn_Wo, L0_xattn_bo, L0_ffn_Wg, L0_ffn_W1, L0_ffn_b1, L0_ffn_Wo, L0_ffn_bo, L1_xattn_Wq, L1_xattn_bq, L1_xattn_Wk, L1_xattn_bk, L1_xattn_Wv, L1_xattn_bv, L1_xattn_Wo, L1_xattn_bo, L1_ffn_W1, L1_ffn_b1, L1_ffn_W2, L1_ffn_b2, L2_xattn_Wq, L2_xattn_bq, L2_xattn_Wk, L2_xattn_bk, L2_xattn_Wv, L2_xattn_bv, L2_xattn_Wo, L2_xattn_bo, L2_ffn_Ws, L2_ffn_bs, L2_ffn_W1, L2_ffn_b1, L2_ffn_W2, L2_ffn_b2, L3_xattn_Wq, L3_xattn_Wk, L3_xattn_Wv, L3_xattn_Wo, L3_ffn_gate_weight, L3_ffn_shared_gate_up, L3_ffn_shared_down, L3_ffn_experts_gate_up, L3_ffn_experts_down):
    import jax
    import jax.numpy as jnp

    def _L0_xattn_ref(queries, keys, values, Wq, bq, Wk, bk, Wv, bv, Wo, bo):
        import jax, jax.numpy as jnp
        import numpy as np
        B, M, N = (2, 512, 512)
        D_MODEL = 256
        H, DH = (16, 64)

        def split_heads(x):
            b, s, _ = x.shape
            return x.reshape(b, s, H, DH).transpose(0, 2, 1, 3)
        Q = split_heads(queries @ Wq.T + bq)
        K = split_heads(keys @ Wk.T + bk)
        V = split_heads(values @ Wv.T + bv)
        e = jnp.einsum('bhmd,bhnd->bhmn', Q, K)
        a = jax.nn.softmax(e, axis=-1)
        O = jnp.einsum('bhmn,bhnd->bhmd', a, V)
        O = O.transpose(0, 2, 1, 3).reshape(O.shape[0], O.shape[2], H * DH)
        return O @ Wo.T + bo

    def _L0_ffn_ref(x, Wg, W1, b1, Wo, bo):
        import jax, jax.numpy as jnp
        import numpy as np
        TOP_K = 2
        EPS = 1e-09
        E = Wg.shape[0]
        gate_logits = jnp.einsum('btd,ed->bte', x, Wg)
        gate_scores = jax.nn.softmax(gate_logits, axis=-1)
        topk_val, topk_idx = jax.lax.top_k(gate_scores, TOP_K)
        topk_val = topk_val / (topk_val.sum(axis=-1, keepdims=True) + EPS)
        comb = (jax.nn.one_hot(topk_idx, E, dtype=x.dtype) * topk_val[..., None]).sum(axis=-2)
        out = jnp.zeros_like(x)
        for e in range(E):
            h = jnp.einsum('btd,hd->bth', x, W1[e]) + b1[e]
            a, b = jnp.split(h, 2, axis=-1)
            g = a * jax.nn.sigmoid(b)
            eo = jnp.einsum('bth,dh->btd', g, Wo) + bo
            out = out + eo * comb[..., e:e + 1]
        return out

    def _L1_xattn_ref(query, key, value, mask, Wq, bq, Wk, bk, Wv, bv, Wo, bo):
        import jax, jax.numpy as jnp
        import numpy as np
        B, S, H = (4, 512, 256)
        q = jnp.einsum('bsh,oh->bso', query, Wq) + bq
        k = jnp.einsum('bsh,oh->bso', key, Wk) + bk
        v = jnp.einsum('bsh,oh->bso', value, Wv) + bv
        scores = jnp.einsum('bqh,bkh->bqk', q, k) / jnp.sqrt(jnp.float32(H))
        scores = jnp.where(mask == 0, jnp.float32(-1000000000.0), scores)
        attn = jax.nn.softmax(scores, axis=-1)
        context = jnp.einsum('bqk,bkh->bqh', attn, v)
        out = jnp.einsum('bqh,oh->bqo', context, Wo) + bo
        return out

    def _L1_ffn_ref(x, W1, b1, W2, b2):
        import jax, jax.numpy as jnp
        import numpy as np
        EMB = 256
        FF = 4 * EMB

        def _ternary(w):
            scale = jnp.maximum(jnp.mean(jnp.abs(w)), 1e-08)
            w_t = jnp.clip(jnp.round(w / scale), -1.0, 1.0)
            return w + jax.lax.stop_gradient(w_t - w)
        h = jnp.einsum('bsd,fd->bsf', x, _ternary(W1)) + b1
        h = jax.nn.gelu(h, approximate=False)
        out = jnp.einsum('bsf,df->bsd', h, _ternary(W2)) + b2
        return out

    def _L2_xattn_ref(queries, keys, values, mask, Wq, bq, Wk, bk, Wv, bv, Wo, bo):
        import jax, jax.numpy as jnp
        import numpy as np
        B, S, D, H = (4, 512, 256, 16)
        HD = D // H
        b, sq, d = queries.shape

        def split_heads(x):
            return x.reshape(b, x.shape[1], H, HD).transpose(0, 2, 1, 3)
        q = split_heads(queries @ Wq + bq)
        k = split_heads(keys @ Wk + bk)
        v = split_heads(values @ Wv + bv)
        scores = jnp.einsum('bhqd,bhkd->bhqk', q, k) / jnp.sqrt(jnp.float32(HD))
        scores = jnp.where(mask, jnp.float32(-1000000000000000.0), scores)
        attn = jax.nn.softmax(scores, axis=-1)
        ctx = jnp.einsum('bhqk,bhkd->bhqd', attn, v)
        ctx = ctx.transpose(0, 2, 1, 3).reshape(b, sq, d)
        return ctx @ Wo + bo

    def _L2_ffn_ref(x, Ws, bs, W1, b1, W2, b2):
        import jax, jax.numpy as jnp
        import numpy as np
        B, S, D, E = (2, 1024, 256, 8)
        b, s, d = x.shape
        xf = x.reshape(-1, d)
        logits = xf @ Ws.T + bs
        probs = jax.nn.softmax(logits, axis=-1)
        routes = jnp.argmax(probs, axis=-1)
        pmax = jnp.max(probs, axis=-1)
        xf = xf * pmax[:, None]
        perm = jnp.argsort(routes, stable=True)
        xs = xf[perm]
        rs = routes[perm]
        h = jax.nn.relu(jnp.einsum('td,edf->etf', xs, W1) + b1[:, None, :])
        y = jnp.einsum('etf,efd->etd', h, W2) + b2[:, None, :]
        out = y[rs, jnp.arange(rs.shape[0])]
        return out.reshape(b, s, d)

    def _L3_xattn_ref(x, context, Wq, Wk, Wv, Wo):
        import jax, jax.numpy as jnp
        import numpy as np
        HEADS = 16
        DIM_HEAD = 64
        QUERY_DIM = 256
        INNER = HEADS * DIM_HEAD
        SCALE = DIM_HEAD ** (-0.5)
        B, N, _ = x.shape
        M = context.shape[1]
        q = (x @ Wq).reshape(B, N, HEADS, DIM_HEAD)
        k = (context @ Wk).reshape(B, M, HEADS, DIM_HEAD)
        v = (context @ Wv).reshape(B, M, HEADS, DIM_HEAD)
        sim = jnp.einsum('bihd,bjhd->bhij', q, k) * SCALE
        attn = jax.nn.softmax(sim, axis=-1)
        out = jnp.einsum('bhij,bjhd->bihd', attn, v)
        out = out.reshape(B, N, INNER)
        return out @ Wo

    def _L3_ffn_ref(hidden_states, gate_weight, shared_gate_up, shared_down, experts_gate_up, experts_down):
        import jax, jax.numpy as jnp
        import numpy as np
        B, S, D = (4, 512, 256)
        E = 8
        TOPK = 2
        I = 938

        def _swiglu(x, gate_up, down):
            h = jnp.einsum('bsd,fd->bsf', x, gate_up)
            g, u = jnp.split(h, 2, axis=-1)
            return jnp.einsum('bsi,di->bsd', jax.nn.silu(g) * u, down)
        x = hidden_states
        out = _swiglu(x, shared_gate_up, shared_down)
        logits = jnp.einsum('bsd,ed->bse', x, gate_weight)
        probs = jax.nn.softmax(logits.astype(jnp.float32), axis=-1)
        top_p, sel = jax.lax.top_k(probs, TOPK)
        top_p = top_p / (jnp.sum(top_p, axis=-1, keepdims=True) + 1e-08)
        cw = jnp.sum(top_p[..., None] * jax.nn.one_hot(sel, E, dtype=top_p.dtype), axis=2)
        for e in range(E):
            y = _swiglu(x, experts_gate_up[e], experts_down[e])
            out = out + cw[..., e:e + 1] * y
        return out
    x = x + _L0_xattn_ref(_layernorm(x, axis=-1), ctx_1024, ctx_1024, L0_xattn_Wq, L0_xattn_bq, L0_xattn_Wk, L0_xattn_bk, L0_xattn_Wv, L0_xattn_bv, L0_xattn_Wo, L0_xattn_bo)
    x = x + _L0_ffn_ref(_layernorm(x, axis=-1), L0_ffn_Wg, L0_ffn_W1, L0_ffn_b1, L0_ffn_Wo, L0_ffn_bo)
    x = x + _L1_xattn_ref(_layernorm(x, axis=-1), ctx_1024, ctx_1024, mask_BxSxS2_if1, L1_xattn_Wq, L1_xattn_bq, L1_xattn_Wk, L1_xattn_bk, L1_xattn_Wv, L1_xattn_bv, L1_xattn_Wo, L1_xattn_bo)
    x = x + _L1_ffn_ref(_layernorm(x, axis=-1), L1_ffn_W1, L1_ffn_b1, L1_ffn_W2, L1_ffn_b2)
    x = x + _L2_xattn_ref(_layernorm(x, axis=-1), ctx_1024, ctx_1024, mask_Bx1xSxS2_bk1, L2_xattn_Wq, L2_xattn_bq, L2_xattn_Wk, L2_xattn_bk, L2_xattn_Wv, L2_xattn_bv, L2_xattn_Wo, L2_xattn_bo)
    x = x + _L2_ffn_ref(_layernorm(x, axis=-1), L2_ffn_Ws, L2_ffn_bs, L2_ffn_W1, L2_ffn_b1, L2_ffn_W2, L2_ffn_b2)
    x = x + _L3_xattn_ref(_layernorm(x, axis=-1), ctx_1024, L3_xattn_Wq, L3_xattn_Wk, L3_xattn_Wv, L3_xattn_Wo)
    x = x + _L3_ffn_ref(_layernorm(x, axis=-1), L3_ffn_gate_weight, L3_ffn_shared_gate_up, L3_ffn_shared_down, L3_ffn_experts_gate_up, L3_ffn_experts_down)
    return x

_drawn_inputs = setup_inputs


def setup_inputs(seed=0):
    import zlib

    import numpy as np

    out = dict(_drawn_inputs(seed))
    spreads = {'L0_xattn_bq': (0.0, 0.1),
     'L0_xattn_bk': (0.0, 2.0),
     'L0_xattn_bv': (0.0, 0.1),
     'L0_xattn_bo': (0.0, 0.1),
     'L1_xattn_bq': (0.0, 0.8),
     'L1_xattn_bk': (0.0, 2.0),
     'L1_xattn_bv': (0.0, 0.1),
     'L1_xattn_bo': (0.0, 0.1),
     'L2_xattn_bq': (0.0, 0.8),
     'L2_xattn_bk': (0.0, 2.0),
     'L2_xattn_bv': (0.0, 0.8),
     'L2_xattn_bo': (0.0, 0.8)}
    factors = {'L0_ffn_Wg': 3.255,
     'L0_ffn_W1': 2.804,
     'L0_ffn_b1': 8.0,
     'L0_ffn_Wo': 2.79,
     'L0_ffn_bo': 6.793,
     'L1_ffn_b1': 8.0,
     'L1_ffn_b2': 8.0,
     'L2_xattn_Wq': 8.0,
     'L2_xattn_Wk': 8.0,
     'L2_xattn_Wv': 8.0,
     'L2_xattn_Wo': 8.0,
     'L2_ffn_Ws': 8.0,
     'L2_ffn_bs': 8.0,
     'L2_ffn_W1': 8.0,
     'L2_ffn_b1': 8.0,
     'L2_ffn_W2': 8.0,
     'L2_ffn_b2': 37.154,
     'L3_xattn_Wq': 8.0,
     'L3_xattn_Wk': 8.0,
     'L3_xattn_Wv': 8.0,
     'L3_xattn_Wo': 8.0,
     'L3_ffn_gate_weight': 8.0,
     'L3_ffn_shared_gate_up': 8.0,
     'L3_ffn_shared_down': 8.0,
     'L3_ffn_experts_gate_up': 8.0,
     'L3_ffn_experts_down': 8.0}
    for name, (base, spread) in spreads.items():
        noise = np.random.default_rng([zlib.crc32(name.encode()), seed]).standard_normal(out[name].shape)
        drawn = base * np.exp(spread * noise) if base else spread * noise
        out[name] = jnp.asarray(drawn.astype(out[name].dtype))
    for name, factor in factors.items():
        out[name] = (out[name] * factor).astype(out[name].dtype)
    return out
```

```python
from contextlib import ExitStack

import concourse.bass as bass
from concourse import mybir

F32 = mybir.dt.float32
BF16 = mybir.dt.bfloat16
I32 = mybir.dt.int32
U32 = mybir.dt.uint32
U8 = mybir.dt.uint8
ALU = mybir.AluOpType
ACT = mybir.ActivationFunctionType
AX_X = mybir.AxisListType.X

P = 128
D = 256
KT = D // P
B = 2
TB = 512
T = B * TB
TT = T // P
TTB = TB // P
SK = 1024
SKT = SK // P
N = 512
E = 8
LN_EPS = 1e-5


class Attention:

    def __init__(self, name, groups, nh, nc, scale, bias, mask, fills):
        self.name, self.groups, self.nh, self.nc = name, groups, nh, nc
        self.rows = P // nh
        self.scale, self.bias, self.mask = scale, bias, mask
        self.steps = TTB * nh
        self.half = self.steps // 2
        self.cols = P * nc
        self.projections = [("Q", c) for c in range(nc)] + [("K", c, n) for c in range(nc) for n in range(SK // N)] \
            + [("V", j) for j in range(SKT * self.cols // N)]
        self.schedule = fills

    def fills(self, kind):
        lag = ("R1", "O0", "O1")
        proj = ("Q", "K", "V")
        out = []
        for s, f in self.schedule:
            if f[0] in lag and kind == "first" or f[0] in proj and kind == "last":
                continue
            out.append((s, f))
        return out

    def index(self, kind, what):
        return [f for _, f in self.fills(kind)].index(what)


def fills_before(att, ph, k):
    kind, loop, c = ph
    n0 = len(att.projections)
    if kind == "first":
        return n0 + k
    full = len(att.fills("mid"))
    base = n0 + len(att.fills("first")) - full
    return count(ph, full, base + k)


def count(ph, per, off):
    _, loop, c = ph
    if loop is None:
        return per * c + off
    return loop * (2 * per) + (per * c + off)


PAIR = [(0, ("R1",)), (1, ("O0",)), (1, ("Q", 0)), (2, ("K", 0, 0)), (3, ("K", 0, 1)), (4, ("R0",)),
        (5, ("O1",)), (5, ("V", 0)), (6, ("V", 1))]
QUAD = [(0, ("R1",)), (1, ("O0",)), (2, ("Q", 0)), (3, ("K", 0, 0)), (4, ("K", 0, 1)), (8, ("R0",)),
        (9, ("O1",)), (10, ("V", 0)), (11, ("V", 1))]
SINGLE = [(0, ("R1",)), (0, ("O0",)), (0, ("Q", 0)), (0, ("Q", 1)), (1, ("K", 0, 0)), (1, ("K", 0, 1)),
          (1, ("K", 1, 0)), (1, ("K", 1, 1)), (2, ("R0",)), (2, ("O1",)), (2, ("V", 0)), (2, ("V", 1)),
          (3, ("V", 2)), (3, ("V", 3))]


def build(nc, a, out):
    ctx = ExitStack()
    with ctx:
        def sb(name, shape, dt=F32, where=ctx):
            return where.enter_context(nc.sbuf_tensor(name, shape, dt))

        def sem(name):
            return ctx.enter_context(nc.semaphore(name))

        psum = ctx.enter_context(nc.psum_tensor("psum", [P, 8, N], F32))
        pool_of_sems, lately_used = {}, []

        def shared(name):
            if name not in pool_of_sems:
                pool_of_sems[name] = sem(name)
            lately_used.append(pool_of_sems[name])
            return pool_of_sems[name]

        def clear_shared():
            with nc.Block() as block:
                @block.sync
                def _(sp):
                    for s in lately_used:
                        sp.sem_clear(s)
            lately_used.clear()

        bank = [psum[:, i, :] for i in range(8)]
        x = sb("x", [P, TT, D])
        xn = sb("xn", [P, TT, D])
        xnT = sb("xnT", [P, KT, T])
        ctxT = sb("ctxT", [P, KT, B * SK])
        ident = sb("ident", [P, P])
        iota = sb("iota", [P, E])
        comb = sb("comb", [P, TT, 1 + E])
        columns_i = sb("columns_i", [P, T], I32)
        rows_i = sb("rows_i", [P, TT], I32)
        column_no = sb("column_no", [P, T])
        token_no = sb("token_no", [P, TT])
        below = sb("below", [P, P])
        ones = sb("ones", [P, P])
        x_loaded = sem("x_loaded")
        ctx_loaded = sem("ctx_loaded")
        ident_made = sem("ident_made")
        x_stored = sem("x_stored")
        spare = sem("spare")

        with nc.Block() as block:
            @block.sync
            def _(sp):
                sp.dma_start(x[:], a["x"].rearrange("(j p) d -> p j d", p=P)).then_inc(x_loaded, 16)
                sp.dma_start(ctxT[:], a["ctxT"].rearrange("(k p) t -> p k t", p=P)).then_inc(ctx_loaded, 16)

            @block.gpsimd
            def _(pool):
                nc.gpsimd.memset(ident[:], 0.0).then_inc(ident_made, 1)
                pool.wait_ge(ident_made, 1)
                nc.gpsimd.affine_select(out=ident[:], in_=ident[:], compare_op=ALU.not_equal, fill=1.0,
                                        base=0, pattern=[[-1, P]], channel_multiplier=1).then_inc(ident_made, 1)
                for e in range(E):
                    nc.gpsimd.memset(iota[:, e:e + 1], float(e)).then_inc(ident_made, 1)
                nc.gpsimd.memset(ones[:], 1.0).then_inc(ident_made, 1)
                nc.gpsimd.iota(columns_i[:], pattern=[[1, T]], base=0, channel_multiplier=0).then_inc(ident_made, 1)
                nc.gpsimd.iota(rows_i[:], pattern=[[P, TT]], base=0, channel_multiplier=1).then_inc(ident_made, 1)
                pool.wait_ge(ident_made, 5 + E)
                nc.gpsimd.affine_select(out=below[:], in_=ones[:], compare_op=ALU.is_gt, fill=0.0,
                                        base=0, pattern=[[1, P]], channel_multiplier=-1).then_inc(ident_made, 1)
                nc.gpsimd.tensor_copy(column_no[:], columns_i[:]).then_inc(ident_made, 1)
                nc.gpsimd.tensor_copy(token_no[:], rows_i[:]).then_inc(ident_made, 1)
                pool.wait_ge(ident_made, 8 + E)

            @block.vector
            def _(dve):
                dve.wait_ge(x_loaded, 16)

        norms = {"calls": 0, "chain": 0, "bo": 0}
        ln_chain = sem("ln_chain")
        ln_bo_loaded = sem("ln_bo_loaded")
        ln_var_ready = sem("ln_var_ready")
        ln_sd_ready = sem("ln_sd_ready")
        ln_xn_ready = sem("ln_xn_ready")
        ln_tr_ready = sem("ln_tr_ready")
        ln_transposed = sem("ln_transposed")

        def layer_norm(name, bo=None):
            n = norms["calls"]
            norms["calls"] += 1
            with ExitStack() as own:
                stats = sb(name + "_stats", [P, TT, 6], F32, own)
                mv = sb(name + "_mv", [P, TT, 2], F32, own)
                ve = sb(name + "_ve", [P, TT], F32, own)
                sd = sb(name + "_sd", [P, TT], F32, own)
                r0 = sb(name + "_r0", [P, TT], F32, own)
                w = sb(name + "_w", [P, TT], F32, own)
                bo_all = sb(name + "_bo", [P, D], F32, own)
                with nc.Block() as block:
                    @block.sync
                    def _(sp):
                        if bo is not None:
                            norms["bo"] += 1
                            sp.dma_start(bo_all[:], a[bo].partition_broadcast(P)).then_inc(ln_bo_loaded, 16)

                    @block.vector
                    def _(dve):
                        def link(ins):
                            norms["chain"] += 1
                            ins.then_inc(ln_chain, 1)
                            dve.wait_ge(ln_chain, norms["chain"])

                        for j in range(TT):
                            last = nc.vector.bn_stats(stats[:, j, :], x[:, j, :])
                        link(last)
                        for j in range(TT):
                            last = nc.vector.bn_aggr(mv[:, j, :], stats[:, j, :])
                        link(last)
                        nc.vector.tensor_scalar(ve[:], mv[:, :, 1], LN_EPS, None, ALU.add).then_inc(ln_var_ready, 1)
                        dve.wait_ge(ln_sd_ready, n + 1)
                        link(nc.vector.reciprocal(r0[:], sd[:]))
                        link(nc.vector.tensor_tensor(w[:], r0[:], r0[:], ALU.mult))
                        link(nc.vector.tensor_tensor(w[:], w[:], ve[:], ALU.mult))
                        link(nc.vector.tensor_scalar(w[:], w[:], -0.5, 1.5, ALU.mult, ALU.add))
                        link(nc.vector.tensor_tensor(r0[:], r0[:], w[:], ALU.mult))
                        for j in range(TT):
                            nc.vector.tensor_scalar(xn[:, j, :], x[:, j, :], mv[:, j, 0:1], r0[:, j:j + 1],
                                                    ALU.subtract, ALU.mult).then_inc(ln_xn_ready, 1)
                        if bo is not None:
                            dve.wait_ge(ln_bo_loaded, 16 * norms["bo"])
                            dve.wait_ge(ln_xn_ready, (n + 1) * TT)
                            link(nc.vector.tensor_tensor(x[:], x[:], bo_all[:].unsqueeze(1).to_broadcast([P, TT, D]),
                                                         ALU.add))
                        for k in range(KT):
                            dve.wait_ge(ln_tr_ready, 2 * KT * n + 2 * k + 2)
                            nc.vector.tensor_copy(xnT[:, k, N:2 * N], bank[2 * k + 1][:, :]).then_inc(ln_transposed, 1)

                    @block.scalar
                    def _(act):
                        act.wait_ge(ln_var_ready, n + 1)
                        nc.scalar.activation(sd[:], ve[:], ACT.Sqrt).then_inc(ln_sd_ready, 1)
                        for k in range(KT):
                            act.wait_ge(ln_tr_ready, 2 * KT * n + 2 * k + 1)
                            nc.scalar.copy(xnT[:, k, 0:N], bank[2 * k][:, :]).then_inc(ln_transposed, 1)

                    @block.tensor
                    def _(pe):
                        pe.wait_ge(ident_made, 2)
                        for k in range(KT):
                            for h in range(2):
                                for j in range(4):
                                    if k == 0:
                                        pe.wait_ge(ln_xn_ready, n * TT + 4 * h + j + 1)
                                    last = nc.tensor.transpose(bank[2 * k + h][:, j * P:(j + 1) * P],
                                                               xn[:, 4 * h + j, k * P:(k + 1) * P], ident[:])
                                last.then_inc(ln_tr_ready, 1)

        def attention(att):
            nm = att.name
            nh, ncc, rows, steps, half, cols = att.nh, att.nc, att.rows, att.steps, att.half, att.cols
            G = att.groups
            kpb = N // cols
            loads = 3 if att.bias else 1
            own = ExitStack()
            with own:
                Q = sb(nm + "_Q", [P, B, max(nh, ncc), TB], F32, own)
                K = sb(nm + "_K", [P, B, ncc, SK], F32, own)
                V = sb(nm + "_V", [P, B, SKT, cols], F32, own)
                prob = sb(nm + "_prob", [P, 2, SK], F32, own)
                probT = sb(nm + "_probT", [P, 2, nh, SKT, 2 * P], F32, own)
                wqkv = sb(nm + "_wqkv", [P, KT, 3 * cols], F32, own)
                wo = sb(nm + "_wo", [P, ncc, D], F32, own)
                negmax = sb(nm + "_negmax", [P, steps], F32, own)
                sums = sb(nm + "_sums", [P, steps], F32, own)
                rexp = sb(nm + "_rexp", [P, 2, nh, rows], F32, own)
                rall = sb(nm + "_rall", [P, 2 * P], F32, own)
                OT = sb(nm + "_OT", [P, ncc, 2 * P], F32, own)
                if att.bias:
                    bqk = sb(nm + "_bqk", [P, 2 * ncc], F32, own)
                    bv = sb(nm + "_bv", [P, cols], F32, own)
                if att.mask:
                    masked = sb(nm + "_masked", [P, 2, SK], F32, own)
                    top = sb(nm + "_top", [P, steps], F32, own)
                if att.mask == "add":
                    mraw = sb(nm + "_mraw", [P, B * TTB, SK], U8, own)
                    mbias = sb(nm + "_mbias", [P, B * TTB, SK], BF16, own)
                if att.mask == "select":
                    mraw = sb(nm + "_mraw", [P, B * TTB, SK], I32, own)
                    keep = sb(nm + "_keep", [P, SK], F32, own)
                    mbias = sb(nm + "_mbias", [P, SK], F32, own)
                w_loaded = shared("att_w_loaded")
                wo_loaded = shared("att_wo_loaded")
                mask_loaded = shared("att_mask_loaded")
                mask_made = shared("att_mask_made")
                q_zeroed = shared("att_q_zeroed")
                scores_ready = shared("att_scores_ready")
                max_ready = shared("att_max_ready")
                dve_chain = shared("att_dve_chain")
                prob_ready = shared("att_prob_ready")
                tr_ready = shared("att_tr_ready")
                evac_act = shared("att_evac_act")
                evac_dve = shared("att_evac_dve")
                fill_ready = shared("att_fill_ready")
                fill_taken = shared("att_fill_taken")
                pv_ready = shared("att_pv_ready")
                o_taken = shared("att_o_taken")
                rsum_ready = shared("att_rsum_ready")
                S = [(bank[0], bank[1]), (bank[2], bank[3])]
                SPAN = [psum[:, 0:2, :].rearrange("p a n -> p (a n)"), psum[:, 2:4, :].rearrange("p a n -> p (a n)")]
                TR = (bank[4], bank[5])
                OB = bank[6]
                FB = bank[7]
                scores_free = max_ready if att.mask else prob_ready

                def phases(run, eng):
                    run(("first", None, 0), 0)
                    if G > 1:
                        with eng.Fori(0, G - 1) as i:
                            run(("mid", i, 1), 1)
                            run(("mid", i, 2), 0)
                    run(("last", None, 2 * G - 1), 1)

                block = own.enter_context(nc.Block())

                @block.sync
                def _(sp):
                    def load_w(g):
                        sp.dma_start(wqkv[:], a[nm + "_wqkv"][g]).then_inc(w_loaded, 16)
                        if att.bias:
                            sp.dma_start(bqk[:], a[nm + "_bqk"][g]).then_inc(w_loaded, 16)
                            sp.dma_start(bv[:], a[nm + "_bv"][g].partition_broadcast(P)).then_inc(w_loaded, 16)

                    load_w(0)
                    sp.dma_start(wo[:], a[nm + "_wo"][0]).then_inc(wo_loaded, 16)
                    if att.mask:
                        for b in range(B):
                            sp.dma_start(mraw[:, b * TTB:(b + 1) * TTB, :],
                                         a[nm + "_mask"][b].rearrange("(j p) s -> p j s", p=P)).then_inc(mask_loaded, 16)
                    if G > 1:
                        lastv = ("V", len([f for f in att.projections if f[0] == "V"]) - 1)
                        ph = ("first", None, 0)
                        sp.wait_ge(fill_taken, fills_before(att, ph, att.index("first", lastv)) + 1)
                        load_w(1)

                        def load_wo(ph, g):
                            sp.wait_ge(fill_taken, fills_before(att, ph, att.index("mid", ("O1",)) + 1))
                            sp.dma_start(wo[:], a[nm + "_wo"][g]).then_inc(wo_loaded, 16)
                        if G > 2:
                            with sp.Fori(0, G - 2) as i:
                                ph = ("mid", i, 2)
                                load_wo(ph, i + 1)
                                sp.wait_ge(fill_taken, fills_before(att, ph, att.index("mid", lastv) + 1))
                                load_w(i + 2)
                        load_wo(("mid", None, 2 * G - 2), G - 1)

                @block.tensor
                def _(pe):
                    def fill(ph, f, k, b):
                        if k is None:
                            before = att.projections.index(f)
                        else:
                            before = fills_before(att, ph, k)
                        if k is not None or before:
                            pe.wait_ge(fill_taken, before)
                        kind = f[0]
                        if kind == "Q":
                            if f[1] == 0:
                                if k is None:
                                    pe.wait_ge(w_loaded, 16 * loads)
                                    pe.wait_ge(ctx_loaded, 16)
                                elif ph[0] == "mid" and ph[2] == 1:
                                    pe.wait_ge(w_loaded, ph[1] * (16 * loads) + 32 * loads)
                            for kt in range(KT):
                                last = nc.tensor.matmul(FB[:, :], wqkv[:, kt, f[1] * P:(f[1] + 1) * P],
                                                        xnT[:, kt, b * TB:(b + 1) * TB],
                                                        start=(kt == 0), stop=(kt == KT - 1))
                        elif kind == "K":
                            for kt in range(KT):
                                last = nc.tensor.matmul(FB[:, :], wqkv[:, kt, cols + f[1] * P:cols + (f[1] + 1) * P],
                                                        ctxT[:, kt, b * SK + f[2] * N:b * SK + (f[2] + 1) * N],
                                                        start=(kt == 0), stop=(kt == KT - 1))
                        elif kind == "V":
                            for i in range(kpb):
                                t = f[1] * kpb + i
                                for kt in range(KT):
                                    last = nc.tensor.matmul(FB[:, i * cols:(i + 1) * cols],
                                                            ctxT[:, kt, b * SK + t * P:b * SK + (t + 1) * P],
                                                            wqkv[:, kt, 2 * cols:3 * cols],
                                                            start=(kt == 0), stop=(kt == KT - 1))
                        elif kind in ("R0", "R1"):
                            h = int(kind[1])
                            pe.wait_ge(rsum_ready, count(ph, 2, h + 1 if h == 0 else 0))
                            for q in range(2):
                                last = nc.tensor.matmul(FB[:, q * P:(q + 1) * P],
                                                        rexp[:, q].rearrange("p h r -> p (h r)"), ident[:],
                                                        start=True, stop=True)
                        else:
                            h = int(kind[1])
                            pe.wait_ge(o_taken, count(ph, 2, h - 1))
                            if h == 0:
                                if ph[0] == "mid" and ph[2] == 1:
                                    pe.wait_ge(wo_loaded, ph[1] * 16 + 16)
                                elif ph[0] == "last":
                                    pe.wait_ge(wo_loaded, 16 * G)
                            for q in range(2):
                                for c in range(ncc):
                                    last = nc.tensor.matmul(FB[:, q * D:(q + 1) * D], OT[:, c, q * P:(q + 1) * P],
                                                            wo[:, c, :], start=(c == 0), stop=(c == ncc - 1))
                        last.then_inc(fill_ready, 1)

                    def scores(ph, s, b):
                        t, h = s // nh, s % nh
                        for n in range(SK // N):
                            for c in range(ncc):
                                lhs = Q[:, b, c if ncc > 1 else h, t * P:(t + 1) * P]
                                last = nc.tensor.matmul(S[s % 2][n][:, :], lhs, K[:, b, c, n * N:(n + 1) * N],
                                                        start=(c == 0), stop=(c == ncc - 1))
                        last.then_inc(scores_ready, 1)

                    def pv(ph, hf, b, part, parts):
                        if ncc == 1:
                            todo = [(kt, h, 0) for kt in range(SKT) for h in range(nh)]
                        else:
                            todo = [(kt, 0, c) for c in range(ncc) for kt in range(SKT)]
                        m = len(todo) // parts
                        for kt, h, c in todo[part * m:(part + 1) * m]:
                            o = OB[h * rows:(h + 1) * rows, c * 2 * P:(c + 1) * 2 * P]
                            last = nc.tensor.matmul(o, V[:, b, kt, (h * rows if ncc == 1 else c * P):
                                                              ((h + 1) * rows if ncc == 1 else (c + 1) * P)],
                                                    probT[:, hf, h, kt, :], start=(kt == 0), stop=(kt == SKT - 1))
                        if part == parts - 1:
                            last.then_inc(pv_ready, 1)

                    def pv_waits(ph, hf):
                        pe.wait_ge(evac_act, count(ph, steps, half * (hf + 1)))
                        pe.wait_ge(evac_dve, count(ph, steps, half * (hf + 1)))
                        if not (ph[0] == "first" and hf == 0):
                            pe.wait_ge(o_taken, count(ph, 2, hf))

                    def before(ph):
                        return (ph[0], ph[1], ph[2] - 1)

                    def transposes(ph, s):
                        pe.wait_ge(prob_ready, count(ph, steps, s + 1))
                        for i in range(2):
                            if not (ph[0] == "first" and s == 0):
                                pe.wait_ge(evac_dve if i else evac_act, count(ph, steps, s))
                            for j in range(4):
                                kt = 4 * i + j
                                last = nc.tensor.transpose(TR[i][:, j * P:(j + 1) * P],
                                                           prob[:, s % 2, kt * P:(kt + 1) * P], ident[:])
                            last.then_inc(tr_ready, 1)

                    def phase(ph, b):
                        kind = ph[0]
                        fl = att.fills(kind)
                        for s in range(steps):
                            if s + 1 < steps:
                                if not (kind == "first" and s == 0):
                                    pe.wait_ge(scores_free, count(ph, steps, s))
                                scores(ph, s + 1, b)
                            elif kind != "last":
                                pe.wait_ge(scores_free, count(ph, steps, s))
                                pe.wait_ge(fill_taken, fills_before(att, ph, att.index(kind, ("K", ncc - 1, 1)) + 1))
                                scores(ph, 0, 1 - b)
                            for k, (fs, f) in enumerate(fl):
                                if fs == s:
                                    fill(ph, f, k, 1 - b)
                            if s < half:
                                if kind != "first":
                                    if s == 0:
                                        pv_waits(before(ph), 1)
                                    pv(ph, 1, 1 - b, s, half)
                            else:
                                if s == half:
                                    pv_waits(ph, 0)
                                pv(ph, 0, b, s - half, half)
                            transposes(ph, s)

                    pe.wait_ge(q_zeroed, 1)
                    for f in att.projections:
                        fill(None, f, None, 0)
                    pe.wait_ge(fill_taken, len(att.projections))
                    scores(None, 0, 0)
                    phases(phase, pe)
                    end = ("mid", None, 2 * G)
                    n0 = len(att.projections) + len(att.fills("first")) + (2 * G - 2) * len(att.fills("mid")) \
                        + len(att.fills("last"))
                    for k, f in enumerate((("R1",), ("O0",), ("O1",))):
                        if k == 2:
                            pv_waits(("last", None, 2 * G - 1), 1)
                            pv(end, 1, 1, 0, 1)
                        pe.wait_ge(fill_taken, n0 + k)
                        h = int(f[0][1])
                        if k == 0:
                            pe.wait_ge(rsum_ready, 4 * G)
                            for q in range(2):
                                last = nc.tensor.matmul(FB[:, q * P:(q + 1) * P],
                                                        rexp[:, q].rearrange("p h r -> p (h r)"), ident[:],
                                                        start=True, stop=True)
                        else:
                            pe.wait_ge(o_taken, 4 * G - 1 + h)
                            for q in range(2):
                                for c in range(ncc):
                                    last = nc.tensor.matmul(FB[:, q * D:(q + 1) * D], OT[:, c, q * P:(q + 1) * P],
                                                            wo[:, c, :], start=(c == 0), stop=(c == ncc - 1))
                        last.then_inc(fill_ready, 1)

                tail_fills = len(att.projections) + len(att.fills("first")) + (2 * G - 2) * len(att.fills("mid")) \
                    + len(att.fills("last"))

                @block.scalar
                def _(act):
                    def take(f, n, b):
                        act.wait_ge(fill_ready, n)
                        if f[0] == "K":
                            dst = K[:, b, f[1], f[2] * N:(f[2] + 1) * N]
                            if att.bias:
                                nc.scalar.activation(dst, FB[:, :], ACT.Identity,
                                                     bias=bqk[:, ncc + f[1]:ncc + f[1] + 1]).then_inc(fill_taken, 1)
                            else:
                                nc.scalar.copy(dst, FB[:, :]).then_inc(fill_taken, 1)
                        else:
                            nc.scalar.copy(rall[:], FB[:, 0:2 * P]).then_inc(fill_taken, 1)

                    def exps(ph, s, off):
                        act.wait_ge(max_ready, count(ph, steps, off + 1))
                        if not (ph[0] == "first" and off < 2):
                            act.wait_ge(tr_ready, count(ph, 2 * steps, 2 * off - 2))
                        src = masked[:, s % 2, :] if att.mask else None
                        if att.mask:
                            nc.scalar.activation(prob[:, s % 2, :], src, ACT.Exp, bias=negmax[:, s:s + 1],
                                                 accum_out=sums[:, s:s + 1]).then_inc(prob_ready, 1)
                        else:
                            nc.scalar.activation(prob[:, s % 2, :], SPAN[s % 2], ACT.Exp, bias=negmax[:, s:s + 1],
                                                 accum_out=sums[:, s:s + 1]).then_inc(prob_ready, 1)

                    def phase(ph, b):
                        kind = ph[0]
                        fl = att.fills(kind)
                        for s in range(steps):
                            if s + 1 < steps:
                                exps(ph, s + 1, s + 1)
                            elif kind != "last":
                                exps(ph, 0, steps)
                            for k, (fs, f) in enumerate(fl):
                                if fs == s and f[0] in ("K", "R0", "R1"):
                                    if f[0][0] == "R":
                                        if kind != "first":
                                            act.wait_ge(o_taken, count(ph, 2, 0 if f[0] == "R0" else -1))
                                    take(f, fills_before(att, ph, k + 1), 1 - b)
                            hf, h, q = s // half, s % nh, s // nh % 2
                            act.wait_ge(tr_ready, count(ph, 2 * steps, 2 * s + 1))
                            if s % half == 0 and kind != "first":
                                act.wait_ge(pv_ready, count(ph, 2, hf - 1))
                            nc.scalar.copy(probT[:, hf, h, 0:4, q * P:(q + 1) * P],
                                           TR[0][:, :].rearrange("p (k q) -> p k q", q=P)).then_inc(evac_act, 1)

                    for n, f in enumerate(att.projections):
                        if f[0] == "K":
                            take(f, n + 1, 0)
                    exps(("first", None, 0), 0, 0)
                    phases(phase, act)
                    act.wait_ge(o_taken, 4 * G - 1)
                    take(("R1",), tail_fills + 1, 1)

                @block.vector
                def _(dve):
                    if ncc == 1:
                        nc.vector.memset(Q[:], 0.0).then_inc(q_zeroed, 1)
                        dve.wait_ge(q_zeroed, 1)
                    else:
                        nc.vector.memset(sums[:], 0.0).then_inc(q_zeroed, 1)
                        dve.wait_ge(q_zeroed, 1)
                    chained = [0]
                    if att.mask == "add":
                        dve.wait_ge(mask_loaded, 16 * B)
                        for j in range(B * TTB):
                            nc.vector.tensor_scalar(mbias[:, j, :], mraw[:, j, :], 0.0, -1e15,
                                                    ALU.not_equal, ALU.mult).then_inc(mask_made, 1)
                        dve.wait_ge(mask_made, B * TTB)

                    def maxes(ph, s, off, b):
                        if att.mask == "select":
                            j = b * TTB + s
                            if j:
                                dve.wait_ge(max_ready, j)
                            else:
                                dve.wait_ge(mask_loaded, 16 * B)
                            nc.vector.tensor_scalar(keep[:], mraw[:, j, :], 0.0, None, ALU.not_equal).then_inc(mask_made, 1)
                            nc.vector.tensor_scalar(mbias[:], mraw[:, j, :], 0.0, -1e9,
                                                    ALU.is_equal, ALU.mult).then_inc(mask_made, 1)
                            dve.wait_ge(mask_made, 2 * j + 2)
                        dve.wait_ge(scores_ready, count(ph, steps, off + 1))
                        if not att.mask:
                            nc.vector.tensor_reduce(negmax[:, s:s + 1], SPAN[s % 2], AX_X, ALU.max,
                                                    negate=True).then_inc(max_ready, 1)
                            return
                        if not (ph[0] == "first" and off < 2):
                            dve.wait_ge(prob_ready, count(ph, steps, off - 1))
                        src, mb = SPAN[s % 2], None
                        if att.mask == "select":
                            nc.vector.tensor_tensor(masked[:, s % 2, :], src, keep[:], ALU.mult).then_inc(dve_chain, 1)
                            dve.wait_ge(dve_chain, count(ph, 2 * steps, 2 * off + 1))
                            src, mb = masked[:, s % 2, :], mbias[:]
                        else:
                            mb = mbias[:, b * TTB + s // nh, :]
                        dve.sem_inc(spare, 1)
                        nc.vector.tensor_tensor_reduce(masked[:, s % 2, :], src, mb, 1.0, -3e38, ALU.add, ALU.max,
                                                       top[:, s:s + 1]).then_inc(dve_chain, 1)
                        per = 2 if att.mask == "select" else 1
                        dve.wait_ge(dve_chain, count(ph, per * steps, per * (off + 1)))
                        nc.vector.tensor_scalar(negmax[:, s:s + 1], top[:, s:s + 1], -1.0, None,
                                                ALU.mult).then_inc(max_ready, 1)

                    def take(f, n, b):
                        dve.wait_ge(fill_ready, n)
                        if f[0] == "Q":
                            for h in range(nh):
                                r = slice(h * rows, (h + 1) * rows)
                                dst = Q[r, b, h if ncc == 1 else f[1], :]
                                if att.bias:
                                    last = nc.vector.tensor_scalar(dst, FB[r, :], bqk[r, f[1]:f[1] + 1], att.scale,
                                                                   ALU.add, ALU.mult)
                                else:
                                    last = nc.vector.tensor_scalar(dst, FB[r, :], att.scale, None, ALU.mult)
                            last.then_inc(fill_taken, 1)
                        elif f[0] == "V":
                            dst = V[:, b, f[1] * kpb:(f[1] + 1) * kpb, :]
                            src = FB[:, :].rearrange("p (k c) -> p k c", c=cols)
                            if att.bias:
                                nc.vector.tensor_tensor(dst, src, bv[:].unsqueeze(1).to_broadcast([P, kpb, cols]),
                                                        ALU.add).then_inc(fill_taken, 1)
                            else:
                                nc.vector.tensor_copy(dst, src).then_inc(fill_taken, 1)
                        else:
                            j = b * TTB + 2 * int(f[0][1])
                            nc.vector.tensor_tensor(x[:, j:j + 2, :], x[:, j:j + 2, :],
                                                    FB[:, :].rearrange("p (q d) -> p q d", d=D),
                                                    ALU.add).then_inc(fill_taken, 1)

                    def reciprocals(ph, hf, done):
                        dve.wait_ge(prob_ready, done)
                        s0 = hf * half
                        src = sums[:, s0:s0 + half].rearrange("p (q h) -> p q h", h=nh)
                        nc.vector.reciprocal(rexp[:], src.unsqueeze(3).to_broadcast([P, 2, nh, rows])).then_inc(rsum_ready, 1)

                    def normalise(n_pv, n_fill):
                        dve.wait_ge(pv_ready, n_pv)
                        dve.wait_ge(fill_taken, n_fill)
                        if ncc == 1:
                            nc.vector.tensor_tensor(OT[:, 0, :], OB[:, 0:2 * P], rall[:], ALU.mult).then_inc(o_taken, 1)
                        else:
                            nc.vector.tensor_tensor(OT[:], OB[:, :].rearrange("p (c q) -> p c q", c=ncc),
                                                    rall[:].unsqueeze(1).to_broadcast([P, ncc, 2 * P]),
                                                    ALU.mult).then_inc(o_taken, 1)

                    def phase(ph, b):
                        kind = ph[0]
                        fl = att.fills(kind)
                        names = [f for _, f in fl]
                        for s in range(steps):
                            if s == 0 and kind != "first":
                                reciprocals(ph, 1, count(ph, steps, 0))
                            if s == half:
                                reciprocals(ph, 0, count(ph, steps, half))
                            if s + 1 < steps:
                                maxes(ph, s + 1, s + 1, b)
                            elif kind != "last":
                                maxes(ph, 0, steps, 1 - b)
                            for k, (fs, f) in enumerate(fl):
                                if fs == s and f[0] in ("Q", "V", "O0", "O1"):
                                    take(f, fills_before(att, ph, k + 1), 1 - b)
                            if s == half - 1 and kind != "first":
                                normalise(count(ph, 2, 0), fills_before(att, ph, names.index(("R1",)) + 1))
                            if s == steps - 1:
                                normalise(count(ph, 2, 1), fills_before(att, ph, names.index(("R0",)) + 1))
                            hf, h, q = s // half, s % nh, s // nh % 2
                            dve.wait_ge(tr_ready, count(ph, 2 * steps, 2 * s + 2))
                            if s % half == 0 and kind != "first":
                                dve.wait_ge(pv_ready, count(ph, 2, hf - 1))
                            nc.vector.tensor_copy(probT[:, hf, h, 4:8, q * P:(q + 1) * P],
                                                  TR[1][:, :].rearrange("p (k q) -> p k q", q=P)).then_inc(evac_dve, 1)

                    for n, f in enumerate(att.projections):
                        if f[0] in ("Q", "V"):
                            take(f, n + 1, 0)
                    maxes(("first", None, 0), 0, 0, 0)
                    phases(phase, dve)
                    reciprocals(("last", None, 2 * G), 1, 2 * G * steps)
                    take(("O0",), tail_fills + 2, 1)
                    normalise(4 * G, tail_fills + 1)
                    take(("O1",), tail_fills + 3, 1)

        def route(name, mode, eps=0.0, bias=False, broadcast=None, b2=None):
            with ExitStack() as own:
                wg = sb(name + "_wg_sb", [P, KT, E], F32, own)
                gb = sb(name + "_gb", [P, E], F32, own)
                lg = sb(name + "_lg", [P, TT, E], F32, own)
                top = sb(name + "_top", [P, TT, 8], F32, own)
                place = sb(name + "_place", [P, TT, 8], U32, own)
                placef = sb(name + "_placef", [P, TT, 8], F32, own)
                ex = sb(name + "_ex", [P, TT, E], F32, own)
                total = sb(name + "_total", [P, TT], F32, own)
                diff = sb(name + "_diff", [P, TT], F32, own)
                second = sb(name + "_second", [P, TT], F32, own)
                w0 = sb(name + "_w0", [P, TT], F32, own)
                w1 = sb(name + "_w1", [P, TT], F32, own)
                hot = sb(name + "_hot", [P, TT, E], F32, own)
                combT = sb(name + "_combT", [E, T], F32, own)
                pick = sb(name + "_pick", [E, E, P], F32, own)
                b2_sb = sb(name + "_b2", [E, D], F32, own)
                if mode == "argmax":
                    tile_sum = sb(name + "_tile_sum", [P, TT, E], F32, own)
                    ahead = sb(name + "_ahead", [P, TT, E], F32, own)
                    expert_sum = sb(name + "_expert_sum", [P, E], F32, own)
                    start_of = sb(name + "_start_of", [P, E + 1], F32, own)
                    beyond = sb(name + "_beyond", [P, TT, E + 1], F32, own)
                    goes_to = sb(name + "_goes_to", [P, TT], F32, own)
                    perm = sb(name + "_perm", [P, TT, T], F32, own)
                loaded = shared("route_loaded")
                logits_ready = shared("route_logits")
                chain = shared("route_chain")
                shifted = shared("route_shifted")
                exps_ready = shared("route_exps")
                comb_ready = shared("route_comb")
                combT_ready = shared("route_combT_ready")
                combT_taken = shared("route_combT_taken")
                row_ready = shared("route_row_ready")
                row_taken = shared("route_row_taken")
                scaled = shared("route_scaled")
                tr_ready = shared("route_tr")
                transposed = shared("route_xnT")
                hot_ready = shared("route_hot_ready")
                counted = shared("route_counted")
                with nc.Block() as block:
                    @block.sync
                    def _(sp):
                        sp.dma_start(wg[:], a[name + "_wg"]).then_inc(loaded, 16)
                        if bias:
                            sp.dma_start(gb[:], a[name + "_gb"].partition_broadcast(P)).then_inc(loaded, 16)
                        if b2:
                            sp.dma_start(b2_sb[:], a[b2]).then_inc(loaded, 16)

                    @block.vector
                    def _(dve):
                        done = [0]

                        def link(ins):
                            done[0] += 1
                            ins.then_inc(chain, 1)
                            dve.wait_ge(chain, done[0])

                        def per_token(v):
                            return v.unsqueeze(2).to_broadcast([P, TT, E])

                        iotas = iota[:].unsqueeze(1).to_broadcast([P, TT, E])
                        dve.wait_ge(logits_ready, 1)
                        src = bank[0][:, 0:TT * E].rearrange("p (j e) -> p j e", e=E)
                        if bias:
                            link(nc.vector.tensor_tensor(lg[:], src, gb[:].unsqueeze(1).to_broadcast([P, TT, E]),
                                                         ALU.add))
                        else:
                            link(nc.vector.tensor_copy(lg[:], src))
                        for j in range(TT):
                            last = nc.vector.max(top[:, j, :], lg[:, j, :])
                        link(last)
                        for j in range(TT):
                            last = nc.vector.max_index(place[:, j, :], top[:, j, :], lg[:, j, :])
                        link(last)
                        nc.vector.tensor_tensor(lg[:], lg[:], per_token(top[:, :, 0]), ALU.subtract).then_inc(shifted, 1)
                        nc.vector.tensor_tensor(diff[:], top[:, :, 1], top[:, :, 0], ALU.subtract).then_inc(shifted, 1)
                        link(nc.vector.tensor_copy(placef[:], place[:]))
                        dve.wait_ge(exps_ready, 2)
                        link(nc.vector.tensor_reduce(total[:], ex[:], AX_X, ALU.add))
                        if mode == "top2":
                            link(nc.vector.scalar_tensor_tensor(out=w1[:], in0=total[:], scalar=eps, in1=second[:],
                                                                op0=ALU.mult, op1=ALU.add))
                            link(nc.vector.tensor_scalar(w1[:], w1[:], 1.0, None, ALU.add))
                            link(nc.vector.reciprocal(w0[:], w1[:]))
                            link(nc.vector.tensor_tensor(w1[:], w0[:], second[:], ALU.mult))
                            link(nc.vector.tensor_tensor(hot[:], iotas, per_token(placef[:, :, 0]), ALU.is_equal))
                            link(nc.vector.tensor_tensor(comb[:, :, 1:], hot[:], per_token(w0[:]), ALU.mult))
                            link(nc.vector.tensor_tensor(hot[:], iotas, per_token(placef[:, :, 1]), ALU.is_equal))
                            link(nc.vector.tensor_tensor(hot[:], hot[:], per_token(w1[:]), ALU.mult))
                            link(nc.vector.tensor_tensor(comb[:, :, 1:], comb[:, :, 1:], hot[:], ALU.add))
                            if broadcast is not None:
                                nc.vector.tensor_tensor(comb[:, :, 0], w0[:], w1[:], ALU.add).then_inc(comb_ready, 1)
                            else:
                                nc.vector.memset(comb[:, :, 0:1], 1.0).then_inc(comb_ready, 1)
                        else:
                            link(nc.vector.reciprocal(w0[:], total[:]))
                            nc.vector.tensor_tensor(hot[:], iotas, per_token(placef[:, :, 0]),
                                                    ALU.is_equal).then_inc(hot_ready, 1)
                            for j in range(TT):
                                last = nc.vector.tensor_scalar(xn[:, j, :], xn[:, j, :], w0[:, j:j + 1], None, ALU.mult)
                            link(last)
                            dve.wait_ge(counted, 1)
                            link(nc.vector.tensor_copy(tile_sum[:], bank[2][:, 0:TT * E].rearrange("p (j e) -> p j e", e=E)))
                            link(nc.vector.tensor_reduce(expert_sum[:], tile_sum[:].rearrange("p j e -> p e j"),
                                                         AX_X, ALU.add))
                            for j in range(1, TT):
                                if j > 1:
                                    link(nc.vector.tensor_tensor(tile_sum[:, j - 1, :], tile_sum[:, j - 1, :],
                                                                 tile_sum[:, j - 2, :], ALU.add))
                            link(nc.vector.tensor_copy(ahead[:], bank[1][:, 0:TT * E].rearrange("p (j e) -> p j e", e=E)))
                            link(nc.vector.tensor_tensor(ahead[:, 1:, :], ahead[:, 1:, :], tile_sum[:, 0:TT - 1, :],
                                                         ALU.add))
                            link(nc.vector.memset(start_of[:, 0:1], 0.0))
                            for e in range(E):
                                link(nc.vector.tensor_tensor(start_of[:, e + 1:e + 2], start_of[:, e:e + 1],
                                                             expert_sum[:, e:e + 1], ALU.add))
                            link(nc.vector.tensor_tensor(ahead[:], ahead[:], start_of[:, 0:E].unsqueeze(1)
                                                         .to_broadcast([P, TT, E]), ALU.add))
                            link(nc.vector.tensor_tensor(ahead[:], ahead[:], hot[:], ALU.mult))
                            link(nc.vector.tensor_reduce(goes_to[:], ahead[:], AX_X, ALU.add))
                            for j in range(TT):
                                nc.vector.tensor_scalar(perm[:, j, :], column_no[:], goes_to[:, j:j + 1], None,
                                                        ALU.is_equal).then_inc(scaled, 1)
                            link(nc.vector.tensor_tensor(beyond[:], token_no[:].unsqueeze(2).to_broadcast([P, TT, E + 1]),
                                                         start_of[:].unsqueeze(1).to_broadcast([P, TT, E + 1]),
                                                         ALU.is_ge))
                            nc.vector.tensor_tensor(comb[:, :, 1:], beyond[:, :, 0:E], beyond[:, :, 1:],
                                                    ALU.subtract).then_inc(comb_ready, 1)
                            for n in range(2 * KT):
                                dve.wait_ge(tr_ready, n + 1)
                                nc.vector.tensor_copy(xnT[:, n // 2, (n % 2) * N:(n % 2 + 1) * N],
                                                      bank[4 + n][:, :]).then_inc(transposed, 1)
                        if broadcast is not None or b2:
                            for h in range(2):
                                dve.wait_ge(combT_ready, h + 1)
                                link(nc.vector.tensor_copy(combT[:, h * N:(h + 1) * N], bank[1 + h][0:E, :]))
                            nc.vector.tensor_copy(pick[:], ident[0:E, 0:E].unsqueeze(2).to_broadcast([E, E, P])
                                                  ).then_inc(combT_taken, 1)
                        if broadcast is not None:
                            for n in range(2 * E):
                                dve.wait_ge(row_ready, n + 1)
                                nc.vector.tensor_copy(broadcast[:, n // 2, (n % 2) * N:(n % 2 + 1) * N],
                                                      bank[4 + n % 4][:, :]).then_inc(row_taken, 1)
                        if b2:
                            for n in range(TT):
                                dve.wait_ge(row_ready, n + 1)
                                nc.vector.tensor_tensor(x[:, n, :], x[:, n, :], bank[5 + n % 3][:, 0:D],
                                                        ALU.add).then_inc(row_taken, 1)

                    @block.scalar
                    def _(act):
                        act.wait_ge(shifted, 2)
                        nc.scalar.activation(ex[:], lg[:], ACT.Exp).then_inc(exps_ready, 1)
                        nc.scalar.activation(second[:], diff[:], ACT.Exp).then_inc(exps_ready, 1)

                    @block.tensor
                    def _(pe):
                        pe.wait_ge(loaded, 16 * (1 + bias + bool(b2)))
                        for j in range(TT):
                            for k in range(KT):
                                last = nc.tensor.matmul(bank[0][:, j * E:(j + 1) * E], xnT[:, k, j * P:(j + 1) * P],
                                                        wg[:, k, :], start=(k == 0), stop=(k == KT - 1))
                        last.then_inc(logits_ready, 1)
                        if mode == "argmax":
                            pe.wait_ge(hot_ready, 1)
                            hots = hot[:].rearrange("p j e -> p (j e)")
                            nc.tensor.matmul(bank[1][:, 0:TT * E], below[:], hots, start=True, stop=True)
                            nc.tensor.matmul(bank[2][:, 0:TT * E], ones[:], hots, start=True, stop=True).then_inc(counted, 1)
                            for j in range(TT):
                                pe.wait_ge(scaled, j + 1)
                                for n in range(2 * KT):
                                    last = nc.tensor.matmul(bank[4 + n][:, :], xn[:, j, (n // 2) * P:(n // 2 + 1) * P],
                                                            perm[:, j, (n % 2) * N:(n % 2 + 1) * N],
                                                            start=(j == 0), stop=(j == TT - 1))
                                    if j == TT - 1:
                                        last.then_inc(tr_ready, 1)
                        pe.wait_ge(comb_ready, 1)
                        if broadcast is not None or b2:
                            for j in range(TT):
                                last = nc.tensor.transpose(bank[1 + j // 4][0:E, (j % 4) * P:(j % 4 + 1) * P],
                                                           comb[:, j, 1:], ident[:])
                                if j % 4 == 3:
                                    last.then_inc(combT_ready, 1)
                        if broadcast is not None:
                            pe.wait_ge(combT_taken, 1)
                            for n in range(2 * E):
                                if n >= 4:
                                    pe.wait_ge(row_taken, n - 3)
                                nc.tensor.matmul(bank[4 + n % 4][:, :], pick[:, n // 2, :],
                                                 combT[:, (n % 2) * N:(n % 2 + 1) * N],
                                                 start=True, stop=True).then_inc(row_ready, 1)
                        if b2:
                            pe.wait_ge(combT_taken, 1)
                            pe.wait_ge(transposed, 2 * KT)
                            for n in range(TT):
                                if n >= 3:
                                    pe.wait_ge(row_taken, n - 2)
                                nc.tensor.matmul(bank[5 + n % 3][:, 0:D], combT[:, n * P:(n + 1) * P], b2_sb[:],
                                                 start=True, stop=True).then_inc(row_ready, 1)

        def feed_forward(name, experts, tiles, hid, gated, func, bias=False, weighted=True, ternary=None, first=0):
            mats = 2 if gated else 1
            NB = 2 if gated else 4
            own = ExitStack()
            with own:
                if ternary:
                    up, down = ternary
                else:
                    up = sb(name + "_up_sb", [P, tiles, KT, mats, hid], F32, own)
                    down = sb(name + "_down_sb", [hid, tiles, D], F32, own)
                b1 = sb(name + "_b1_sb", [hid, tiles], F32, own)
                gate_act = sb(name + "_gate_act", [hid, 2, N], F32, own)
                hidden = sb(name + "_hidden", [hid, 2, tiles, N], F32, own)
                up_loaded = [shared(f"ff_up_loaded{i}") for i in range(2)]
                down_loaded = shared("ff_down_loaded")
                b1_loaded = shared("ff_b1_loaded")
                up_ready = shared("ff_up_ready")
                gate_ready = shared("ff_gate_ready")
                hidden_ready = shared("ff_hidden_ready")
                down_ready = shared("ff_down_ready")
                down_taken = shared("ff_down_taken")
                block = own.enter_context(nc.Block())
                per = 2 * tiles
                half = tiles // 2

                def over_experts(run, eng):
                    run(0, 0)
                    if experts > 1:
                        with eng.Fori(1, experts) as e:
                            run(e, 1)

                @block.sync
                def _(sp):
                    def load(e, i):
                        s = slice(i * half, (i + 1) * half)
                        sp.dma_start(up[:, s], a[name + "_up"][e][:, s]).then_inc(up_loaded[i], 16)

                    def run(e, later):
                        if not ternary:
                            for i in range(2):
                                if later:
                                    sp.wait_ge(up_ready, e * per - (1 - i) * half)
                                load(e, i)
                        if bias:
                            if later:
                                sp.wait_ge(hidden_ready, e * per)
                            sp.dma_start(b1[:], a[name + "_b1"][e]).then_inc(b1_loaded, 16)
                        if not ternary:
                            if later:
                                sp.wait_ge(down_ready, e * TT)
                            sp.dma_start(down[:], a[name + "_down"][e]).then_inc(down_loaded, 16)

                    over_experts(run, sp)

                @block.tensor
                def _(pe):
                    def run(e, later):
                        for h in range(2):
                            for t in range(tiles):
                                n = h * tiles + t
                                if h == 0 and t % half == 0 and not ternary:
                                    pe.wait_ge(up_loaded[t // half], e * 16 + 16)
                                if later or n >= NB:
                                    pe.wait_ge(hidden_ready, e * per + (n - NB + 1))
                                for m in range(mats):
                                    for k in range(KT):
                                        last = nc.tensor.matmul(bank[(n % NB) * mats + m][0:hid, :],
                                                                up[:, t, k, m, :], xnT[:, k, h * N:(h + 1) * N],
                                                                start=(k == 0), stop=(k == KT - 1))
                                last.then_inc(up_ready, 1)
                        if not ternary:
                            pe.wait_ge(down_loaded, e * 16 + 16)
                        for h in range(2):
                            pe.wait_ge(hidden_ready, e * per + (h + 1) * tiles)
                            for j in range(4):
                                n = h * 4 + j
                                if later or n >= 4:
                                    pe.wait_ge(down_taken, e * TT + (n - 3))
                                for t in range(tiles):
                                    last = nc.tensor.matmul(bank[4 + j][:, 0:D], hidden[:, h, t, j * P:(j + 1) * P],
                                                            down[:, t, :], start=(t == 0), stop=(t == tiles - 1))
                                last.then_inc(down_ready, 1)

                    over_experts(run, pe)

                @block.scalar
                def _(act):
                    def run(e, later):
                        for h in range(2):
                            for t in range(tiles):
                                n = h * tiles + t
                                if bias and n == 0:
                                    act.wait_ge(b1_loaded, e * 16 + 16)
                                act.wait_ge(up_ready, e * per + (n + 1))
                                src = bank[(n % NB) * mats][0:hid, :]
                                if gated:
                                    if later or n >= 2:
                                        act.wait_ge(hidden_ready, e * per + (n - 1))
                                    nc.scalar.activation(gate_act[:, n % 2, :], src, func).then_inc(gate_ready, 1)
                                else:
                                    if later and t == 0:
                                        act.wait_ge(down_ready, e * TT + (h * 4 - 4))
                                    nc.scalar.activation(hidden[:, h, t, :], src, func,
                                                         bias=b1[:, t:t + 1]).then_inc(hidden_ready, 1)

                    over_experts(run, act)

                @block.vector
                def _(dve):
                    def run(e, later):
                        if gated:
                            for h in range(2):
                                for t in range(tiles):
                                    n = h * tiles + t
                                    dve.wait_ge(gate_ready, e * per + (n + 1))
                                    if later and t == 0:
                                        dve.wait_ge(down_ready, e * TT + (h * 4 - 4))
                                    nc.vector.tensor_tensor(hidden[:, h, t, :], bank[(n % NB) * mats + 1][0:hid, :],
                                                            gate_act[:, n % 2, :], ALU.mult).then_inc(hidden_ready, 1)
                        for n in range(TT):
                            dve.wait_ge(down_ready, e * TT + (n + 1))
                            src = bank[4 + n % 4][:, 0:D]
                            if weighted:
                                w = comb[:, n, bass.ds(e + first, 1)]
                                nc.vector.scalar_tensor_tensor(out=x[:, n, :], in0=src, scalar=w, in1=x[:, n, :],
                                                               op0=ALU.mult, op1=ALU.add).then_inc(down_taken, 1)
                            else:
                                nc.vector.tensor_tensor(x[:, n, :], x[:, n, :], src, ALU.add).then_inc(down_taken, 1)

                    over_experts(run, dve)

        def glu_experts(name, rows_of):
            tiles = 4
            own = ExitStack()
            with own:
                up = sb(name + "_up_sb", [P, tiles, KT, 2, P], F32, own)
                b1 = sb(name + "_b1_sb", [P, tiles, 2], F32, own)
                wo = sb(name + "_wo_sb", [P, tiles, D], F32, own)
                bo = sb(name + "_bo_sb", [P, D], F32, own)
                sig = sb(name + "_sig", [P, 2, N], F32, own)
                glu = sb(name + "_glu", [P, 4, N], F32, own)
                total = sb(name + "_sum", [P, tiles, T], F32, own)
                up_loaded = shared("ff_up_loaded")
                wo_loaded = shared("ff_wo_loaded")
                up_ready = shared("ff_up_ready")
                sig_ready = shared("ff_sig_ready")
                glu_ready = shared("ff_glu_ready")
                weighed = shared("ff_weighed")
                summed = shared("ff_summed")
                down_ready = shared("ff_down_ready")
                down_taken = shared("ff_down_taken")
                block = own.enter_context(nc.Block())
                per = 2 * tiles

                def over_experts(run, eng):
                    run(0, 0)
                    with eng.Fori(1, E) as e:
                        run(e, 1)

                @block.sync
                def _(sp):
                    def run(e, later):
                        if later:
                            sp.wait_ge(up_ready, e * per)
                            sp.wait_ge(glu_ready, e * per)
                        sp.dma_start(up[:], a[name + "_up"][e]).then_inc(up_loaded, 16)
                        sp.dma_start(b1[:], a[name + "_b1"][e]).then_inc(up_loaded, 16)

                    run(0, 0)
                    sp.dma_start(wo[:], a[name + "_wo"]).then_inc(wo_loaded, 16)
                    sp.dma_start(bo[:], a[name + "_bo"].partition_broadcast(P)).then_inc(wo_loaded, 16)
                    with sp.Fori(1, E) as e:
                        run(e, 1)

                @block.tensor
                def _(pe):
                    def run(e, later):
                        pe.wait_ge(up_loaded, e * 32 + 32)
                        for n in range(per):
                            h, t = n // tiles, n % tiles
                            if later or n >= 2:
                                pe.wait_ge(glu_ready, e * per + (n - 1))
                            for m in range(2):
                                for k in range(KT):
                                    last = nc.tensor.matmul(bank[(n % 2) * 2 + m][:, :], up[:, t, k, m, :],
                                                            xnT[:, k, h * N:(h + 1) * N],
                                                            start=(k == 0), stop=(k == KT - 1))
                            last.then_inc(up_ready, 1)

                    over_experts(run, pe)
                    pe.wait_ge(wo_loaded, 32)
                    for j in range(TT):
                        if j % 4 == 0:
                            pe.wait_ge(summed, (E - 1) * per + (j // 4 + 1) * tiles)
                        if j >= 4:
                            pe.wait_ge(down_taken, j - 3)
                        for t in range(tiles):
                            last = nc.tensor.matmul(bank[4 + j % 4][:, 0:D], total[:, t, j * P:(j + 1) * P],
                                                    wo[:, t, :], start=(t == 0), stop=(t == tiles - 1))
                        last.then_inc(down_ready, 1)

                @block.scalar
                def _(act):
                    def run(e, later):
                        for n in range(per):
                            act.wait_ge(up_ready, e * per + (n + 1))
                            if later or n >= 2:
                                act.wait_ge(glu_ready, e * per + (n - 1))
                            nc.scalar.activation(sig[:, n % 2, :], bank[(n % 2) * 2 + 1][:, :], ACT.Sigmoid,
                                                 bias=b1[:, n % tiles, 1:2]).then_inc(sig_ready, 1)

                    over_experts(run, act)

                @block.vector
                def _(dve):
                    def run(e, later):
                        for n in range(per):
                            dve.wait_ge(sig_ready, e * per + (n + 1))
                            if later or n >= 4:
                                dve.wait_ge(summed, e * per + (n - 3))
                            nc.vector.scalar_tensor_tensor(out=glu[:, n % 4, :], in0=bank[(n % 2) * 2][:, :],
                                                           scalar=b1[:, n % tiles, 0:1], in1=sig[:, n % 2, :],
                                                           op0=ALU.add, op1=ALU.mult).then_inc(glu_ready, 1)

                    over_experts(run, dve)
                    for j in range(TT):
                        dve.wait_ge(down_ready, j + 1)
                        nc.vector.tensor_tensor(x[:, j, :], x[:, j, :], bank[4 + j % 4][:, 0:D],
                                                ALU.add).then_inc(down_taken, 1)
                    dve.wait_ge(wo_loaded, 32)
                    for j in range(TT):
                        dve.wait_ge(down_taken, j + 1)
                        nc.vector.scalar_tensor_tensor(out=x[:, j, :], in0=bo[:], scalar=comb[:, j, 0:1],
                                                       in1=x[:, j, :], op0=ALU.mult, op1=ALU.add).then_inc(down_taken, 1)
                    dve.wait_ge(down_taken, 2 * TT)

                @block.gpsimd
                def _(pool):
                    def run(e, later):
                        for n in range(per):
                            h, t = n // tiles, n % tiles
                            dst = total[:, t, h * N:(h + 1) * N]
                            w = rows_of[:, bass.ds(e, 1), h * N:(h + 1) * N].rearrange("p a n -> p (a n)")
                            pool.wait_ge(glu_ready, e * per + (n + 1))
                            pool.sem_inc(spare, 1)
                            if not later:
                                nc.gpsimd.tensor_tensor(dst, glu[:, n % 4, :], w, ALU.mult).then_inc(summed, 1)
                                continue
                            nc.gpsimd.tensor_tensor(glu[:, n % 4, :], glu[:, n % 4, :], w, ALU.mult).then_inc(weighed, 1)
                            pool.wait_ge(weighed, (e - 1) * per + (n + 1))
                            nc.gpsimd.tensor_tensor(dst, dst, glu[:, n % 4, :], ALU.add).then_inc(summed, 1)

                    over_experts(run, pool)

        def make_ternary(up, down):
            with ExitStack() as own:
                raw = [sb("tern_raw_up", [P, 2048], F32, own), sb("tern_raw_down", [P, 2048], F32, own)]
                below = sb("tern_below", [P, 2048], F32, own)
                mags = sb("tern_mags", [P, 2], F32, own)
                bound = sb("tern_bound", [P, 2, 2], F32, own)
                loaded = sem("tern_loaded")
                chain = sem("tern_chain")
                mags_ready = sem("tern_mags_ready")
                mean_ready = sem("tern_mean_ready")
                with nc.Block() as block:
                    @block.sync
                    def _(sp):
                        sp.dma_start(raw[0][:], a["L1f_up"]).then_inc(loaded, 16)
                        sp.dma_start(raw[1][:], a["L1f_down"]).then_inc(loaded, 16)

                    @block.tensor
                    def _(pe):
                        pe.wait_ge(mags_ready, 1)
                        nc.tensor.matmul(bank[0][:, 0:2], ones[:], mags[:], start=True, stop=True).then_inc(mean_ready, 1)

                    @block.vector
                    def _(dve):
                        done = [0]

                        def link(ins):
                            done[0] += 1
                            ins.then_inc(chain, 1)
                            dve.wait_ge(chain, done[0])

                        dve.wait_ge(loaded, 32)
                        for m in range(2):
                            last = nc.vector.tensor_reduce(mags[:, m:m + 1], raw[m][:], AX_X, ALU.add,
                                                           apply_absolute_value=True)
                        last.then_inc(mags_ready, 1)
                        dve.wait_ge(mean_ready, 1)
                        link(nc.vector.tensor_scalar(bound[:, :, 0], bank[0][:, 0:2], 1.0 / (P * 2048), 1e-8,
                                                     ALU.mult, ALU.max))
                        link(nc.vector.tensor_scalar(bound[:, :, 1], bound[:, :, 0], -0.5, None, ALU.mult))
                        link(nc.vector.tensor_scalar(bound[:, :, 0], bound[:, :, 0], 0.5, None, ALU.mult))
                        for m, dst in enumerate((up, down)):
                            link(nc.vector.tensor_scalar(below[:], raw[m][:], bound[:, m, 1:2], None, ALU.is_lt))
                            link(nc.vector.scalar_tensor_tensor(out=dst, in0=raw[m][:], scalar=bound[:, m, 0:1],
                                                                in1=below[:], op0=ALU.is_gt, op1=ALU.subtract))

        PAIRS = dict(nh=2, nc=1, groups=8, fills=PAIR)
        layer_norm("n0", bo="L0_bo")
        attention(Attention("L0", scale=1.0, bias=True, mask=None, **PAIRS))
        clear_shared()
        layer_norm("n1")
        with ExitStack() as own:
            rows_of = sb("L0f_rows", [P, E, T], F32, own)
            route("L0f", "top2", eps=1e-9, broadcast=rows_of)
            clear_shared()
            glu_experts("L0f", rows_of)
            clear_shared()
        layer_norm("n2", bo="L1_bo")
        attention(Attention("L1", scale=1 / 16, bias=True, mask="select", nh=1, nc=2, groups=1, fills=SINGLE))
        clear_shared()
        layer_norm("n3", bo="L1f_b2")
        with ExitStack() as own:
            up = sb("L1f_up_sb", [P, 8, KT, 1, P], F32, own)
            down = sb("L1f_down_sb", [P, 8, D], F32, own)
            make_ternary(up[:].rearrange("p t k m h -> p (t k m h)"), down[:].rearrange("p t d -> p (t d)"))
            feed_forward("L1f", 1, 8, P, False, ACT.Gelu, bias=True, weighted=False, ternary=(up, down))
            clear_shared()
        layer_norm("n4", bo="L2_bo")
        attention(Attention("L2", scale=1 / 4, bias=True, mask="add", nh=4, nc=1, groups=4, fills=QUAD))
        clear_shared()
        layer_norm("n5")
        route("L2f", "argmax", bias=True, b2="L2f_b2")
        clear_shared()
        feed_forward("L2f", E, 2, P, False, ACT.Relu, bias=True, first=1)
        clear_shared()
        layer_norm("n6")
        attention(Attention("L3", scale=1 / 8, bias=False, mask=None, **PAIRS))
        clear_shared()
        layer_norm("n7")
        route("L3f", "top2", eps=1e-8)
        clear_shared()
        feed_forward("L3f", 1 + E, 8, 118, True, ACT.Silu)
        clear_shared()

        with nc.Block() as block:
            @block.sync
            def _(sp):
                sp.dma_start(out.rearrange("(j p) d -> p j d", p=P), x[:]).then_inc(x_stored, 16)
                sp.wait_ge(x_stored, 16)





def kernel(**inputs):
    import numpy as np
    import concourse.bacc as bacc
    from concourse.bass_utils import run_bass_kernel_spmd as run

    i = {k: np.asarray(v) for k, v in inputs.items()}

    def grouped(w, groups, heads, rows, head_rows):
        per = heads // groups
        w = w.reshape(w.shape[0], groups, per, head_rows)
        if rows != head_rows:
            padded = np.zeros(w.shape[:3] + (rows,), w.dtype)
            padded[..., :head_rows] = w
            w = padded
        return w.transpose(1, 0, 2, 3).reshape(groups, w.shape[0], per * rows)

    def attention_arrays(name, wq, wk, wv, wo, biases, groups, heads, rows):
        dh = wq.shape[1] // heads
        g = [grouped(w, groups, heads, rows, dh) for w in (wq, wk, wv)]
        cols = g[0].shape[2]
        w = np.concatenate(g, axis=2).reshape(groups, KT, P, 3 * cols).transpose(0, 2, 1, 3)
        o = grouped(wo.T, groups, heads, rows, dh).transpose(0, 2, 1).reshape(groups, cols // P, P, D)
        arrays[name + "_wqkv"] = w
        arrays[name + "_wo"] = o.transpose(0, 2, 1, 3)
        if biases:
            q, k, v = (grouped(b[None], groups, heads, rows, dh)[:, 0] for b in biases)
            qk = np.concatenate([q, k], axis=1).reshape(groups, 2 * cols // P, P)
            arrays[name + "_bqk"] = qk.transpose(0, 2, 1)
            arrays[name + "_bv"] = v

    arrays = {"x": i["x"].reshape(T, D), "ctxT": i["ctx_1024"].reshape(B * SK, D).T}
    attention_arrays("L0", i["L0_xattn_Wq"].T, i["L0_xattn_Wk"].T, i["L0_xattn_Wv"].T, i["L0_xattn_Wo"].T,
                     [i["L0_xattn_b" + c] for c in "qkv"], 8, 16, 64)
    attention_arrays("L1", i["L1_xattn_Wq"].T, i["L1_xattn_Wk"].T, i["L1_xattn_Wv"].T, i["L1_xattn_Wo"].T,
                     [i["L1_xattn_b" + c] for c in "qkv"], 1, 1, 256)
    attention_arrays("L2", i["L2_xattn_Wq"], i["L2_xattn_Wk"], i["L2_xattn_Wv"], i["L2_xattn_Wo"],
                     [i["L2_xattn_b" + c] for c in "qkv"], 4, 16, 32)
    attention_arrays("L3", i["L3_xattn_Wq"], i["L3_xattn_Wk"], i["L3_xattn_Wv"], i["L3_xattn_Wo"], None, 8, 16, 64)
    for n in range(3):
        arrays[f"L{n}_bo"] = i[f"L{n}_xattn_bo"]
    arrays["L1_mask"] = i["mask_BxSxS2_if1"]
    arrays["L2_mask"] = i["mask_Bx1xSxS2_bk1"][:, 0]

    def columns(w, tiles, rows):
        e = w.shape[0]
        full = np.zeros((e, tiles * rows, D), w.dtype)
        full[:, :w.shape[1]] = w
        return full.reshape(e, tiles, rows, KT, P).transpose(0, 4, 1, 3, 2)

    def rows_first(w, tiles, rows):
        e = w.shape[0]
        full = np.zeros((e, D, tiles * rows), w.dtype)
        full[:, :, :w.shape[2]] = w
        return full.reshape(e, D, tiles, rows).transpose(0, 3, 2, 1)

    def gates(w):
        return w.reshape(E, KT, P).transpose(2, 1, 0)

    w1 = i["L0_ffn_W1"]
    arrays["L0f_wg"] = gates(i["L0_ffn_Wg"])
    arrays["L0f_up"] = np.stack([columns(w1[:, :512], 4, P), columns(w1[:, 512:], 4, P)], axis=4)
    arrays["L0f_b1"] = i["L0_ffn_b1"].reshape(E, 2, 4, P).transpose(0, 3, 2, 1)
    arrays["L0f_wo"] = rows_first(i["L0_ffn_Wo"][None], 4, P)[0]
    arrays["L0f_bo"] = i["L0_ffn_bo"]
    arrays["L1f_up"] = columns(i["L1_ffn_W1"][None], 8, P)[0].reshape(P, 2048)
    arrays["L1f_down"] = rows_first(i["L1_ffn_W2"][None], 8, P)[0].reshape(P, 2048)
    arrays["L1f_b1"] = i["L1_ffn_b1"].reshape(1, 8, P).transpose(0, 2, 1)
    arrays["L1f_b2"] = i["L1_ffn_b2"]
    arrays["L2f_wg"] = gates(i["L2_ffn_Ws"])
    arrays["L2f_gb"] = i["L2_ffn_bs"]
    arrays["L2f_up"] = columns(i["L2_ffn_W1"].transpose(0, 2, 1), 2, P)[:, :, :, :, None]
    arrays["L2f_down"] = rows_first(i["L2_ffn_W2"].transpose(0, 2, 1), 2, P)
    arrays["L2f_b1"] = i["L2_ffn_b1"].reshape(E, 2, P).transpose(0, 2, 1)
    arrays["L2f_b2"] = i["L2_ffn_b2"]
    gu = np.concatenate([i["L3_ffn_shared_gate_up"][None], i["L3_ffn_experts_gate_up"]])
    dn = np.concatenate([i["L3_ffn_shared_down"][None], i["L3_ffn_experts_down"]])
    width = dn.shape[2]
    arrays["L3f_wg"] = gates(i["L3_ffn_gate_weight"])
    arrays["L3f_up"] = np.stack([columns(gu[:, :width], 8, 118), columns(gu[:, width:], 8, 118)], axis=4)
    arrays["L3f_down"] = rows_first(dn, 8, 118)

    nc = bacc.Bacc("TRN2", target_bir_lowering=False, num_devices=1)
    feed, aps = {}, {}
    for name, v in arrays.items():
        v = np.ascontiguousarray(v)
        feed["in_" + name] = v
        aps[name] = nc.dram_tensor("in_" + name, v.shape, mybir.dt.from_np(v.dtype), kind="ExternalInput").ap()
    out = nc.dram_tensor("out_x", (T, D), F32, kind="ExternalOutput").ap()
    build(nc, aps, out)
    r = run(nc, [feed], core_ids=[0])
    return r.results[0]["out_x"].reshape(B, TB, D)
```

```python
from contextlib import ExitStack

import concourse.bass as bass
from concourse import mybir

F32 = mybir.dt.float32
BF16 = mybir.dt.bfloat16
F32R = mybir.dt.float32r
I32 = mybir.dt.int32
U32 = mybir.dt.uint32
U8 = mybir.dt.uint8
ALU = mybir.AluOpType
ACT = mybir.ActivationFunctionType
AX_X = mybir.AxisListType.X

P = 128
D = 256
KT = D // P
B = 2
TB = 512
T = B * TB
TT = T // P
TTB = TB // P
SK = 1024
SKT = SK // P
N = 512
E = 8
SLOT_TILES = 2 * TT + E
LN_EPS = 1e-5


class Attention:

    def __init__(self, name, groups, nh, nc, scale, bias, mask, fills, packed=False, twice=False):
        self.name, self.groups, self.nh, self.nc = name, groups, nh, nc
        self.rows = P // nh
        self.scale, self.bias, self.mask = scale, bias, mask
        self.packed, self.twice = packed, twice
        self.steps = TTB * nh
        self.half = self.steps // 2
        self.cols = P * nc
        self.projections = [("Q", c) for c in range(nc)] + [("K", c, n) for c in range(nc) for n in range(SK // N)] \
            + [("V", j) for j in range(SKT * self.cols // N)]
        self.schedule = fills

    def fills(self, kind):
        lag = ("R1", "O0", "O1")
        proj = ("Q", "K", "V")
        out = []
        for s, f in self.schedule:
            if f[0] in lag and kind == "first" or f[0] in proj and kind == "last":
                continue
            out.append((s, f))
        return out

    def index(self, kind, what):
        return [f for _, f in self.fills(kind)].index(what)


def fills_before(att, ph, k):
    kind, loop, c = ph
    n0 = len(att.projections)
    if kind == "first":
        return n0 + k
    full = len(att.fills("mid"))
    base = n0 + len(att.fills("first")) - full
    return count(ph, full, base + k)


def count(ph, per, off):
    _, loop, c = ph
    if loop is None:
        return per * c + off
    return loop * (2 * per) + (per * c + off)


PAIR = [(0, ("Q", 0)), (1, ("O0",)), (1, ("R1",)), (2, ("K", 0, 0)), (3, ("K", 0, 1)), (4, ("O1",)), (5, ("V", 0)), (5, ("R0",)), (6, ("V", 1))]
QUAD = [(1, ("O0",)), (2, ("R1",)), (3, ("Q", 0)), (4, ("K", 0, 0)), (5, ("K", 0, 1)), (9, ("R0",)),
        (10, ("O1",)), (12, ("V", 0)), (13, ("V", 1))]
SINGLE = [(0, ("R1",)), (0, ("O0",)), (0, ("Q", 0)), (0, ("Q", 1)), (1, ("K", 0, 0)), (1, ("K", 0, 1)),
          (1, ("K", 1, 0)), (1, ("K", 1, 1)), (2, ("R0",)), (2, ("O1",)), (2, ("V", 0)), (2, ("V", 1)),
          (3, ("V", 2)), (3, ("V", 3))]


def build(nc, a, out):
    ctx = ExitStack()
    with ctx:
        def sb(name, shape, dt=F32, where=ctx):
            return where.enter_context(nc.sbuf_tensor(name, shape, dt))

        def sem(name):
            return ctx.enter_context(nc.semaphore(name))

        psum = ctx.enter_context(nc.psum_tensor("psum", [P, 8, N], F32))
        pool_of_sems, lately_used = {}, []

        def shared(name):
            if name not in pool_of_sems:
                pool_of_sems[name] = sem(name)
            lately_used.append(pool_of_sems[name])
            return pool_of_sems[name]

        def clear_shared():
            with nc.Block() as block:
                @block.sync
                def _(sp):
                    for s in lately_used:
                        sp.sem_clear(s)
            lately_used.clear()

        bank = [psum[:, i, :] for i in range(8)]
        x = sb("x", [P, TT, D])
        xn = sb("xn", [P, TT, D])
        xnT = sb("xnT", [P, KT, T])
        ctxT = sb("ctxT", [P, KT, B * SK])
        ident = sb("ident", [P, P])
        iota = sb("iota", [P, E])
        weights = sb("weights", [P, 3, TT])
        put = sb("put", [P, 2, TT], I32)
        take = sb("take", [P, 2, TT], I32)
        tile_start = sb("tile_start", [P, E + 1], I32)
        zeros = sb("zeros", [P, D])
        rows_i = sb("rows_i", [P, TT], I32)
        token_no = sb("token_no", [P, TT])
        below = sb("below", [P, P])
        ones = sb("ones", [P, P])
        x_loaded = sem("x_loaded")
        ctx_loaded = sem("ctx_loaded")
        ident_made = sem("ident_made")
        x_stored = sem("x_stored")
        spare = sem("spare")
        zeros_made = sem("zeros_made")
        slots_cleared = sem("slots_cleared")
        by_slot = nc.dram_tensor("by_slot", (SLOT_TILES * P, D), F32, kind="Internal").ap()
        result_by_slot = nc.dram_tensor("result_by_slot", (SLOT_TILES * P, D), F32, kind="Internal").ap()

        with nc.Block() as block:
            @block.sync
            def _(sp):
                sp.dma_start(x[:], a["x"].rearrange("(j p) d -> p j d", p=P)).then_inc(x_loaded, 16)
                sp.dma_start(ctxT[:], a["ctxT"].rearrange("(k p) t -> p k t", p=P)).then_inc(ctx_loaded, 16)
                sp.wait_ge(zeros_made, 1)
                for rows in (by_slot, result_by_slot):
                    sp.dma_start(rows.rearrange("(g p) d -> p g d", p=P),
                                 zeros[:].unsqueeze(1).to_broadcast([P, SLOT_TILES, D])).then_inc(slots_cleared, 16)

            @block.gpsimd
            def _(pool):
                nc.gpsimd.memset(zeros[:], 0.0).then_inc(zeros_made, 1)
                nc.gpsimd.memset(ident[:], 0.0).then_inc(ident_made, 1)
                pool.wait_ge(ident_made, 1)
                nc.gpsimd.affine_select(out=ident[:], in_=ident[:], compare_op=ALU.not_equal, fill=1.0,
                                        base=0, pattern=[[-1, P]], channel_multiplier=1).then_inc(ident_made, 1)
                for e in range(E):
                    nc.gpsimd.memset(iota[:, e:e + 1], float(e)).then_inc(ident_made, 1)
                nc.gpsimd.memset(ones[:], 1.0).then_inc(ident_made, 1)
                nc.gpsimd.iota(rows_i[:], pattern=[[P, TT]], base=0, channel_multiplier=1).then_inc(ident_made, 1)
                pool.wait_ge(ident_made, 4 + E)
                nc.gpsimd.affine_select(out=below[:], in_=ones[:], compare_op=ALU.is_gt, fill=0.0,
                                        base=0, pattern=[[1, P]], channel_multiplier=-1).then_inc(ident_made, 1)
                nc.gpsimd.tensor_copy(token_no[:], rows_i[:]).then_inc(ident_made, 1)
                pool.wait_ge(ident_made, 6 + E)

            @block.vector
            def _(dve):
                dve.wait_ge(x_loaded, 16)

        norms = {"calls": 0, "chain": 0, "bo": 0}
        ln_chain = sem("ln_chain")
        ln_bo_loaded = sem("ln_bo_loaded")
        ln_var_ready = sem("ln_var_ready")
        ln_sd_ready = sem("ln_sd_ready")
        ln_xn_ready = sem("ln_xn_ready")
        ln_tr_ready = sem("ln_tr_ready")
        ln_transposed = sem("ln_transposed")

        def layer_norm(name, bo=None):
            n = norms["calls"]
            norms["calls"] += 1
            with ExitStack() as own:
                stats = sb(name + "_stats", [P, TT, 6], F32, own)
                mv = sb(name + "_mv", [P, TT, 2], F32, own)
                ve = sb(name + "_ve", [P, TT], F32, own)
                sd = sb(name + "_sd", [P, TT], F32, own)
                r0 = sb(name + "_r0", [P, TT], F32, own)
                w = sb(name + "_w", [P, TT], F32, own)
                bo_all = sb(name + "_bo", [P, D], F32, own)
                with nc.Block() as block:
                    @block.sync
                    def _(sp):
                        if bo is not None:
                            norms["bo"] += 1
                            sp.dma_start(bo_all[:], a[bo].partition_broadcast(P)).then_inc(ln_bo_loaded, 16)

                    @block.vector
                    def _(dve):
                        def link(ins):
                            norms["chain"] += 1
                            ins.then_inc(ln_chain, 1)
                            dve.wait_ge(ln_chain, norms["chain"])

                        for j in range(TT):
                            last = nc.vector.bn_stats(stats[:, j, :], x[:, j, :])
                        link(last)
                        for j in range(TT):
                            last = nc.vector.bn_aggr(mv[:, j, :], stats[:, j, :])
                        link(last)
                        nc.vector.tensor_scalar(ve[:], mv[:, :, 1], LN_EPS, None, ALU.add).then_inc(ln_var_ready, 1)
                        dve.wait_ge(ln_sd_ready, n + 1)
                        link(nc.vector.reciprocal(r0[:], sd[:]))
                        link(nc.vector.tensor_tensor(w[:], r0[:], r0[:], ALU.mult))
                        link(nc.vector.tensor_tensor(w[:], w[:], ve[:], ALU.mult))
                        link(nc.vector.tensor_scalar(w[:], w[:], -0.5, 1.5, ALU.mult, ALU.add))
                        link(nc.vector.tensor_tensor(r0[:], r0[:], w[:], ALU.mult))
                        for j in range(TT):
                            nc.vector.tensor_scalar(xn[:, j, :], x[:, j, :], mv[:, j, 0:1], r0[:, j:j + 1],
                                                    ALU.subtract, ALU.mult).then_inc(ln_xn_ready, 1)
                        if bo is not None:
                            dve.wait_ge(ln_bo_loaded, 16 * norms["bo"])
                            dve.wait_ge(ln_xn_ready, (n + 1) * TT)
                            link(nc.vector.tensor_tensor(x[:], x[:], bo_all[:].unsqueeze(1).to_broadcast([P, TT, D]),
                                                         ALU.add))
                        for k in range(KT):
                            dve.wait_ge(ln_tr_ready, 2 * KT * n + 2 * k + 2)
                            nc.vector.tensor_copy(xnT[:, k, N:2 * N], bank[2 * k + 1][:, :]).then_inc(ln_transposed, 1)

                    @block.scalar
                    def _(act):
                        act.wait_ge(ln_var_ready, n + 1)
                        nc.scalar.activation(sd[:], ve[:], ACT.Sqrt).then_inc(ln_sd_ready, 1)
                        for k in range(KT):
                            act.wait_ge(ln_tr_ready, 2 * KT * n + 2 * k + 1)
                            nc.scalar.copy(xnT[:, k, 0:N], bank[2 * k][:, :]).then_inc(ln_transposed, 1)

                    @block.tensor
                    def _(pe):
                        pe.wait_ge(ident_made, 2)
                        for k in range(KT):
                            for h in range(2):
                                for j in range(4):
                                    if k == 0:
                                        pe.wait_ge(ln_xn_ready, n * TT + 4 * h + j + 1)
                                    last = nc.tensor.transpose(bank[2 * k + h][:, j * P:(j + 1) * P],
                                                               xn[:, 4 * h + j, k * P:(k + 1) * P], ident[:])
                                last.then_inc(ln_tr_ready, 1)

        def attention(att):
            nm = att.name
            nh, ncc, rows, steps, half, cols = att.nh, att.nc, att.rows, att.steps, att.half, att.cols
            G = att.groups
            kpb = N // cols
            loads = 3 if att.bias else 1
            own = ExitStack()
            with own:
                if att.packed:
                    Q = sb(nm + "_Q", [P, B, nh, TB], F32R, own)
                    K = sb(nm + "_K", [P, B, 1 if att.twice else nh, 2, SK], F32R, own)
                    q_raw = sb(nm + "_q_raw", [P, TB], F32, own)
                    k_raw = sb(nm + "_k_raw", [P, SK], F32, own)
                    if att.twice:
                        q_near = sb(nm + "_q_near", [P, TB], F32R, own)
                        q_off = sb(nm + "_q_off", [P, TB], F32, own)
                        low_row = sb(nm + "_low_row", [P, 1], F32, own)
                        low_row_i = sb(nm + "_low_row_i", [P, 1], I32, own)
                    else:
                        q_low = sb(nm + "_q_low", [P, TB], F32R, own)
                else:
                    Q = sb(nm + "_Q", [P, B, max(nh, ncc), TB], F32, own)
                    K = sb(nm + "_K", [P, B, ncc, SK], F32, own)
                own_rows = [slice(h * rows, (h + 1) * rows) for h in range(nh)]
                other_rows = own_rows[::-1]
                copies = 16 * 2 * (1 + SK // N)
                V = sb(nm + "_V", [P, B, SKT, cols], F32, own)
                prob = sb(nm + "_prob", [P, 2, SK], F32, own)
                probT = sb(nm + "_probT", [P, 2, nh, SKT, 2 * P], F32, own)
                wqkv = sb(nm + "_wqkv", [P, KT, 3 * cols], F32, own)
                wo = sb(nm + "_wo", [P, ncc, D], F32, own)
                negmax = sb(nm + "_negmax", [P, steps], F32, own)
                sums = sb(nm + "_sums", [P, steps], F32, own)
                recip = sb(nm + "_recip", [P, 2, nh], F32, own)
                rexp = sb(nm + "_rexp", [P, 2, nh, rows], F32, own)
                rall = sb(nm + "_rall", [P, 2 * P], F32, own)
                OT = sb(nm + "_OT", [P, ncc, 2 * P], F32, own)
                if att.bias:
                    bqk = sb(nm + "_bqk", [P, 2 * ncc], F32, own)
                    bv = sb(nm + "_bv", [P, cols], F32, own)
                if att.mask:
                    masked = prob if att.twice else sb(nm + "_masked", [P, 2, SK], F32, own)
                    top = sb(nm + "_top", [P, steps], F32, own)
                if att.mask == "add":
                    mraw = xn[:].bitcast(U8)
                    mbias = sb(nm + "_mbias", [P, B * TTB, SK], BF16, own)
                if att.mask == "select":
                    mraw = sb(nm + "_mraw", [P, B * TTB, SK], I32, own)
                    keep = sb(nm + "_keep", [P, SK], F32, own)
                    mbias = sb(nm + "_mbias", [P, SK], F32, own)
                w_loaded = shared("att_w_loaded")
                wo_loaded = shared("att_wo_loaded")
                k_high = shared("att_k_high")
                q_high = shared("att_q_high")
                low_row_made = shared("att_low_row_made")
                near_ready = shared("att_near_ready")
                low_chain = shared("att_low_chain")
                qk_split = shared("att_qk_split")
                qk_copied = shared("att_qk_copied")
                mask_loaded = shared("att_mask_loaded")
                mask_made = shared("att_mask_made")
                q_zeroed = shared("att_q_zeroed")
                scores_ready = shared("att_scores_ready")
                max_ready = shared("att_max_ready")
                dve_chain = shared("att_dve_chain")
                prob_ready = shared("att_prob_ready")
                tr_ready = shared("att_tr_ready")
                evac_act = shared("att_evac_act")
                evac_dve = shared("att_evac_dve")
                fill_ready = shared("att_fill_ready")
                fill_taken = shared("att_fill_taken")
                pv_ready = shared("att_pv_ready")
                o_taken = shared("att_o_taken")
                recip_ready = shared("att_recip_ready")
                rsum_ready = shared("att_rsum_ready")
                S = [(bank[0], bank[1]), (bank[2], bank[3])]
                SPAN = [psum[:, 0:2, :].rearrange("p a n -> p (a n)"), psum[:, 2:4, :].rearrange("p a n -> p (a n)")]
                TR = (bank[4], bank[5])
                OB = bank[6]
                FB = bank[7]
                scores_free = max_ready if att.mask else prob_ready

                def phases(run, eng):
                    run(("first", None, 0), 0)
                    if G > 1:
                        with eng.Fori(0, G - 1) as i:
                            run(("mid", i, 1), 1)
                            run(("mid", i, 2), 0)
                    run(("last", None, 2 * G - 1), 1)

                block = own.enter_context(nc.Block())

                @block.sync
                def _(sp):
                    def load_w(g):
                        sp.dma_start(wqkv[:], a[nm + "_wqkv"][g]).then_inc(w_loaded, 16)
                        if att.bias:
                            sp.dma_start(bqk[:], a[nm + "_bqk"][g]).then_inc(w_loaded, 16)
                            sp.dma_start(bv[:], a[nm + "_bv"][g].partition_broadcast(P)).then_inc(w_loaded, 16)

                    load_w(0)
                    sp.dma_start(wo[:], a[nm + "_wo"][0]).then_inc(wo_loaded, 16)
                    if att.mask:
                        for b in range(B):
                            sp.dma_start(mraw[:, b * TTB:(b + 1) * TTB, :],
                                         a[nm + "_mask"][b].rearrange("(j p) s -> p j s", p=P)).then_inc(mask_loaded, 16)
                    def copy_rows(b, n_split):
                        sp.wait_ge(qk_split, n_split(1))
                        for h in range(nh):
                            sp.dma_start(Q[other_rows[h], b, h, :].bitcast(F32), q_low[own_rows[h], :].bitcast(F32)).then_inc(qk_copied, 16)
                        for n in range(SK // N):
                            sp.wait_ge(qk_split, n_split(n + 2))
                            for h in range(nh):
                                part = K[:, b, h, :, n * N:(n + 1) * N].bitcast(F32)
                                sp.dma_start(part[other_rows[h]], part[own_rows[h]]).then_inc(qk_copied, 16)

                    if att.packed and not att.twice:
                        copy_rows(0, lambda i: i)

                        def phase(ph, b):
                            kind = ph[0]
                            if kind != "last":
                                copy_rows(1 - b, lambda i: count(ph, 3, 3 + i))
                            if kind == "mid" and ph[2] == 2:
                                sp.wait_ge(fill_taken, fills_before(att, ph, att.index(kind, ("O1",)) + 1))
                                sp.dma_start(wo[:], a[nm + "_wo"][ph[1] + 1]).then_inc(wo_loaded, 16)
                            if kind == "first" or kind == "mid" and ph[2] == 2:
                                sp.wait_ge(fill_taken, fills_before(att, ph, att.index(kind, ("V", 1)) + 1))
                                load_w(1 if kind == "first" else ph[1] + 2)

                        phases(phase, sp)
                        sp.wait_ge(w_loaded, 16 * loads * (G + 1))
                    elif G > 1:
                        lastv = ("V", len([f for f in att.projections if f[0] == "V"]) - 1)
                        ph = ("first", None, 0)
                        sp.wait_ge(fill_taken, fills_before(att, ph, att.index("first", lastv)) + 1)
                        load_w(1)

                        def load_wo(ph, g):
                            sp.wait_ge(fill_taken, fills_before(att, ph, att.index("mid", ("O1",)) + 1))
                            sp.dma_start(wo[:], a[nm + "_wo"][g]).then_inc(wo_loaded, 16)
                        if G > 2:
                            with sp.Fori(0, G - 2) as i:
                                ph = ("mid", i, 2)
                                load_wo(ph, i + 1)
                                sp.wait_ge(fill_taken, fills_before(att, ph, att.index("mid", lastv) + 1))
                                load_w(i + 2)
                        load_wo(("mid", None, 2 * G - 2), G - 1)

                @block.tensor
                def _(pe):
                    def fill(ph, f, k, b):
                        if k is None:
                            before = att.projections.index(f)
                        else:
                            before = fills_before(att, ph, k)
                        if k is not None or before:
                            pe.wait_ge(fill_taken, before)
                        kind = f[0]
                        if kind == "Q":
                            if f[1] == 0:
                                if k is None:
                                    pe.wait_ge(w_loaded, 16 * loads)
                                    pe.wait_ge(ctx_loaded, 16)
                                elif ph[0] == "mid" and ph[2] == 1:
                                    pe.wait_ge(w_loaded, ph[1] * (16 * loads) + 32 * loads)
                            for kt in range(KT):
                                last = nc.tensor.matmul(FB[:, :], wqkv[:, kt, f[1] * P:(f[1] + 1) * P],
                                                        xnT[:, kt, b * TB:(b + 1) * TB],
                                                        start=(kt == 0), stop=(kt == KT - 1))
                        elif kind == "K":
                            for kt in range(KT):
                                last = nc.tensor.matmul(FB[:, :], wqkv[:, kt, cols + f[1] * P:cols + (f[1] + 1) * P],
                                                        ctxT[:, kt, b * SK + f[2] * N:b * SK + (f[2] + 1) * N],
                                                        start=(kt == 0), stop=(kt == KT - 1))
                        elif kind == "V":
                            for i in range(kpb):
                                t = f[1] * kpb + i
                                for kt in range(KT):
                                    last = nc.tensor.matmul(FB[:, i * cols:(i + 1) * cols],
                                                            ctxT[:, kt, b * SK + t * P:b * SK + (t + 1) * P],
                                                            wqkv[:, kt, 2 * cols:3 * cols],
                                                            start=(kt == 0), stop=(kt == KT - 1))
                        elif kind in ("R0", "R1"):
                            h = int(kind[1])
                            pe.wait_ge(rsum_ready, count(ph, 2, h + 1 if h == 0 else 0))
                            for q in range(2):
                                last = nc.tensor.matmul(FB[:, q * P:(q + 1) * P],
                                                        rexp[:, q].rearrange("p h r -> p (h r)"), ident[:],
                                                        start=True, stop=True)
                        else:
                            h = int(kind[1])
                            pe.wait_ge(o_taken, count(ph, 2, h - 1))
                            if h == 0:
                                if ph[0] == "mid" and ph[2] == 1:
                                    pe.wait_ge(wo_loaded, ph[1] * 16 + 16)
                                elif ph[0] == "last":
                                    pe.wait_ge(wo_loaded, 16 * G)
                            for q in range(2):
                                for c in range(ncc):
                                    last = nc.tensor.matmul(FB[:, q * D:(q + 1) * D], OT[:, c, q * P:(q + 1) * P],
                                                            wo[:, c, :], start=(c == 0), stop=(c == ncc - 1))
                        last.then_inc(fill_ready, 1)

                    def scores(ph, s, b):
                        t, h = s // nh, s % nh
                        for n in range(SK // N):
                            for part in range(2 if att.packed else 0):
                                last = nc.tensor.matmul(S[s % 2][n][:, :], Q[:, b, h, t * P:(t + 1) * P],
                                                        K[:, b, 0 if att.twice else h, part, n * N:(n + 1) * N],
                                                        start=(part == 0), stop=(part == 1))
                            for c in range(0 if att.packed else ncc):
                                lhs = Q[:, b, c if ncc > 1 else h, t * P:(t + 1) * P]
                                last = nc.tensor.matmul(S[s % 2][n][:, :], lhs, K[:, b, c, n * N:(n + 1) * N],
                                                        start=(c == 0), stop=(c == ncc - 1))
                        last.then_inc(scores_ready, 1)

                    def pv(ph, hf, b, part, parts):
                        if ncc == 1:
                            todo = [(kt, h, 0) for kt in range(SKT) for h in range(nh)]
                        else:
                            todo = [(kt, 0, c) for c in range(ncc) for kt in range(SKT)]
                        m = len(todo) // parts
                        for kt, h, c in todo[part * m:(part + 1) * m]:
                            o = OB[h * rows:(h + 1) * rows, c * 2 * P:(c + 1) * 2 * P]
                            last = nc.tensor.matmul(o, V[:, b, kt, (h * rows if ncc == 1 else c * P):
                                                              ((h + 1) * rows if ncc == 1 else (c + 1) * P)],
                                                    probT[:, hf, h, kt, :], start=(kt == 0), stop=(kt == SKT - 1))
                        if part == parts - 1:
                            last.then_inc(pv_ready, 1)

                    def pv_waits(ph, hf):
                        pe.wait_ge(evac_act, count(ph, steps, half * (hf + 1)))
                        pe.wait_ge(evac_dve, count(ph, steps, half * (hf + 1)))
                        if not (ph[0] == "first" and hf == 0):
                            pe.wait_ge(o_taken, count(ph, 2, hf))

                    def before(ph):
                        return (ph[0], ph[1], ph[2] - 1)

                    def transposes(ph, s):
                        pe.wait_ge(prob_ready, count(ph, steps, s + 1))
                        for i in range(2):
                            if not (ph[0] == "first" and s == 0):
                                pe.wait_ge(evac_dve if i else evac_act, count(ph, steps, s))
                            for j in range(4):
                                kt = 4 * i + j
                                last = nc.tensor.transpose(TR[i][:, j * P:(j + 1) * P],
                                                           prob[:, s % 2, kt * P:(kt + 1) * P], ident[:])
                            last.then_inc(tr_ready, 1)

                    def phase(ph, b):
                        kind = ph[0]
                        fl = att.fills(kind)
                        for s in range(steps):
                            if s + 1 < steps:
                                if not (kind == "first" and s == 0):
                                    pe.wait_ge(scores_free, count(ph, steps, s))
                                scores(ph, s + 1, b)
                            elif kind != "last":
                                pe.wait_ge(scores_free, count(ph, steps, s))
                                if att.twice:
                                    pe.wait_ge(qk_split, count(ph, 3, 6))
                                elif att.packed:
                                    pe.wait_ge(qk_copied, count(ph, copies, 2 * copies))
                                else:
                                    pe.wait_ge(fill_taken, fills_before(att, ph, att.index(kind, ("K", ncc - 1, 1)) + 1))
                                scores(ph, 0, 1 - b)
                            now = [(k, f) for k, (fs, f) in enumerate(fl) if fs == s]
                            cut = len(now) // 2 if len(now) > 1 else len(now)
                            for k, f in now[:cut]:
                                fill(ph, f, k, 1 - b)
                            if s < half:
                                if kind != "first":
                                    if s == 0:
                                        pv_waits(before(ph), 1)
                                    pv(ph, 1, 1 - b, s, half)
                            else:
                                if s == half:
                                    pv_waits(ph, 0)
                                pv(ph, 0, b, s - half, half)
                            for k, f in now[cut:]:
                                fill(ph, f, k, 1 - b)
                            transposes(ph, s)

                    if not att.packed or att.twice:
                        pe.wait_ge(q_zeroed, 1)
                    for f in att.projections:
                        fill(None, f, None, 0)
                    pe.wait_ge(fill_taken, len(att.projections))
                    if att.twice:
                        pe.wait_ge(qk_split, 3)
                    elif att.packed:
                        pe.wait_ge(qk_copied, copies)
                    scores(None, 0, 0)
                    phases(phase, pe)
                    end = ("mid", None, 2 * G)
                    n0 = len(att.projections) + len(att.fills("first")) + (2 * G - 2) * len(att.fills("mid")) \
                        + len(att.fills("last"))
                    for k, f in enumerate((("R1",), ("O0",), ("O1",))):
                        if k == 2:
                            pv_waits(("last", None, 2 * G - 1), 1)
                            pv(end, 1, 1, 0, 1)
                        pe.wait_ge(fill_taken, n0 + k)
                        h = int(f[0][1])
                        if k == 0:
                            pe.wait_ge(rsum_ready, 4 * G)
                            for q in range(2):
                                last = nc.tensor.matmul(FB[:, q * P:(q + 1) * P],
                                                        rexp[:, q].rearrange("p h r -> p (h r)"), ident[:],
                                                        start=True, stop=True)
                        else:
                            pe.wait_ge(o_taken, 4 * G - 1 + h)
                            for q in range(2):
                                for c in range(ncc):
                                    last = nc.tensor.matmul(FB[:, q * D:(q + 1) * D], OT[:, c, q * P:(q + 1) * P],
                                                            wo[:, c, :], start=(c == 0), stop=(c == ncc - 1))
                        last.then_inc(fill_ready, 1)

                tail_fills = len(att.projections) + len(att.fills("first")) + (2 * G - 2) * len(att.fills("mid")) \
                    + len(att.fills("last"))

                @block.scalar
                def _(act):
                    def take(f, n, b):
                        act.wait_ge(fill_ready, n)
                        if f[0] == "K" and att.packed:
                            cut = slice(f[2] * N, (f[2] + 1) * N)
                            if att.bias:
                                nc.scalar.activation(k_raw[:, cut], FB[:, :], ACT.Identity,
                                                     bias=bqk[:, 1:2]).then_inc(fill_taken, 1)
                            else:
                                nc.scalar.copy(k_raw[:, cut], FB[:, :]).then_inc(fill_taken, 1)
                            act.wait_ge(fill_taken, n)
                            for h, r in enumerate([slice(0, P)] if att.twice else own_rows):
                                last = nc.scalar.copy(K[r, b, h, 0, cut], k_raw[r, cut])
                            last.then_inc(k_high, 1)
                        elif f[0] == "K":
                            dst = K[:, b, f[1], f[2] * N:(f[2] + 1) * N]
                            if att.bias:
                                nc.scalar.activation(dst, FB[:, :], ACT.Identity,
                                                     bias=bqk[:, ncc + f[1]:ncc + f[1] + 1]).then_inc(fill_taken, 1)
                            else:
                                nc.scalar.copy(dst, FB[:, :]).then_inc(fill_taken, 1)
                        else:
                            nc.scalar.copy(rall[:], FB[:, 0:2 * P]).then_inc(fill_taken, 1)

                    def exps(ph, s, off):
                        act.wait_ge(max_ready, count(ph, steps, off + 1))
                        if not (ph[0] == "first" and off < 2):
                            act.wait_ge(tr_ready, count(ph, 2 * steps, 2 * off - 2))
                        src = masked[:, s % 2, :] if att.mask else None
                        if att.mask:
                            nc.scalar.activation(prob[:, s % 2, :], src, ACT.Exp, bias=negmax[:, s:s + 1],
                                                 accum_out=sums[:, s:s + 1]).then_inc(prob_ready, 1)
                        else:
                            nc.scalar.activation(prob[:, s % 2, :], SPAN[s % 2], ACT.Exp, bias=negmax[:, s:s + 1],
                                                 accum_out=sums[:, s:s + 1]).then_inc(prob_ready, 1)

                    def phase(ph, b):
                        kind = ph[0]
                        fl = att.fills(kind)
                        for s in range(steps):
                            if s + 1 < steps:
                                exps(ph, s + 1, s + 1)
                            elif kind != "last":
                                exps(ph, 0, steps)
                            for k, (fs, f) in enumerate(fl):
                                if fs == s and f[0] in ("K", "R0", "R1"):
                                    if f[0][0] == "R":
                                        if kind != "first":
                                            act.wait_ge(o_taken, count(ph, 2, 0 if f[0] == "R0" else -1))
                                    take(f, fills_before(att, ph, k + 1), 1 - b)
                            hf, h, q = s // half, s % nh, s // nh % 2
                            act.wait_ge(tr_ready, count(ph, 2 * steps, 2 * s + 1))
                            if s % half == 0 and kind != "first":
                                act.wait_ge(pv_ready, count(ph, 2, hf - 1))
                            nc.scalar.copy(probT[:, hf, h, 0:4, q * P:(q + 1) * P],
                                           TR[0][:, :].rearrange("p (k q) -> p k q", q=P)).then_inc(evac_act, 1)

                    for n, f in enumerate(att.projections):
                        if f[0] == "K":
                            take(f, n + 1, 0)
                    exps(("first", None, 0), 0, 0)
                    phases(phase, act)
                    act.wait_ge(o_taken, 4 * G - 1)
                    take(("R1",), tail_fills + 1, 1)

                @block.vector
                def _(dve):
                    if att.twice:
                        dve.wait_ge(low_row_made, 1)
                        nc.vector.tensor_scalar(low_row_i[:], low_row_i[:], 4, 1, ALU.logical_shift_right,
                                                ALU.bitwise_and).then_inc(low_row_made, 1)
                        dve.wait_ge(low_row_made, 2)
                        nc.vector.tensor_copy(low_row[:], low_row_i[:]).then_inc(low_row_made, 1)
                        dve.wait_ge(low_row_made, 3)
                        nc.vector.memset(Q[:].bitcast(F32), 0.0).then_inc(q_zeroed, 1)
                        dve.wait_ge(q_zeroed, 1)
                    elif att.packed:
                        pass
                    elif ncc == 1:
                        nc.vector.memset(Q[:], 0.0).then_inc(q_zeroed, 1)
                        dve.wait_ge(q_zeroed, 1)
                    else:
                        nc.vector.memset(sums[:], 0.0).then_inc(q_zeroed, 1)
                        dve.wait_ge(q_zeroed, 1)
                    if att.mask == "add":
                        dve.wait_ge(mask_loaded, 16 * B)
                        for j in range(B * TTB):
                            nc.vector.tensor_scalar(mbias[:, j, :], mraw[:, j, :], 0.0, -1e15,
                                                    ALU.not_equal, ALU.mult).then_inc(mask_made, 1)
                        dve.wait_ge(mask_made, B * TTB)

                    def maxes(ph, s, off, b):
                        if att.mask == "select":
                            j = b * TTB + s
                            if j:
                                dve.wait_ge(max_ready, j)
                            else:
                                dve.wait_ge(mask_loaded, 16 * B)
                            nc.vector.tensor_scalar(keep[:], mraw[:, j, :], 0.0, None, ALU.not_equal).then_inc(mask_made, 1)
                            nc.vector.tensor_scalar(mbias[:], mraw[:, j, :], 0.0, -1e9,
                                                    ALU.is_equal, ALU.mult).then_inc(mask_made, 1)
                            dve.wait_ge(mask_made, 2 * j + 2)
                        dve.wait_ge(scores_ready, count(ph, steps, off + 1))
                        if not att.mask:
                            nc.vector.tensor_reduce(negmax[:, s:s + 1], SPAN[s % 2], AX_X, ALU.max,
                                                    negate=True).then_inc(max_ready, 1)
                            return
                        if not (ph[0] == "first" and off < 2):
                            if att.twice:
                                dve.wait_ge(tr_ready, count(ph, 2 * steps, 2 * off - 2))
                            else:
                                dve.wait_ge(prob_ready, count(ph, steps, off - 1))
                        src, mb = SPAN[s % 2], None
                        if att.mask == "select":
                            nc.vector.tensor_tensor(masked[:, s % 2, :], src, keep[:], ALU.mult).then_inc(dve_chain, 1)
                            dve.wait_ge(dve_chain, count(ph, 2 * steps, 2 * off + 1))
                            src, mb = masked[:, s % 2, :], mbias[:]
                        else:
                            mb = mbias[:, b * TTB + s // nh, :]
                        dve.sem_inc(spare, 1)
                        nc.vector.tensor_tensor_reduce(masked[:, s % 2, :], src, mb, 1.0, -3e38, ALU.add, ALU.max,
                                                       top[:, s:s + 1]).then_inc(dve_chain, 1)
                        per = 2 if att.mask == "select" else 1
                        dve.wait_ge(dve_chain, count(ph, per * steps, per * (off + 1)))
                        nc.vector.tensor_scalar(negmax[:, s:s + 1], top[:, s:s + 1], -1.0, None,
                                                ALU.mult).then_inc(max_ready, 1)

                    dve_takes = ("Q", "V", "O0", "O1")

                    def take_q(n, b, n_near):
                        if att.bias:
                            nc.vector.tensor_scalar(q_raw[:], FB[:, :], bqk[:, 0:1], att.scale,
                                                    ALU.add, ALU.mult).then_inc(fill_taken, 1)
                        else:
                            nc.vector.tensor_scalar(q_raw[:], FB[:, :], att.scale, None, ALU.mult).then_inc(fill_taken, 1)
                        dve.wait_ge(fill_taken, n)
                        if att.twice:
                            nc.vector.tensor_copy(q_near[:], q_raw[:]).then_inc(near_ready, 1)
                            dve.wait_ge(near_ready, n_near)
                            last = nc.vector.tensor_scalar(q_off[:], q_near[:], low_row[:, 0:1], None, ALU.mult)
                        for h, r in enumerate([] if att.twice else own_rows):
                            last = nc.vector.tensor_copy(Q[r, b, h, :], q_raw[r, :])
                        last.then_inc(q_high, 1)

                    def take(f, n, b, ph=None):
                        dve.wait_ge(fill_ready, n)
                        if f[0] == "Q" and att.packed:
                            take_q(n, b, 1 if ph is None else count(ph, 1, 2))
                        elif f[0] == "Q":
                            for h in range(nh):
                                r = slice(h * rows, (h + 1) * rows)
                                dst = Q[r, b, h if ncc == 1 else f[1], :]
                                if att.bias:
                                    last = nc.vector.tensor_scalar(dst, FB[r, :], bqk[r, f[1]:f[1] + 1], att.scale,
                                                                   ALU.add, ALU.mult)
                                else:
                                    last = nc.vector.tensor_scalar(dst, FB[r, :], att.scale, None, ALU.mult)
                            last.then_inc(fill_taken, 1)
                        elif f[0] == "V":
                            dst = V[:, b, f[1] * kpb:(f[1] + 1) * kpb, :]
                            src = FB[:, :].rearrange("p (k c) -> p k c", c=cols)
                            if att.bias:
                                nc.vector.tensor_tensor(dst, src, bv[:].unsqueeze(1).to_broadcast([P, kpb, cols]),
                                                        ALU.add).then_inc(fill_taken, 1)
                            else:
                                nc.vector.tensor_copy(dst, src).then_inc(fill_taken, 1)
                        else:
                            j = b * TTB + 2 * int(f[0][1])
                            nc.vector.tensor_tensor(x[:, j:j + 2, :], x[:, j:j + 2, :],
                                                    FB[:, :].rearrange("p (q d) -> p q d", d=D),
                                                    ALU.add).then_inc(fill_taken, 1)

                    def reciprocals(ph, hf, done):
                        dve.wait_ge(prob_ready, done)
                        s0 = hf * half
                        src = sums[:, s0:s0 + half].rearrange("p (q h) -> p q h", h=nh)
                        nc.vector.reciprocal(recip[:], src).then_inc(recip_ready, 1)

                    def normalise(n_pv, n_fill):
                        dve.wait_ge(pv_ready, n_pv)
                        dve.wait_ge(fill_taken, n_fill)
                        if ncc == 1:
                            nc.vector.tensor_tensor(OT[:, 0, :], OB[:, 0:2 * P], rall[:], ALU.mult).then_inc(o_taken, 1)
                        else:
                            nc.vector.tensor_tensor(OT[:], OB[:, :].rearrange("p (c q) -> p c q", c=ncc),
                                                    rall[:].unsqueeze(1).to_broadcast([P, ncc, 2 * P]),
                                                    ALU.mult).then_inc(o_taken, 1)

                    def phase(ph, b):
                        kind = ph[0]
                        fl = att.fills(kind)
                        names = [f for _, f in fl]
                        for s in range(steps):
                            if s == 0 and kind != "first":
                                reciprocals(ph, 1, count(ph, steps, 0))
                            if s == half:
                                reciprocals(ph, 0, count(ph, steps, half))
                            if s + 1 < steps:
                                maxes(ph, s + 1, s + 1, b)
                            elif kind != "last":
                                maxes(ph, 0, steps, 1 - b)
                            for k, (fs, f) in enumerate(fl):
                                if fs == s and f[0] in dve_takes:
                                    take(f, fills_before(att, ph, k + 1), 1 - b, ph)
                            if s == half - 1 and kind != "first":
                                normalise(count(ph, 2, 0), fills_before(att, ph, names.index(("R1",)) + 1))
                            if s == steps - 1:
                                normalise(count(ph, 2, 1), fills_before(att, ph, names.index(("R0",)) + 1))
                            hf, h, q = s // half, s % nh, s // nh % 2
                            dve.wait_ge(tr_ready, count(ph, 2 * steps, 2 * s + 2))
                            if s % half == 0 and kind != "first":
                                dve.wait_ge(pv_ready, count(ph, 2, hf - 1))
                            nc.vector.tensor_copy(probT[:, hf, h, 4:8, q * P:(q + 1) * P],
                                                  TR[1][:, :].rearrange("p (k q) -> p k q", q=P)).then_inc(evac_dve, 1)

                    for n, f in enumerate(att.projections):
                        if f[0] in dve_takes:
                            take(f, n + 1, 0)
                    maxes(("first", None, 0), 0, 0, 0)
                    phases(phase, dve)
                    reciprocals(("last", None, 2 * G), 1, 2 * G * steps)
                    take(("O0",), tail_fills + 2, 1)
                    normalise(4 * G, tail_fills + 1)
                    take(("O1",), tail_fills + 3, 1)

                @block.gpsimd
                def _(pool):
                    def spread(n):
                        pool.wait_ge(recip_ready, n)
                        pool.sem_inc(spare, 1)
                        nc.gpsimd.tensor_copy(rexp[:], recip[:].unsqueeze(3).to_broadcast([P, 2, nh, rows])
                                              ).then_inc(rsum_ready, 1)

                    def lows(b, n):
                        for i in range(1 + SK // N):
                            if i == 0:
                                pool.wait_ge(q_high, n(1, 1))
                            else:
                                pool.wait_ge(k_high, n(2, i))
                            cut = slice((i - 1) * N, i * N)
                            for h, r in enumerate([slice(0, P)] if att.twice and i else own_rows):
                                if i == 0:
                                    dst, high = (Q[r, b, h, :], q_off[r, :]) if att.twice else (q_low[r, :], Q[r, b, h, :])
                                    last = nc.gpsimd.tensor_tensor(dst, q_raw[r, :], high, ALU.subtract)
                                else:
                                    last = nc.gpsimd.tensor_tensor(K[r, b, h, 1, cut], k_raw[r, cut],
                                                                   K[r, b, h, 0, cut], ALU.subtract)
                                if att.twice and i == 0 and h + 1 < nh:
                                    last.then_inc(low_chain, 1)
                                    pool.wait_ge(low_chain, n(3, h + 1))
                                elif not att.twice and h == 0:
                                    last.then_inc(low_chain, 1)
                                    pool.wait_ge(low_chain, n(3, i + 1))
                            last.then_inc(qk_split, 1)
                            pool.wait_ge(qk_split, n(3, i + 1))

                    def phase(ph, b):
                        if ph[0] != "first":
                            spread(count(ph, 2, 0))
                        if att.packed and ph[0] != "last":
                            lows(1 - b, lambda per, off: count(ph, per, per + off))
                        spread(count(ph, 2, 1))

                    if att.twice:
                        nc.gpsimd.iota(low_row_i[:], pattern=[[1, 1]], base=0, channel_multiplier=1).then_inc(low_row_made, 1)
                    if att.packed:
                        lows(0, lambda per, off: off)
                    phases(phase, pool)
                    spread(4 * G)

        def route(name, mode, eps=0.0, bias=False, b2=None):
            choices = 2 if mode == "top2" else 1
            with ExitStack() as own:
                wg = sb(name + "_wg_sb", [P, KT, E], F32, own)
                gb = sb(name + "_gb", [P, E], F32, own)
                lg = sb(name + "_lg", [P, TT, E], F32, own)
                top = sb(name + "_top", [P, TT, 8], F32, own)
                place = sb(name + "_place", [P, TT, 8], U32, own)
                placef = sb(name + "_placef", [P, TT, 8], F32, own)
                ex = sb(name + "_ex", [P, TT, E], F32, own)
                total = sb(name + "_total", [P, TT], F32, own)
                diff = sb(name + "_diff", [P, TT], F32, own)
                second = sb(name + "_second", [P, TT], F32, own)
                w0, w1 = weights[:, 0, :], weights[:, 1, :]
                hot = sb(name + "_hot", [P, choices, TT, E], F32, own)
                both = sb(name + "_both", [P, TT, E], F32, own)
                tile_sum = sb(name + "_tile_sum", [P, TT, E], F32, own)
                ahead = sb(name + "_ahead", [P, TT, E], F32, own)
                place_of = sb(name + "_place_of", [P, TT, E], F32, own)
                expert_sum = sb(name + "_expert_sum", [P, E], F32, own)
                more = sb(name + "_more", [P, E, E - 1], F32, own)
                bounds = sb(name + "_bounds", [P, E - 1], F32, own)
                tiles_of = sb(name + "_tiles_of", [P, E], F32, own)
                first_tile = sb(name + "_first_tile", [P, E + 1], F32, own)
                first_slot = sb(name + "_first_slot", [P, E], F32, own)
                slot = sb(name + "_slot", [P, TT], F32, own)
                if mode == "argmax":
                    start_of = sb(name + "_start_of", [P, E + 1], F32, own)
                    beyond = sb(name + "_beyond", [P, TT, E + 1], F32, own)
                    comb = sb(name + "_comb", [P, TT, E], F32, own)
                    combT = sb(name + "_combT", [E, T], F32, own)
                    b2_sb = sb(name + "_b2", [E, D], F32, own)
                loaded = shared("route_loaded")
                logits_ready = shared("route_logits")
                chain = shared("route_chain")
                shifted = shared("route_shifted")
                exps_ready = shared("route_exps")
                hot_ready = shared("route_hot_ready")
                counted = shared("route_counted")
                comb_ready = shared("route_comb")
                combT_ready = shared("route_combT_ready")
                combT_taken = shared("route_combT_taken")
                row_ready = shared("route_row_ready")
                row_taken = shared("route_row_taken")
                with nc.Block() as block:
                    @block.sync
                    def _(sp):
                        sp.dma_start(wg[:], a[name + "_wg"]).then_inc(loaded, 16)
                        if bias:
                            sp.dma_start(gb[:], a[name + "_gb"].partition_broadcast(P)).then_inc(loaded, 16)
                        if b2:
                            sp.dma_start(b2_sb[:], a[b2]).then_inc(loaded, 16)

                    @block.vector
                    def _(dve):
                        done = [0]

                        def link(ins):
                            done[0] += 1
                            ins.then_inc(chain, 1)
                            dve.wait_ge(chain, done[0])

                        def per_token(v):
                            return v.unsqueeze(2).to_broadcast([P, TT, E])

                        def per_expert(v):
                            return v.unsqueeze(1).to_broadcast([P, TT, E])

                        dve.wait_ge(logits_ready, 1)
                        src = bank[0][:, 0:TT * E].rearrange("p (j e) -> p j e", e=E)
                        if bias:
                            link(nc.vector.tensor_tensor(lg[:], src, per_expert(gb[:]), ALU.add))
                        else:
                            link(nc.vector.tensor_copy(lg[:], src))
                        for j in range(TT):
                            last = nc.vector.max(top[:, j, :], lg[:, j, :])
                        link(last)
                        for j in range(TT):
                            last = nc.vector.max_index(place[:, j, :], top[:, j, :], lg[:, j, :])
                        link(last)
                        nc.vector.tensor_tensor(lg[:], lg[:], per_token(top[:, :, 0]), ALU.subtract).then_inc(shifted, 1)
                        nc.vector.tensor_tensor(diff[:], top[:, :, 1], top[:, :, 0], ALU.subtract).then_inc(shifted, 1)
                        link(nc.vector.tensor_copy(placef[:], place[:]))
                        for c in range(choices):
                            link(nc.vector.tensor_tensor(hot[:, c], per_expert(iota[:]), per_token(placef[:, :, c]),
                                                         ALU.is_equal))
                        if choices == 2:
                            nc.vector.tensor_tensor(both[:], hot[:, 0], hot[:, 1], ALU.add).then_inc(hot_ready, 1)
                        else:
                            nc.vector.tensor_copy(both[:], hot[:, 0]).then_inc(hot_ready, 1)
                        dve.wait_ge(exps_ready, 2)
                        link(nc.vector.tensor_reduce(total[:], ex[:], AX_X, ALU.add))
                        if mode == "top2":
                            link(nc.vector.scalar_tensor_tensor(out=w1, in0=total[:], scalar=eps, in1=second[:],
                                                                op0=ALU.mult, op1=ALU.add))
                            link(nc.vector.tensor_scalar(w1, w1, 1.0, None, ALU.add))
                            link(nc.vector.reciprocal(w0, w1))
                            link(nc.vector.tensor_tensor(w1, w0, second[:], ALU.mult))
                            nc.vector.tensor_tensor(weights[:, 2, :], w0, w1, ALU.add)
                        else:
                            link(nc.vector.reciprocal(w0, total[:]))
                            for j in range(TT):
                                nc.vector.tensor_scalar(xn[:, j, :], xn[:, j, :], w0[:, j:j + 1], None, ALU.mult)
                        link(nc.vector.tensor_scalar(bounds[:], iota[:, 1:E], float(P), None, ALU.mult))
                        dve.wait_ge(counted, 1)
                        link(nc.vector.tensor_copy(tile_sum[:], bank[2][:, 0:TT * E].rearrange("p (j e) -> p j e", e=E)))
                        link(nc.vector.tensor_copy(ahead[:], bank[1][:, 0:TT * E].rearrange("p (j e) -> p j e", e=E)))
                        link(nc.vector.tensor_reduce(expert_sum[:], tile_sum[:].rearrange("p j e -> p e j"),
                                                     AX_X, ALU.add))
                        link(nc.vector.tensor_tensor(more[:], expert_sum[:].unsqueeze(2).to_broadcast([P, E, E - 1]),
                                                     bounds[:].unsqueeze(1).to_broadcast([P, E, E - 1]), ALU.is_gt))
                        link(nc.vector.tensor_reduce(tiles_of[:], more[:], AX_X, ALU.add))
                        link(nc.vector.tensor_scalar(tiles_of[:], tiles_of[:], 1.0, None, ALU.add))
                        link(nc.vector.memset(first_tile[:, 0:1], 0.0))
                        for e in range(E):
                            link(nc.vector.tensor_tensor(first_tile[:, e + 1:e + 2], first_tile[:, e:e + 1],
                                                         tiles_of[:, e:e + 1], ALU.add))
                        link(nc.vector.tensor_copy(tile_start[:], first_tile[:]))
                        link(nc.vector.tensor_scalar(first_slot[:], first_tile[:, 0:E], float(P), None, ALU.mult))
                        for j in range(2, TT):
                            link(nc.vector.tensor_tensor(tile_sum[:, j - 1, :], tile_sum[:, j - 1, :],
                                                         tile_sum[:, j - 2, :], ALU.add))
                        link(nc.vector.tensor_tensor(ahead[:, 1:, :], ahead[:, 1:, :], tile_sum[:, 0:TT - 1, :],
                                                     ALU.add))
                        link(nc.vector.tensor_tensor(ahead[:], ahead[:], per_expert(first_slot[:]), ALU.add))
                        for c in range(choices):
                            link(nc.vector.tensor_tensor(place_of[:], ahead[:], hot[:, c], ALU.mult))
                            link(nc.vector.tensor_reduce(slot[:], place_of[:], AX_X, ALU.add))
                            link(nc.vector.tensor_copy(put[:, c, :], slot[:]))
                            if mode == "top2":
                                link(nc.vector.tensor_copy(take[:, c, :], slot[:]))
                        if mode == "argmax":
                            link(nc.vector.memset(start_of[:, 0:1], 0.0))
                            for e in range(E):
                                link(nc.vector.tensor_tensor(start_of[:, e + 1:e + 2], start_of[:, e:e + 1],
                                                             expert_sum[:, e:e + 1], ALU.add))
                            link(nc.vector.tensor_tensor(beyond[:], token_no[:].unsqueeze(2).to_broadcast([P, TT, E + 1]),
                                                         start_of[:].unsqueeze(1).to_broadcast([P, TT, E + 1]),
                                                         ALU.is_ge))
                            nc.vector.tensor_tensor(comb[:], beyond[:, :, 0:E], beyond[:, :, 1:],
                                                    ALU.subtract).then_inc(comb_ready, 1)
                            link(nc.vector.tensor_tensor(first_slot[:], first_slot[:], start_of[:, 0:E], ALU.subtract))
                            dve.wait_ge(comb_ready, 1)
                            link(nc.vector.tensor_tensor(place_of[:], comb[:], per_expert(first_slot[:]), ALU.mult))
                            link(nc.vector.tensor_reduce(slot[:], place_of[:], AX_X, ALU.add))
                            link(nc.vector.tensor_tensor(slot[:], slot[:], token_no[:], ALU.add))
                            link(nc.vector.tensor_copy(take[:, 0, :], slot[:]))
                            for h in range(2):
                                dve.wait_ge(combT_ready, h + 1)
                                nc.vector.tensor_copy(combT[:, h * N:(h + 1) * N], bank[1 + h][0:E, :]
                                                      ).then_inc(combT_taken, 1)
                            for n in range(TT):
                                dve.wait_ge(row_ready, n + 1)
                                nc.vector.tensor_tensor(x[:, n, :], x[:, n, :], bank[5 + n % 3][:, 0:D],
                                                        ALU.add).then_inc(row_taken, 1)

                    @block.scalar
                    def _(act):
                        act.wait_ge(shifted, 2)
                        nc.scalar.activation(ex[:], lg[:], ACT.Exp).then_inc(exps_ready, 1)
                        nc.scalar.activation(second[:], diff[:], ACT.Exp).then_inc(exps_ready, 1)

                    @block.tensor
                    def _(pe):
                        pe.wait_ge(loaded, 16 * (1 + bias + bool(b2)))
                        for j in range(TT):
                            for k in range(KT):
                                last = nc.tensor.matmul(bank[0][:, j * E:(j + 1) * E], xnT[:, k, j * P:(j + 1) * P],
                                                        wg[:, k, :], start=(k == 0), stop=(k == KT - 1))
                        last.then_inc(logits_ready, 1)
                        pe.wait_ge(hot_ready, 1)
                        hots = both[:].rearrange("p j e -> p (j e)")
                        nc.tensor.matmul(bank[1][:, 0:TT * E], below[:], hots, start=True, stop=True)
                        nc.tensor.matmul(bank[2][:, 0:TT * E], ones[:], hots, start=True, stop=True).then_inc(counted, 1)
                        if mode == "argmax":
                            pe.wait_ge(comb_ready, 1)
                            for j in range(TT):
                                last = nc.tensor.transpose(bank[1 + j // 4][0:E, (j % 4) * P:(j % 4 + 1) * P],
                                                           comb[:, j, :], ident[:])
                                if j % 4 == 3:
                                    last.then_inc(combT_ready, 1)
                            pe.wait_ge(combT_taken, 2)
                            for n in range(TT):
                                if n >= 3:
                                    pe.wait_ge(row_taken, n - 2)
                                nc.tensor.matmul(bank[5 + n % 3][:, 0:D], combT[:, n * P:(n + 1) * P], b2_sb[:],
                                                 start=True, stop=True).then_inc(row_ready, 1)

        def feed_forward(name, experts, tiles, hid, gated, func, bias=False, ternary=None, beside=None):
            mats = 2 if gated else 1
            NB = 2 if gated else 4
            own = ExitStack()
            with own:
                if ternary:
                    up, down = ternary
                else:
                    up = sb(name + "_up_sb", [P, tiles, KT, mats, hid], F32, own)
                    down = sb(name + "_down_sb", [hid, tiles, D], F32, own)
                b1 = sb(name + "_b1_sb", [hid, tiles], F32, own)
                gate_act = sb(name + "_gate_act", [hid, 2, N], F32, own)
                hidden = sb(name + "_hidden", [hid, 2, tiles, N], F32, own)
                up_loaded = [shared(f"ff_up_loaded{i}") for i in range(2)]
                down_loaded = shared("ff_down_loaded")
                b1_loaded = shared("ff_b1_loaded")
                up_ready = shared("ff_up_ready")
                gate_ready = shared("ff_gate_ready")
                hidden_ready = shared("ff_hidden_ready")
                down_ready = shared("ff_down_ready")
                down_taken = shared("ff_down_taken")
                block = own.enter_context(nc.Block())
                per = 2 * tiles
                half = tiles // 2

                def over_experts(run, eng):
                    run(0, 0)
                    if experts > 1:
                        with eng.Fori(1, experts) as e:
                            run(e, 1)

                @block.sync
                def _(sp):
                    def load(e, i):
                        s = slice(i * half, (i + 1) * half)
                        sp.dma_start(up[:, s], a[name + "_up"][e][:, s]).then_inc(up_loaded[i], 16)

                    def run(e, later):
                        if not ternary:
                            for i in range(2):
                                if later:
                                    sp.wait_ge(up_ready, e * per - (1 - i) * half)
                                load(e, i)
                        if bias:
                            if later:
                                sp.wait_ge(hidden_ready, e * per)
                            sp.dma_start(b1[:], a[name + "_b1"][e]).then_inc(b1_loaded, 16)
                        if not ternary:
                            if later:
                                sp.wait_ge(down_ready, e * TT)
                            sp.dma_start(down[:], a[name + "_down"][e]).then_inc(down_loaded, 16)

                    over_experts(run, sp)
                    if beside:
                        beside[1](sp)

                @block.gpsimd
                def _(pool):
                    if beside:
                        beside[0](pool)

                @block.tensor
                def _(pe):
                    def run(e, later):
                        for h in range(2):
                            for t in range(tiles):
                                n = h * tiles + t
                                if h == 0 and t % half == 0 and not ternary:
                                    pe.wait_ge(up_loaded[t // half], e * 16 + 16)
                                if later or n >= NB:
                                    pe.wait_ge(hidden_ready, e * per + (n - NB + 1))
                                for m in range(mats):
                                    for k in range(KT):
                                        last = nc.tensor.matmul(bank[(n % NB) * mats + m][0:hid, :],
                                                                up[:, t, k, m, :], xnT[:, k, h * N:(h + 1) * N],
                                                                start=(k == 0), stop=(k == KT - 1))
                                last.then_inc(up_ready, 1)
                        if not ternary:
                            pe.wait_ge(down_loaded, e * 16 + 16)
                        for h in range(2):
                            pe.wait_ge(hidden_ready, e * per + (h + 1) * tiles)
                            for j in range(4):
                                n = h * 4 + j
                                if later or n >= 4:
                                    pe.wait_ge(down_taken, e * TT + (n - 3))
                                for t in range(tiles):
                                    last = nc.tensor.matmul(bank[4 + j][:, 0:D], hidden[:, h, t, j * P:(j + 1) * P],
                                                            down[:, t, :], start=(t == 0), stop=(t == tiles - 1))
                                last.then_inc(down_ready, 1)

                    over_experts(run, pe)

                @block.scalar
                def _(act):
                    def run(e, later):
                        for h in range(2):
                            for t in range(tiles):
                                n = h * tiles + t
                                if bias and n == 0:
                                    act.wait_ge(b1_loaded, e * 16 + 16)
                                act.wait_ge(up_ready, e * per + (n + 1))
                                src = bank[(n % NB) * mats][0:hid, :]
                                if gated:
                                    if later or n >= 2:
                                        act.wait_ge(hidden_ready, e * per + (n - 1))
                                    nc.scalar.activation(gate_act[:, n % 2, :], src, func).then_inc(gate_ready, 1)
                                else:
                                    if later and t == 0:
                                        act.wait_ge(down_ready, e * TT + (h * 4 - 4))
                                    nc.scalar.activation(hidden[:, h, t, :], src, func,
                                                         bias=b1[:, t:t + 1]).then_inc(hidden_ready, 1)

                    over_experts(run, act)

                @block.vector
                def _(dve):
                    def run(e, later):
                        if gated:
                            for h in range(2):
                                for t in range(tiles):
                                    n = h * tiles + t
                                    dve.wait_ge(gate_ready, e * per + (n + 1))
                                    if later and t == 0:
                                        dve.wait_ge(down_ready, e * TT + (h * 4 - 4))
                                    nc.vector.tensor_tensor(hidden[:, h, t, :], bank[(n % NB) * mats + 1][0:hid, :],
                                                            gate_act[:, n % 2, :], ALU.mult).then_inc(hidden_ready, 1)
                        for n in range(TT):
                            dve.wait_ge(down_ready, e * TT + (n + 1))
                            src = bank[4 + n % 4][:, 0:D]
                            nc.vector.tensor_tensor(x[:, n, :], x[:, n, :], src, ALU.add).then_inc(down_taken, 1)

                    over_experts(run, dve)

        scattered = sem("ex_scattered")
        gathered = [sem(f"ex_gathered{c}") for c in range(2)]
        moved = {"scattered": 0, "gathered": [0, 0]}

        def routed_experts(name, kind, tiles, hid, choices, own_down=True, bo=False, shared_expert=None):
            mats = 1 if kind == "relu" else 2
            half = tiles // 2
            NT = choices * TT + E
            parts = NT // TT
            biased = kind != "silu"
            loads = 1 + own_down + biased
            outer = ExitStack()
            with outer:
                up = sb(name + "_up_sb", [P, 2, tiles, KT, mats, hid], F32, outer)
                down = sb(name + "_down_sb", [hid, 2 if own_down else 1, tiles, D], F32, outer)
                b1 = sb(name + "_b1_sb", [hid, 2, tiles, mats], F32, outer) if biased else None
                sorted_x = sb(name + "_sorted_x", [P, NT, D], F32, outer)
                y = sorted_x
                w_loaded = [shared(f"ex_w_loaded{c}") for c in range(2)]
                fixed_loaded = shared("ex_fixed_loaded")
                scattered_before, gathered_before = moved["scattered"], moved["gathered"][:]
                moved["scattered"] += 16 * choices * TT
                for c in range(choices):
                    moved["gathered"][c] += 16 * TT
                sorted_loaded = [shared(f"ex_sorted_loaded{i}") for i in range(parts)]

                def load_weights(sp, e, c):
                    sp.dma_start(up[:, c], a[name + "_up"][e]).then_inc(w_loaded[c], 16)
                    if own_down:
                        sp.dma_start(down[:, c], a[name + "_down"][e]).then_inc(w_loaded[c], 16)
                    if biased:
                        sp.dma_start(b1[:, c], a[name + "_b1"][e]).then_inc(w_loaded[c], 16)

                def scatter(pool):
                    pool.wait_ge(slots_cleared, 32)
                    for c in range(choices):
                        for j in range(TT):
                            nc.gpsimd.indirect_dma_start(by_slot, bass.IndirectOffsetOnAxis(put[:, c, j:j + 1], 0),
                                                         xn[:, j, :], None).then_inc(scattered, 16)

                def load_sorted(sp):
                    for e in range(2):
                        load_weights(sp, e, e)
                    if bo:
                        sp.dma_start(bo_sb[:], a[name + "_bo"].partition_broadcast(P)).then_inc(fixed_loaded, 16)
                    if not own_down:
                        sp.dma_start(down[:, 0], a[name + "_wo"]).then_inc(fixed_loaded, 16)
                    sp.wait_ge(scattered, scattered_before + 16 * choices * TT)
                    for i in range(parts):
                        sp.dma_start(sorted_x[:, i * TT:(i + 1) * TT, :],
                                     by_slot[i * TT * P:(i + 1) * TT * P, :].rearrange("(j p) d -> p j d", p=P)
                                     ).then_inc(sorted_loaded[i], 16)

                bo_sb = sb(name + "_bo_sb", [P, D], F32, outer) if bo else None
                if shared_expert:
                    shared_expert(scatter, load_sorted)
                sortedT = sb(name + "_sortedT", [P, KT, NT * P], F32, outer)
                gathered_y = sb(name + "_gathered_y", [P, choices, TT, D], F32, outer)
                gate = sb(name + "_gate", [hid, 2, half, P], F32, outer) if mats == 2 else None
                hidden = sb(name + "_hidden", [hid, tiles, P], F32, outer)
                tr_ready = shared("ex_tr_ready")
                evac_act = shared("ex_evac_act")
                evac_dve = shared("ex_evac_dve")
                up_ready = shared("ex_up_ready")
                gate_ready = shared("ex_gate_ready")
                hidden_ready = shared("ex_hidden_ready")
                down_ready = shared("ex_down_ready")
                y_taken = shared("ex_y_taken")
                y_stored = shared("ex_y_stored")
                added = shared("ex_added")
                block = outer.enter_context(nc.Block())

                def tiles_of_expert(eng, e, c, body):
                    start = eng.value_load(tile_start[0:1, bass.ds(e, 1)], min_val=0, max_val=NT)
                    end = eng.value_load(tile_start[0:1, bass.ds(e + 1, 1)], min_val=0, max_val=NT)
                    with eng.Fori(start, end) as g:
                        body(g, c)

                def up_banks(hf):
                    return [bank[2 * hf + m][0:hid, 0:half * P].rearrange("p (t q) -> p t q", q=P) for m in range(2)]

                @block.sync
                def _(sp):
                    def store(g, c):
                        sp.wait_ge(y_taken, g + 2)
                        sp.dma_start(result_by_slot[bass.ds(g * P, P), :],
                                     y[:, bass.ds(g, 1), :].rearrange("p a d -> p (a d)")).then_inc(y_stored, 16)

                    if not shared_expert:
                        load_sorted(sp)
                    with sp.Fori(0, E // 2 - 1) as i:
                        for c in range(2):
                            tiles_of_expert(sp, 2 * i + c, c, store)
                            load_weights(sp, 2 * i + (c + 2), c)
                    for c in range(2):
                        tiles_of_expert(sp, E - 2 + c, c, store)

                @block.gpsimd
                def _(pool):
                    if not shared_expert:
                        scatter(pool)
                    end = pool.value_load(tile_start[0:1, E:E + 1], min_val=E, max_val=NT)
                    pool.wait_ge(y_stored, end * 16)
                    pool.sem_inc(spare, 1)
                    for c in range(choices):
                        for j in range(TT):
                            nc.gpsimd.indirect_dma_start(gathered_y[:, c, j, :], None, result_by_slot,
                                                         bass.IndirectOffsetOnAxis(take[:, c, j:j + 1], 0)
                                                         ).then_inc(gathered[c], 16)

                @block.tensor
                def _(pe):
                    for n in range(NT // 4):
                        if n % 2 == 0:
                            pe.wait_ge(sorted_loaded[n // 2], 16)
                        if n >= 2:
                            pe.wait_ge(evac_act, n - 1)
                            pe.wait_ge(evac_dve, n - 1)
                        for k in range(KT):
                            for i in range(4):
                                last = nc.tensor.transpose(bank[2 * (n % 2) + k][:, i * P:(i + 1) * P],
                                                           sorted_x[:, 4 * n + i, k * P:(k + 1) * P], ident[:])
                        last.then_inc(tr_ready, 1)
                    pe.wait_ge(evac_act, NT // 4)
                    pe.wait_ge(evac_dve, NT // 4)
                    if not own_down:
                        pe.wait_ge(fixed_loaded, 16 * (bo + 1))

                    def tile(g, c):
                        for hf in range(2):
                            dst = up_banks(hf)
                            for t in range(half):
                                for m in range(mats):
                                    for k in range(KT):
                                        last = nc.tensor.matmul(dst[m][:, t, :], up[:, c, hf * half + t, k, m, :],
                                                                sortedT[:, k, bass.ds(g * P, P)],
                                                                start=(k == 0), stop=(k == KT - 1))
                            last.then_inc(up_ready, 1)
                        pe.wait_ge(y_taken, g + 1)
                        for hf in range(2):
                            pe.wait_ge(hidden_ready, 2 * g + (hf + 1))
                            for t in range(hf * half, hf * half + half):
                                last = nc.tensor.matmul(bank[4][:, 0:D], hidden[:, t, :],
                                                        down[:, c if own_down else 0, t, :],
                                                        start=(t == 0), stop=(t == tiles - 1))
                        last.then_inc(down_ready, 1)

                    with pe.Fori(0, E // 2) as i:
                        for c in range(2):
                            pe.wait_ge(w_loaded[c], i * (16 * loads) + 16 * loads)
                            pe.sem_inc(spare, 1)
                            tiles_of_expert(pe, 2 * i + c, c, tile)

                @block.scalar
                def _(act):
                    for n in range(NT // 4):
                        act.wait_ge(tr_ready, n + 1)
                        nc.scalar.copy(sortedT[:, 0, n * N:(n + 1) * N], bank[2 * (n % 2)][:, :]).then_inc(evac_act, 1)

                    def tile(g, c):
                        for hf in range(2):
                            act.wait_ge(up_ready, 2 * g + (hf + 1))
                            first, second = up_banks(hf)
                            ts = range(hf * half, hf * half + half)
                            if kind == "silu":
                                nc.scalar.activation(gate[:, hf], first, ACT.Silu).then_inc(gate_ready, 1)
                            for t in ts if kind == "glu" else ():
                                last = nc.scalar.activation(gate[:, hf, t % half, :], second[:, t % half, :],
                                                            ACT.Sigmoid, bias=b1[:, c, t, 1:2])
                            for t in ts if kind == "relu" else ():
                                last = nc.scalar.activation(hidden[:, t, :], first[:, t % half, :], ACT.Relu,
                                                            bias=b1[:, c, t, 0:1])
                            if kind != "silu":
                                last.then_inc(hidden_ready if kind == "relu" else gate_ready, 1)

                    with act.Fori(0, E // 2) as i:
                        for c in range(2):
                            if biased:
                                act.wait_ge(w_loaded[c], i * (16 * loads) + 16 * loads)
                                act.sem_inc(spare, 1)
                            tiles_of_expert(act, 2 * i + c, c, tile)

                @block.vector
                def _(dve):
                    for n in range(NT // 4):
                        dve.wait_ge(tr_ready, n + 1)
                        nc.vector.tensor_copy(sortedT[:, 1, n * N:(n + 1) * N],
                                              bank[2 * (n % 2) + 1][:, :]).then_inc(evac_dve, 1)
                    dve.sem_inc(y_taken, 1)

                    def tile(g, c):
                        for hf in range(2) if mats == 2 else ():
                            dve.wait_ge(gate_ready, 2 * g + (hf + 1))
                            first, second = up_banks(hf)
                            if kind == "silu":
                                nc.vector.tensor_tensor(hidden[:, hf * half:(hf + 1) * half, :], second, gate[:, hf],
                                                        ALU.mult).then_inc(hidden_ready, 1)
                                continue
                            for t in range(half):
                                last = nc.vector.scalar_tensor_tensor(out=hidden[:, hf * half + t, :],
                                                                      in0=first[:, t, :],
                                                                      scalar=b1[:, c, hf * half + t, 0:1],
                                                                      in1=gate[:, hf, t, :], op0=ALU.add, op1=ALU.mult)
                            last.then_inc(hidden_ready, 1)
                        dve.wait_ge(down_ready, g + 1)
                        nc.vector.tensor_copy(y[:, bass.ds(g, 1), :].rearrange("p a d -> p (a d)"),
                                              bank[4][:, 0:D]).then_inc(y_taken, 1)

                    with dve.Fori(0, E // 2) as i:
                        for c in range(2):
                            if biased:
                                dve.wait_ge(w_loaded[c], i * (16 * loads) + 16 * loads)
                                dve.sem_inc(spare, 1)
                            tiles_of_expert(dve, 2 * i + c, c, tile)
                    if bo:
                        dve.wait_ge(fixed_loaded, 32)
                        for j in range(TT):
                            nc.vector.scalar_tensor_tensor(out=x[:, j, :], in0=bo_sb[:], scalar=weights[:, 2, j:j + 1],
                                                           in1=x[:, j, :], op0=ALU.mult, op1=ALU.add).then_inc(added, 1)
                    n_added = TT if bo else 0
                    for c in range(choices):
                        dve.wait_ge(gathered[c], gathered_before[c] + 16 * TT)
                        if n_added:
                            dve.wait_ge(added, n_added)
                        for j in range(TT):
                            if choices == 2:
                                nc.vector.scalar_tensor_tensor(out=x[:, j, :], in0=gathered_y[:, c, j, :],
                                                               scalar=weights[:, c, j:j + 1], in1=x[:, j, :],
                                                               op0=ALU.mult, op1=ALU.add).then_inc(added, 1)
                            else:
                                nc.vector.tensor_tensor(x[:, j, :], x[:, j, :], gathered_y[:, c, j, :],
                                                        ALU.add).then_inc(added, 1)
                        n_added += TT

        def make_ternary(up, down):
            with ExitStack() as own:
                raw = [sb("tern_raw_up", [P, 2048], F32, own), sb("tern_raw_down", [P, 2048], F32, own)]
                below = sb("tern_below", [P, 2048], F32, own)
                mags = sb("tern_mags", [P, 2], F32, own)
                bound = sb("tern_bound", [P, 2, 2], F32, own)
                loaded = sem("tern_loaded")
                chain = sem("tern_chain")
                mags_ready = sem("tern_mags_ready")
                mean_ready = sem("tern_mean_ready")
                with nc.Block() as block:
                    @block.sync
                    def _(sp):
                        sp.dma_start(raw[0][:], a["L1f_up"]).then_inc(loaded, 16)
                        sp.dma_start(raw[1][:], a["L1f_down"]).then_inc(loaded, 16)

                    @block.tensor
                    def _(pe):
                        pe.wait_ge(mags_ready, 1)
                        nc.tensor.matmul(bank[0][:, 0:2], ones[:], mags[:], start=True, stop=True).then_inc(mean_ready, 1)

                    @block.vector
                    def _(dve):
                        done = [0]

                        def link(ins):
                            done[0] += 1
                            ins.then_inc(chain, 1)
                            dve.wait_ge(chain, done[0])

                        dve.wait_ge(loaded, 32)
                        for m in range(2):
                            last = nc.vector.tensor_reduce(mags[:, m:m + 1], raw[m][:], AX_X, ALU.add,
                                                           apply_absolute_value=True)
                        last.then_inc(mags_ready, 1)
                        dve.wait_ge(mean_ready, 1)
                        link(nc.vector.tensor_scalar(bound[:, :, 0], bank[0][:, 0:2], 1.0 / (P * 2048), 1e-8,
                                                     ALU.mult, ALU.max))
                        link(nc.vector.tensor_scalar(bound[:, :, 1], bound[:, :, 0], -0.5, None, ALU.mult))
                        link(nc.vector.tensor_scalar(bound[:, :, 0], bound[:, :, 0], 0.5, None, ALU.mult))
                        for m, dst in enumerate((up, down)):
                            link(nc.vector.tensor_scalar(below[:], raw[m][:], bound[:, m, 1:2], None, ALU.is_lt))
                            link(nc.vector.scalar_tensor_tensor(out=dst, in0=raw[m][:], scalar=bound[:, m, 0:1],
                                                                in1=below[:], op0=ALU.is_gt, op1=ALU.subtract))

        PAIRS = dict(nh=2, nc=1, groups=8, fills=PAIR, packed=True)
        layer_norm("n0", bo="L0_bo")
        attention(Attention("L0", scale=1.0, bias=True, mask=None, **PAIRS))
        clear_shared()
        layer_norm("n1")
        route("L0f", "top2", eps=1e-9)
        routed_experts("L0f", "glu", tiles=4, hid=P, choices=2, own_down=False, bo=True)
        clear_shared()
        layer_norm("n2", bo="L1_bo")
        attention(Attention("L1", scale=1 / 16, bias=True, mask="select", nh=1, nc=2, groups=1, fills=SINGLE))
        clear_shared()
        layer_norm("n3", bo="L1f_b2")
        with ExitStack() as own:
            up = sb("L1f_up_sb", [P, 8, KT, 1, P], F32, own)
            down = sb("L1f_down_sb", [P, 8, D], F32, own)
            make_ternary(up[:].rearrange("p t k m h -> p (t k m h)"), down[:].rearrange("p t d -> p (t d)"))
            feed_forward("L1f", 1, 8, P, False, ACT.Gelu, bias=True, ternary=(up, down))
            clear_shared()
        layer_norm("n4", bo="L2_bo")
        attention(Attention("L2", scale=1 / 4, bias=True, mask="add", nh=4, nc=1, groups=4, fills=QUAD,
                            packed=True, twice=True))
        clear_shared()
        layer_norm("n5")
        route("L2f", "argmax", bias=True, b2="L2f_b2")
        routed_experts("L2f", "relu", tiles=2, hid=P, choices=1)
        clear_shared()
        layer_norm("n6")
        attention(Attention("L3", scale=1 / 8, bias=False, mask=None, **PAIRS))
        clear_shared()
        layer_norm("n7")
        route("L3f", "top2", eps=1e-8)
        routed_experts("L3f", "silu", tiles=8, hid=118, choices=2,
                       shared_expert=lambda *beside: feed_forward("L3s", 1, 8, 118, True, ACT.Silu, beside=beside))
        clear_shared()

        with nc.Block() as block:
            @block.sync
            def _(sp):
                sp.dma_start(out.rearrange("(j p) d -> p j d", p=P), x[:]).then_inc(x_stored, 16)
                sp.wait_ge(x_stored, 16)





def kernel(**inputs):
    import numpy as np
    import concourse.bacc as bacc
    from concourse.bass_utils import run_bass_kernel_spmd as run

    i = {k: np.asarray(v) for k, v in inputs.items()}

    def grouped(w, groups, heads, rows, head_rows, twice=False):
        per = heads // groups
        w = w.reshape(w.shape[0], groups, per, head_rows)
        if twice:
            w = np.concatenate([w, w], axis=3)
        elif rows != head_rows:
            padded = np.zeros(w.shape[:3] + (rows,), w.dtype)
            padded[..., :head_rows] = w
            w = padded
        return w.transpose(1, 0, 2, 3).reshape(groups, w.shape[0], per * rows)

    def attention_arrays(name, wq, wk, wv, wo, biases, groups, heads, rows):
        dh = wq.shape[1] // heads
        twice = rows == 2 * dh
        g = [grouped(wq, groups, heads, rows, dh, twice), grouped(wk, groups, heads, rows, dh, twice),
             grouped(wv, groups, heads, rows, dh)]
        cols = g[0].shape[2]
        w = np.concatenate(g, axis=2).reshape(groups, KT, P, 3 * cols).transpose(0, 2, 1, 3)
        o = grouped(wo.T, groups, heads, rows, dh).transpose(0, 2, 1).reshape(groups, cols // P, P, D)
        again = (lambda v: np.concatenate([v, v[:1]])) if groups == 8 else (lambda v: v)
        arrays[name + "_wqkv"] = again(w)
        arrays[name + "_wo"] = o.transpose(0, 2, 1, 3)
        if biases:
            q, k, v = (grouped(b[None], groups, heads, rows, dh, twice and n < 2)[:, 0] for n, b in enumerate(biases))
            qk = np.concatenate([q, k], axis=1).reshape(groups, 2 * cols // P, P)
            arrays[name + "_bqk"] = again(qk.transpose(0, 2, 1))
            arrays[name + "_bv"] = again(v)

    arrays = {"x": i["x"].reshape(T, D), "ctxT": i["ctx_1024"].reshape(B * SK, D).T}
    attention_arrays("L0", i["L0_xattn_Wq"].T, i["L0_xattn_Wk"].T, i["L0_xattn_Wv"].T, i["L0_xattn_Wo"].T,
                     [i["L0_xattn_b" + c] for c in "qkv"], 8, 16, 64)
    attention_arrays("L1", i["L1_xattn_Wq"].T, i["L1_xattn_Wk"].T, i["L1_xattn_Wv"].T, i["L1_xattn_Wo"].T,
                     [i["L1_xattn_b" + c] for c in "qkv"], 1, 1, 256)
    attention_arrays("L2", i["L2_xattn_Wq"], i["L2_xattn_Wk"], i["L2_xattn_Wv"], i["L2_xattn_Wo"],
                     [i["L2_xattn_b" + c] for c in "qkv"], 4, 16, 32)
    attention_arrays("L3", i["L3_xattn_Wq"], i["L3_xattn_Wk"], i["L3_xattn_Wv"], i["L3_xattn_Wo"], None, 8, 16, 64)
    for n in range(3):
        arrays[f"L{n}_bo"] = i[f"L{n}_xattn_bo"]
    arrays["L1_mask"] = i["mask_BxSxS2_if1"]
    arrays["L2_mask"] = i["mask_Bx1xSxS2_bk1"][:, 0]

    def columns(w, tiles, rows):
        e = w.shape[0]
        full = np.zeros((e, tiles * rows, D), w.dtype)
        full[:, :w.shape[1]] = w
        return full.reshape(e, tiles, rows, KT, P).transpose(0, 4, 1, 3, 2)

    def rows_first(w, tiles, rows):
        e = w.shape[0]
        full = np.zeros((e, D, tiles * rows), w.dtype)
        full[:, :, :w.shape[2]] = w
        return full.reshape(e, D, tiles, rows).transpose(0, 3, 2, 1)

    def gates(w):
        return w.reshape(E, KT, P).transpose(2, 1, 0)

    w1 = i["L0_ffn_W1"]
    arrays["L0f_wg"] = gates(i["L0_ffn_Wg"])
    arrays["L0f_up"] = np.stack([columns(w1[:, :512], 4, P), columns(w1[:, 512:], 4, P)], axis=4)
    arrays["L0f_b1"] = i["L0_ffn_b1"].reshape(E, 2, 4, P).transpose(0, 3, 2, 1)
    arrays["L0f_wo"] = rows_first(i["L0_ffn_Wo"][None], 4, P)[0]
    arrays["L0f_bo"] = i["L0_ffn_bo"]
    arrays["L1f_up"] = columns(i["L1_ffn_W1"][None], 8, P)[0].reshape(P, 2048)
    arrays["L1f_down"] = rows_first(i["L1_ffn_W2"][None], 8, P)[0].reshape(P, 2048)
    arrays["L1f_b1"] = i["L1_ffn_b1"].reshape(1, 8, P).transpose(0, 2, 1)
    arrays["L1f_b2"] = i["L1_ffn_b2"]
    arrays["L2f_wg"] = gates(i["L2_ffn_Ws"])
    arrays["L2f_gb"] = i["L2_ffn_bs"]
    arrays["L2f_up"] = columns(i["L2_ffn_W1"].transpose(0, 2, 1), 2, P)[:, :, :, :, None]
    arrays["L2f_down"] = rows_first(i["L2_ffn_W2"].transpose(0, 2, 1), 2, P)
    arrays["L2f_b1"] = i["L2_ffn_b1"].reshape(E, 2, P, 1).transpose(0, 2, 1, 3)
    arrays["L2f_b2"] = i["L2_ffn_b2"]
    for name, gu, dn in (("L3s", i["L3_ffn_shared_gate_up"][None], i["L3_ffn_shared_down"][None]),
                         ("L3f", i["L3_ffn_experts_gate_up"], i["L3_ffn_experts_down"])):
        width = dn.shape[2]
        arrays[name + "_up"] = np.stack([columns(gu[:, :width], 8, 118), columns(gu[:, width:], 8, 118)], axis=4)
        arrays[name + "_down"] = rows_first(dn, 8, 118)
    arrays["L3f_wg"] = gates(i["L3_ffn_gate_weight"])

    nc = bacc.Bacc("TRN2", target_bir_lowering=False, num_devices=1)
    feed, aps = {}, {}
    for name, v in arrays.items():
        v = np.ascontiguousarray(v)
        feed["in_" + name] = v
        aps[name] = nc.dram_tensor("in_" + name, v.shape, mybir.dt.from_np(v.dtype), kind="ExternalInput").ap()
    out = nc.dram_tensor("out_x", (T, D), F32, kind="ExternalOutput").ap()
    build(nc, aps, out)
    r = run(nc, [feed], core_ids=[0])
    return r.results[0]["out_x"].reshape(B, TB, D)
```

```python
from contextlib import ExitStack

import concourse.bass as bass
from concourse import mybir

F32 = mybir.dt.float32
BF16 = mybir.dt.bfloat16
F32R = mybir.dt.float32r
I32 = mybir.dt.int32
U32 = mybir.dt.uint32
U8 = mybir.dt.uint8
ALU = mybir.AluOpType
ACT = mybir.ActivationFunctionType
AX_X = mybir.AxisListType.X

P = 128
D = 256
KT = D // P
B = 2
TB = 512
T = B * TB
TT = T // P
TTB = TB // P
SK = 1024
SKT = SK // P
N = 512
E = 8
GROUP = 2
SLOT_TILES = 2 * TT + E
LN_EPS = 1e-5


class Attention:

    def __init__(self, name, groups, nh, nc, scale, bias, mask, fills, packed=False, twice=False):
        self.name, self.groups, self.nh, self.nc = name, groups, nh, nc
        self.rows = P // nh
        self.scale, self.bias, self.mask = scale, bias, mask
        self.packed, self.twice = packed, twice
        self.parted = packed and not twice
        self.steps = TTB * nh
        self.half = self.steps // 2
        self.cols = P * nc
        self.projections = [("Q", c) for c in range(nc)] + [("K", c, n) for c in range(nc) for n in range(SK // N)] \
            + [("V", j) for j in range(SKT * self.cols // N)]
        self.schedule = fills

    def fills(self, kind):
        lag = ("R1", "O0", "O1")
        proj = ("Q", "K", "V")
        out = []
        for s, f in self.schedule:
            if f[0] in lag and kind == "first" or f[0] in proj and kind == "last":
                continue
            out.append((s, f))
        return out

    def index(self, kind, what):
        return [f for _, f in self.fills(kind)].index(what)


def fills_before(att, ph, k):
    kind, loop, c = ph
    n0 = len(att.projections)
    if kind == "first":
        return n0 + k
    full = len(att.fills("mid"))
    base = n0 + len(att.fills("first")) - full
    return count(ph, full, base + k)


def count(ph, per, off):
    _, loop, c = ph
    if loop is None:
        return per * c + off
    return loop * (2 * per) + (per * c + off)


PAIR = [(0, ("O0",)), (1, ("Q", 0)), (1, ("R1",)), (2, ("K", 0, 0)), (3, ("K", 0, 1)), (4, ("O1",)),
        (5, ("V", 0)), (6, ("V", 1)), (6, ("R0",))]
QUAD = [(0, ("Q", 0)), (1, ("O0",)), (3, ("R1",)), (4, ("K", 0, 0)), (6, ("K", 0, 1)), (8, ("V", 0)), (9, ("O1",)), (11, ("R0",)), (13, ("V", 1))]
SINGLE = [(0, ("O0",)), (0, ("Q", 0)), (0, ("R1",)), (0, ("Q", 1)), (1, ("K", 0, 0)), (1, ("K", 0, 1)),
          (1, ("K", 1, 0)), (1, ("K", 1, 1)), (2, ("O1",)), (2, ("V", 0)), (2, ("R0",)), (2, ("V", 1)),
          (3, ("V", 2)), (3, ("V", 3))]


def build(nc, a, out):
    ctx = ExitStack()
    with ctx:
        def sb(name, shape, dt=F32, where=ctx):
            return where.enter_context(nc.sbuf_tensor(name, shape, dt))

        def sem(name):
            return ctx.enter_context(nc.semaphore(name))

        psum = ctx.enter_context(nc.psum_tensor("psum", [P, 8, N], F32))
        pool_of_sems, lately_used = {}, []

        def shared(name):
            if name not in pool_of_sems:
                pool_of_sems[name] = sem(name)
            lately_used.append(pool_of_sems[name])
            return pool_of_sems[name]

        def clear_shared():
            with nc.Block() as block:
                @block.sync
                def _(sp):
                    for s in lately_used:
                        sp.sem_clear(s)
            lately_used.clear()

        bank = [psum[:, i, :] for i in range(8)]
        x = sb("x", [P, TT, D])
        xn = sb("xn", [P, TT, D])
        xnT = sb("xnT", [P, KT, T])
        ctxT = sb("ctxT", [P, KT, B * SK])
        ident = sb("ident", [P, P])
        iota = sb("iota", [P, E])
        weights = sb("weights", [P, 3, TT])
        put = sb("put", [P, 2, TT], I32)
        take = sb("take", [P, 2, TT], I32)
        tile_start = sb("tile_start", [P, E + 1], I32)
        zeros = sb("zeros", [P, D])
        rows_i = sb("rows_i", [P, TT], I32)
        token_no = sb("token_no", [P, TT])
        below = sb("below", [P, P])
        ones = sb("ones", [P, P])
        x_loaded = sem("x_loaded")
        ctx_loaded = [sem(f"ctx_loaded{b}") for b in range(B)]
        ident_made = sem("ident_made")
        x_stored = sem("x_stored")
        spare = sem("spare")
        zeros_made = sem("zeros_made")
        slots_cleared = sem("slots_cleared")
        by_slot = nc.dram_tensor("by_slot", (SLOT_TILES * P, D), F32, kind="Internal").ap()
        result_by_slot = nc.dram_tensor("result_by_slot", (SLOT_TILES * P, D), F32, kind="Internal").ap()

        with nc.Block() as block:
            @block.sync
            def _(sp):
                sp.dma_start(x[:], a["x"].rearrange("(j p) d -> p j d", p=P)).then_inc(x_loaded, 16)

            @block.gpsimd
            def _(pool):
                nc.gpsimd.memset(zeros[:], 0.0).then_inc(zeros_made, 1)
                nc.gpsimd.memset(ident[:], 0.0).then_inc(ident_made, 1)
                pool.wait_ge(ident_made, 1)
                nc.gpsimd.affine_select(out=ident[:], in_=ident[:], compare_op=ALU.not_equal, fill=1.0,
                                        base=0, pattern=[[-1, P]], channel_multiplier=1).then_inc(ident_made, 1)
                for e in range(E):
                    nc.gpsimd.memset(iota[:, e:e + 1], float(e)).then_inc(ident_made, 1)
                nc.gpsimd.memset(ones[:], 1.0).then_inc(ident_made, 1)
                nc.gpsimd.iota(rows_i[:], pattern=[[P, TT]], base=0, channel_multiplier=1).then_inc(ident_made, 1)
                pool.wait_ge(ident_made, 4 + E)
                nc.gpsimd.affine_select(out=below[:], in_=ones[:], compare_op=ALU.is_gt, fill=0.0,
                                        base=0, pattern=[[1, P]], channel_multiplier=-1).then_inc(ident_made, 1)
                nc.gpsimd.tensor_copy(token_no[:], rows_i[:]).then_inc(ident_made, 1)
                pool.wait_ge(ident_made, 6 + E)

            @block.vector
            def _(dve):
                dve.wait_ge(x_loaded, 16)

        def first_loads(sp):
            for b in range(B):
                sp.dma_start(ctxT[:, :, b * SK:(b + 1) * SK], a["ctxT"].rearrange("(k p) t -> p k t", p=P)
                             [:, :, b * SK:(b + 1) * SK]).then_inc(ctx_loaded[b], 16)
            sp.wait_ge(zeros_made, 1)
            for rows in (by_slot, result_by_slot):
                sp.dma_start(rows.rearrange("(g p) d -> p g d", p=P),
                             zeros[:].unsqueeze(1).to_broadcast([P, SLOT_TILES, D])).then_inc(slots_cleared, 16)

        norms = {"calls": 0, "chain": 0, "bo": 0}
        ln_chain = sem("ln_chain")
        ln_bo_loaded = sem("ln_bo_loaded")
        ln_var_ready = sem("ln_var_ready")
        ln_sd_ready = sem("ln_sd_ready")
        ln_xn_ready = sem("ln_xn_ready")
        ln_tr_ready = sem("ln_tr_ready")
        ln_transposed = sem("ln_transposed")

        def layer_norm(name, bo=None, early=None, beside=None):
            n = norms["calls"]
            norms["calls"] += 1
            with ExitStack() as own:
                stats = sb(name + "_stats", [P, TT, 6], F32, own)
                mv = sb(name + "_mv", [P, TT, 2], F32, own)
                ve = sb(name + "_ve", [P, TT], F32, own)
                sd = sb(name + "_sd", [P, TT], F32, own)
                r0 = sb(name + "_r0", [P, TT], F32, own)
                sd_early = sb(name + "_sd_early", [P, 1], F32, own)
                w = sb(name + "_w", [P, TT], F32, own)
                bo_all = sb(name + "_bo", [P, D], F32, own)
                with nc.Block() as block:
                    @block.sync
                    def _(sp):
                        if bo is not None:
                            norms["bo"] += 1
                            sp.dma_start(bo_all[:], a[bo].partition_broadcast(P)).then_inc(ln_bo_loaded, 16)
                        if early:
                            early(sp)

                    @block.vector
                    def _(dve):
                        def link(ins):
                            norms["chain"] += 1
                            ins.then_inc(ln_chain, 1)
                            dve.wait_ge(ln_chain, norms["chain"])

                        for j in range(TT):
                            last = nc.vector.bn_stats(stats[:, j, :], x[:, j, :])
                        link(last)
                        for j in range(TT):
                            last = nc.vector.bn_aggr(mv[:, j, :], stats[:, j, :])
                        link(last)
                        nc.vector.tensor_scalar(ve[:], mv[:, :, 1], LN_EPS, None, ALU.add).then_inc(ln_var_ready, 1)
                        dve.wait_ge(ln_sd_ready, n + 1)
                        link(nc.vector.reciprocal(r0[:], sd[:]))
                        link(nc.vector.tensor_tensor(w[:], r0[:], r0[:], ALU.mult))
                        link(nc.vector.tensor_tensor(w[:], w[:], ve[:], ALU.mult))
                        link(nc.vector.tensor_scalar(w[:], w[:], -0.5, 1.5, ALU.mult, ALU.add))
                        link(nc.vector.tensor_tensor(r0[:], r0[:], w[:], ALU.mult))
                        for j in range(TT):
                            nc.vector.tensor_scalar(xn[:, j, :], x[:, j, :], mv[:, j, 0:1], r0[:, j:j + 1],
                                                    ALU.subtract, ALU.mult).then_inc(ln_xn_ready, 1)
                        if bo is not None:
                            dve.wait_ge(ln_bo_loaded, 16 * norms["bo"])
                            dve.wait_ge(ln_xn_ready, (n + 1) * TT)
                            link(nc.vector.tensor_tensor(x[:], x[:], bo_all[:].unsqueeze(1).to_broadcast([P, TT, D]),
                                                         ALU.add))
                        for k in range(KT):
                            dve.wait_ge(ln_tr_ready, 2 * KT * n + 2 * k + 2)
                            nc.vector.tensor_copy(xnT[:, k, N:2 * N], bank[2 * k + 1][:, :]).then_inc(ln_transposed, 1)

                    @block.scalar
                    def _(act):
                        if beside:
                            beside[0](act)
                        act.wait_ge(ident_made, 3 + E)
                        nc.scalar.activation(sd_early[:], ones[:, 0:1], ACT.Sqrt)
                        act.wait_ge(ln_var_ready, n + 1)
                        nc.scalar.activation(sd[:], ve[:], ACT.Sqrt).then_inc(ln_sd_ready, 1)
                        for k in range(KT):
                            act.wait_ge(ln_tr_ready, 2 * KT * n + 2 * k + 1)
                            nc.scalar.copy(xnT[:, k, 0:N], bank[2 * k][:, :]).then_inc(ln_transposed, 1)

                    @block.tensor
                    def _(pe):
                        if beside:
                            beside[1](pe)
                        pe.wait_ge(ident_made, 2)
                        for k in range(KT):
                            for h in range(2):
                                for j in range(4):
                                    if k == 0:
                                        pe.wait_ge(ln_xn_ready, n * TT + 4 * h + j + 1)
                                    last = nc.tensor.transpose(bank[2 * k + h][:, j * P:(j + 1) * P],
                                                               xn[:, 4 * h + j, k * P:(k + 1) * P], ident[:])
                                last.then_inc(ln_tr_ready, 1)

        def attention(att, norm, bo=None, first=False, early=None):
            nm = att.name
            nh, ncc, rows, steps, half, cols = att.nh, att.nc, att.rows, att.steps, att.half, att.cols
            G = att.groups
            kpb = N // cols
            loads = 3 if att.bias else 1
            own = ExitStack()
            with own:
                wqkv = sb(nm + "_wqkv", [P, KT, 3 * cols], F32, own)
                wo = sb(nm + "_wo", [P, ncc, D], F32, own)
                if att.bias:
                    bqk = sb(nm + "_bqk", [P, 2 * ncc], F32, own)
                    bv = sb(nm + "_bv", [P, cols], F32, own)
                w_loaded = shared("att_w_loaded")
                wo_loaded = shared("att_wo_loaded")
                wqk_loaded = shared("att_wqk_loaded")
                w_high = shared("att_w_high")
                w_split = shared("att_w_split")
                qk_cols, v_cols = slice(0, 2 * cols), slice(2 * cols, 3 * cols)

                def load_w(sp, g):
                    if att.parted:
                        sp.dma_start(wqkv[:, :, v_cols], a[nm + "_wqkv"][g][:, :, v_cols]).then_inc(w_loaded, 16)
                    else:
                        sp.dma_start(wqkv[:], a[nm + "_wqkv"][g]).then_inc(w_loaded, 16)
                    if att.bias:
                        sp.dma_start(bqk[:], a[nm + "_bqk"][g]).then_inc(w_loaded, 16)
                        sp.dma_start(bv[:], a[nm + "_bv"][g].partition_broadcast(P)).then_inc(w_loaded, 16)

                def load_wqk(sp, g):
                    sp.dma_start(wqkv[:, :, qk_cols], a[nm + "_wqkv"][g][:, :, qk_cols]).then_inc(wqk_loaded, 16)

                def first_of_all(sp):
                    if att.parted:
                        load_wqk(sp, 0)
                    load_w(sp, 0)
                    sp.dma_start(wo[:], a[nm + "_wo"][0]).then_inc(wo_loaded, 16)
                    if first:
                        first_loads(sp)
                    if early:
                        early(sp)

                layer_norm(norm, bo=bo, early=first_of_all)
                if att.packed:
                    Q = sb(nm + "_Q", [P, B, nh, TB], F32R, own)
                    K = sb(nm + "_K", [P, B, 1 if att.twice else nh, 2, SK], F32R, own)
                    q_raw = sb(nm + "_q_raw", [P, TB], F32, own)
                    k_raw = sb(nm + "_k_raw", [P, SK], F32, own)
                    if att.twice:
                        q_near = sb(nm + "_q_near", [P, TB], F32R, own)
                        q_off = sb(nm + "_q_off", [P, TB], F32, own)
                        low_row = sb(nm + "_low_row", [P, 1], F32, own)
                        low_row_i = sb(nm + "_low_row_i", [P, 1], I32, own)
                    else:
                        q_low = sb(nm + "_q_low", [P, TB], F32R, own)
                else:
                    Q = sb(nm + "_Q", [P, B, max(nh, ncc), TB], F32, own)
                    K = sb(nm + "_K", [P, B, ncc, SK], F32, own)
                if att.parted:
                    xs = [sb(nm + "_x" + part, [P, KT, T], F32R, own) for part in ("_high", "_low")]
                    cs = [sb(nm + "_ctx" + part, [P, KT, B * SK], F32R, own) for part in ("_high", "_low")]
                    ws = [sb(nm + "_w" + part, [P, KT, 2 * cols], F32R, own) for part in ("_high", "_low")]
                own_rows = [slice(h * rows, (h + 1) * rows) for h in range(nh)]
                other_rows = own_rows[::-1]
                copies = 16 * 2 * (1 + SK // N)
                V = sb(nm + "_V", [P, B, SKT, cols], F32, own)
                prob = sb(nm + "_prob", [P, 2, SK], F32, own)
                probT = sb(nm + "_probT", [P, 2, nh, SKT, 2 * P], F32, own)
                negmax = sb(nm + "_negmax", [P, steps], F32, own)
                sums = sb(nm + "_sums", [P, steps], F32, own)
                recip = sb(nm + "_recip", [P, 2, nh], F32, own)
                rexp = sb(nm + "_rexp", [P, 2, nh, rows], F32, own)
                rall = sb(nm + "_rall", [P, 2 * P], F32, own)
                OT = sb(nm + "_OT", [P, ncc, 2 * P], F32, own)
                if att.mask:
                    masked = prob if att.twice else sb(nm + "_masked", [P, 2, SK], F32, own)
                    top = sb(nm + "_top", [P, steps], F32, own)
                if att.mask == "add":
                    mraw = xn[:].bitcast(U8)
                    mbias = sb(nm + "_mbias", [P, B * TTB, SK], BF16, own)
                if att.mask == "select":
                    mraw = sb(nm + "_mraw", [P, B * TTB, SK], I32, own)
                    keep = sb(nm + "_keep", [P, SK], F32, own)
                    mbias = sb(nm + "_mbias", [P, SK], F32, own)
                x_high = shared("att_x_high")
                x_split = shared("att_x_split")
                k_high = shared("att_k_high")
                q_high = shared("att_q_high")
                low_row_made = shared("att_low_row_made")
                near_ready = shared("att_near_ready")
                low_chain = shared("att_low_chain")
                qk_split = shared("att_qk_split")
                qk_copied = shared("att_qk_copied")
                mask_loaded = shared("att_mask_loaded")
                mask_made = shared("att_mask_made")
                q_zeroed = shared("att_q_zeroed")
                scores_ready = shared("att_scores_ready")
                max_ready = shared("att_max_ready")
                dve_chain = shared("att_dve_chain")
                prob_ready = shared("att_prob_ready")
                tr_ready = shared("att_tr_ready")
                evac_act = shared("att_evac_act")
                evac_dve = shared("att_evac_dve")
                fill_ready = shared("att_fill_ready")
                fill_taken = shared("att_fill_taken")
                pv_ready = shared("att_pv_ready")
                o_taken = shared("att_o_taken")
                recip_ready = shared("att_recip_ready")
                rsum_ready = shared("att_rsum_ready")
                S = [(bank[0], bank[1]), (bank[2], bank[3])]
                SPAN = [psum[:, 0:2, :].rearrange("p a n -> p (a n)"), psum[:, 2:4, :].rearrange("p a n -> p (a n)")]
                TR = (bank[4], bank[5])
                OB = bank[6]
                FB = bank[7]
                scores_free = max_ready if att.mask else prob_ready

                def phases(run, eng):
                    run(("first", None, 0), 0)
                    if G > 1:
                        with eng.Fori(0, G - 1) as i:
                            run(("mid", i, 1), 1)
                            run(("mid", i, 2), 0)
                    run(("last", None, 2 * G - 1), 1)

                block = own.enter_context(nc.Block())

                @block.sync
                def _(sp):
                    if att.mask:
                        for b in range(B):
                            sp.dma_start(mraw[:, b * TTB:(b + 1) * TTB, :],
                                         a[nm + "_mask"][b].rearrange("(j p) s -> p j s", p=P)).then_inc(mask_loaded, 16)
                    def copy_rows(b, n_split):
                        sp.wait_ge(qk_split, n_split(1))
                        for h in range(nh):
                            sp.dma_start(Q[other_rows[h], b, h, :].bitcast(F32), q_low[own_rows[h], :].bitcast(F32)).then_inc(qk_copied, 16)
                        for n in range(SK // N):
                            sp.wait_ge(qk_split, n_split(n + 2))
                            for h in range(nh):
                                part = K[:, b, h, :, n * N:(n + 1) * N].bitcast(F32)
                                sp.dma_start(part[other_rows[h]], part[own_rows[h]]).then_inc(qk_copied, 16)

                    if att.packed and not att.twice:
                        sp.wait_ge(w_split, 1)
                        load_wqk(sp, 1)
                        copy_rows(0, lambda i: i)

                        def phase(ph, b):
                            kind = ph[0]
                            if kind != "last":
                                copy_rows(1 - b, lambda i: count(ph, 3, 3 + i))
                            if kind == "mid" and ph[2] == 2:
                                sp.wait_ge(fill_taken, fills_before(att, ph, att.index(kind, ("O1",)) + 1))
                                sp.dma_start(wo[:], a[nm + "_wo"][ph[1] + 1]).then_inc(wo_loaded, 16)
                            if kind == "first" or kind == "mid" and ph[2] == 2:
                                sp.wait_ge(fill_taken, fills_before(att, ph, att.index(kind, ("V", 1)) + 1))
                                g = 1 if kind == "first" else ph[1] + 2
                                load_w(sp, g)
                                sp.wait_ge(w_split, g + 1)
                                load_wqk(sp, g + 1)

                        phases(phase, sp)
                        sp.wait_ge(w_loaded, 16 * loads * (G + 1))
                        sp.wait_ge(wqk_loaded, 16 * (G + 2))
                    elif G > 1:
                        lastv = ("V", len([f for f in att.projections if f[0] == "V"]) - 1)
                        ph = ("first", None, 0)
                        sp.wait_ge(fill_taken, fills_before(att, ph, att.index("first", lastv)) + 1)
                        load_w(sp, 1)

                        def load_wo(ph, g):
                            sp.wait_ge(fill_taken, fills_before(att, ph, att.index("mid", ("O1",)) + 1))
                            sp.dma_start(wo[:], a[nm + "_wo"][g]).then_inc(wo_loaded, 16)
                        if G > 2:
                            with sp.Fori(0, G - 2) as i:
                                ph = ("mid", i, 2)
                                load_wo(ph, i + 1)
                                sp.wait_ge(fill_taken, fills_before(att, ph, att.index("mid", lastv) + 1))
                                load_w(sp, i + 2)
                        load_wo(("mid", None, 2 * G - 2), G - 1)

                @block.tensor
                def _(pe):
                    def by_parts(w_cols, rhs, rhs_cols):
                        for kt in range(KT):
                            for n, (i, j) in enumerate([(0, 0), (0, 1), (1, 0)]):
                                last = nc.tensor.matmul(FB[:, :], ws[i][:, kt, w_cols], rhs[j][:, kt, rhs_cols],
                                                        start=(kt == 0 and n == 0), stop=(kt == KT - 1 and n == 2))
                        return last

                    def fill(ph, f, k, b):
                        if k is None:
                            before = att.projections.index(f)
                        else:
                            before = fills_before(att, ph, k)
                        if k is not None or before:
                            pe.wait_ge(fill_taken, before)
                        kind = f[0]
                        if kind == "Q":
                            if att.parted and k is None:
                                pe.wait_ge(w_split, 1)
                                pe.wait_ge(x_split, KT)
                            elif att.parted and ph[0] == "mid" and ph[2] == 1:
                                pe.wait_ge(w_split, ph[1] + 2)
                            if f[1] == 0:
                                if k is None:
                                    pe.wait_ge(w_loaded, 16 * loads)
                                    pe.wait_ge(ctx_loaded[0], 16)
                                elif ph[0] == "first":
                                    pe.wait_ge(ctx_loaded[1], 16)
                                elif ph[0] == "mid" and ph[2] == 1:
                                    pe.wait_ge(w_loaded, ph[1] * (16 * loads) + 32 * loads)
                            if att.parted:
                                last = by_parts(slice(0, cols), xs, slice(b * TB, (b + 1) * TB))
                            for kt in range(0 if att.parted else KT):
                                last = nc.tensor.matmul(FB[:, :], wqkv[:, kt, f[1] * P:(f[1] + 1) * P],
                                                        xnT[:, kt, b * TB:(b + 1) * TB],
                                                        start=(kt == 0), stop=(kt == KT - 1))
                        elif kind == "K":
                            if att.parted:
                                if k is None or ph[0] == "first":
                                    pe.wait_ge(x_split, KT * (2 + b))
                                last = by_parts(slice(cols, 2 * cols), cs,
                                                slice(b * SK + f[2] * N, b * SK + (f[2] + 1) * N))
                            for kt in range(0 if att.parted else KT):
                                last = nc.tensor.matmul(FB[:, :], wqkv[:, kt, cols + f[1] * P:cols + (f[1] + 1) * P],
                                                        ctxT[:, kt, b * SK + f[2] * N:b * SK + (f[2] + 1) * N],
                                                        start=(kt == 0), stop=(kt == KT - 1))
                        elif kind == "V":
                            for i in range(kpb):
                                t = f[1] * kpb + i
                                for kt in range(KT):
                                    last = nc.tensor.matmul(FB[:, i * cols:(i + 1) * cols],
                                                            ctxT[:, kt, b * SK + t * P:b * SK + (t + 1) * P],
                                                            wqkv[:, kt, 2 * cols:3 * cols],
                                                            start=(kt == 0), stop=(kt == KT - 1))
                        elif kind in ("R0", "R1"):
                            h = int(kind[1])
                            pe.wait_ge(rsum_ready, count(ph, 2, h + 1 if h == 0 else 0))
                            for q in range(2):
                                last = nc.tensor.matmul(FB[:, q * P:(q + 1) * P],
                                                        rexp[:, q].rearrange("p h r -> p (h r)"), ident[:],
                                                        start=True, stop=True)
                        else:
                            h = int(kind[1])
                            pe.wait_ge(o_taken, count(ph, 2, h - 1))
                            if h == 0:
                                if ph[0] == "mid" and ph[2] == 1:
                                    pe.wait_ge(wo_loaded, ph[1] * 16 + 16)
                                elif ph[0] == "last":
                                    pe.wait_ge(wo_loaded, 16 * G)
                            for q in range(2):
                                for c in range(ncc):
                                    last = nc.tensor.matmul(FB[:, q * D:(q + 1) * D], OT[:, c, q * P:(q + 1) * P],
                                                            wo[:, c, :], start=(c == 0), stop=(c == ncc - 1))
                        last.then_inc(fill_ready, 1)

                    def scores(ph, s, b):
                        t, h = s // nh, s % nh
                        for n in range(SK // N):
                            for part in range(2 if att.packed else 0):
                                last = nc.tensor.matmul(S[s % 2][n][:, :], Q[:, b, h, t * P:(t + 1) * P],
                                                        K[:, b, 0 if att.twice else h, part, n * N:(n + 1) * N],
                                                        start=(part == 0), stop=(part == 1))
                            for c in range(0 if att.packed else ncc):
                                lhs = Q[:, b, c if ncc > 1 else h, t * P:(t + 1) * P]
                                last = nc.tensor.matmul(S[s % 2][n][:, :], lhs, K[:, b, c, n * N:(n + 1) * N],
                                                        start=(c == 0), stop=(c == ncc - 1))
                        last.then_inc(scores_ready, 1)

                    def pv(ph, hf, b, part, parts):
                        if ncc == 1:
                            todo = [(kt, h, 0) for kt in range(SKT) for h in range(nh)]
                        else:
                            todo = [(kt, 0, c) for c in range(ncc) for kt in range(SKT)]
                        m = len(todo) // parts
                        for kt, h, c in todo[part * m:(part + 1) * m]:
                            o = OB[h * rows:(h + 1) * rows, c * 2 * P:(c + 1) * 2 * P]
                            last = nc.tensor.matmul(o, V[:, b, kt, (h * rows if ncc == 1 else c * P):
                                                              ((h + 1) * rows if ncc == 1 else (c + 1) * P)],
                                                    probT[:, hf, h, kt, :], start=(kt == 0), stop=(kt == SKT - 1))
                        if part == parts - 1:
                            last.then_inc(pv_ready, 1)

                    def pv_waits(ph, hf):
                        pe.wait_ge(evac_act, count(ph, steps, half * (hf + 1)))
                        pe.wait_ge(evac_dve, count(ph, steps, half * (hf + 1)))
                        if not (ph[0] == "first" and hf == 0):
                            pe.wait_ge(o_taken, count(ph, 2, hf))

                    def before(ph):
                        return (ph[0], ph[1], ph[2] - 1)

                    def transposes(ph, s):
                        pe.wait_ge(prob_ready, count(ph, steps, s + 1))
                        for i in range(2):
                            if not (ph[0] == "first" and s == 0):
                                pe.wait_ge(evac_dve if i else evac_act, count(ph, steps, s))
                            for j in range(4):
                                kt = 4 * i + j
                                last = nc.tensor.transpose(TR[i][:, j * P:(j + 1) * P],
                                                           prob[:, s % 2, kt * P:(kt + 1) * P], ident[:])
                            last.then_inc(tr_ready, 1)

                    def phase(ph, b):
                        kind = ph[0]
                        fl = att.fills(kind)
                        for s in range(steps):
                            if s + 1 < steps:
                                if not (kind == "first" and s == 0):
                                    pe.wait_ge(scores_free, count(ph, steps, s))
                                scores(ph, s + 1, b)
                            elif kind != "last":
                                pe.wait_ge(scores_free, count(ph, steps, s))
                                if att.twice:
                                    pe.wait_ge(qk_split, count(ph, 3, 6))
                                elif att.packed:
                                    pe.wait_ge(qk_copied, count(ph, copies, 2 * copies))
                                else:
                                    pe.wait_ge(fill_taken, fills_before(att, ph, att.index(kind, ("K", ncc - 1, 1)) + 1))
                                scores(ph, 0, 1 - b)
                            now = [(k, f) for k, (fs, f) in enumerate(fl) if fs == s]
                            cut = len(now) // 2 if len(now) > 1 else len(now)
                            for k, f in now[:cut]:
                                fill(ph, f, k, 1 - b)
                            if s < half:
                                if kind != "first":
                                    if s == 0:
                                        pv_waits(before(ph), 1)
                                    pv(ph, 1, 1 - b, s, half)
                            else:
                                if s == half:
                                    pv_waits(ph, 0)
                                pv(ph, 0, b, s - half, half)
                            for k, f in now[cut:]:
                                fill(ph, f, k, 1 - b)
                            transposes(ph, s)

                    if not att.packed or att.twice:
                        pe.wait_ge(q_zeroed, 1)
                    for f in att.projections:
                        fill(None, f, None, 0)
                    pe.wait_ge(fill_taken, len(att.projections))
                    if att.twice:
                        pe.wait_ge(qk_split, 3)
                    elif att.packed:
                        pe.wait_ge(qk_copied, copies)
                    scores(None, 0, 0)
                    phases(phase, pe)
                    end = ("mid", None, 2 * G)
                    n0 = len(att.projections) + len(att.fills("first")) + (2 * G - 2) * len(att.fills("mid")) \
                        + len(att.fills("last"))
                    for k, f in enumerate((("R1",), ("O0",), ("O1",))):
                        if k == 2:
                            pv_waits(("last", None, 2 * G - 1), 1)
                            pv(end, 1, 1, 0, 1)
                        pe.wait_ge(fill_taken, n0 + k)
                        h = int(f[0][1])
                        if k == 0:
                            pe.wait_ge(rsum_ready, 4 * G)
                            for q in range(2):
                                last = nc.tensor.matmul(FB[:, q * P:(q + 1) * P],
                                                        rexp[:, q].rearrange("p h r -> p (h r)"), ident[:],
                                                        start=True, stop=True)
                        else:
                            pe.wait_ge(o_taken, 4 * G - 1 + h)
                            for q in range(2):
                                for c in range(ncc):
                                    last = nc.tensor.matmul(FB[:, q * D:(q + 1) * D], OT[:, c, q * P:(q + 1) * P],
                                                            wo[:, c, :], start=(c == 0), stop=(c == ncc - 1))
                        last.then_inc(fill_ready, 1)

                tail_fills = len(att.projections) + len(att.fills("first")) + (2 * G - 2) * len(att.fills("mid")) \
                    + len(att.fills("last"))

                @block.scalar
                def _(act):
                    def take(f, n, b):
                        act.wait_ge(fill_ready, n)
                        if f[0] == "K" and att.packed:
                            cut = slice(f[2] * N, (f[2] + 1) * N)
                            if att.bias:
                                nc.scalar.activation(k_raw[:, cut], FB[:, :], ACT.Identity,
                                                     bias=bqk[:, 1:2]).then_inc(fill_taken, 1)
                            else:
                                nc.scalar.copy(k_raw[:, cut], FB[:, :]).then_inc(fill_taken, 1)
                            act.wait_ge(fill_taken, n)
                            for h, r in enumerate([slice(0, P)] if att.twice else own_rows):
                                last = nc.scalar.copy(K[r, b, h, 0, cut], k_raw[r, cut])
                            last.then_inc(k_high, 1)
                        elif f[0] == "K":
                            dst = K[:, b, f[1], f[2] * N:(f[2] + 1) * N]
                            if att.bias:
                                nc.scalar.activation(dst, FB[:, :], ACT.Identity,
                                                     bias=bqk[:, ncc + f[1]:ncc + f[1] + 1]).then_inc(fill_taken, 1)
                            else:
                                nc.scalar.copy(dst, FB[:, :]).then_inc(fill_taken, 1)
                        else:
                            nc.scalar.copy(rall[:], FB[:, 0:2 * P]).then_inc(fill_taken, 1)

                    def exps(ph, s, off):
                        act.wait_ge(max_ready, count(ph, steps, off + 1))
                        if not (ph[0] == "first" and off < 2):
                            act.wait_ge(tr_ready, count(ph, 2 * steps, 2 * off - 2))
                        src = masked[:, s % 2, :] if att.mask else None
                        if att.mask:
                            nc.scalar.activation(prob[:, s % 2, :], src, ACT.Exp, bias=negmax[:, s:s + 1],
                                                 accum_out=sums[:, s:s + 1]).then_inc(prob_ready, 1)
                        else:
                            nc.scalar.activation(prob[:, s % 2, :], SPAN[s % 2], ACT.Exp, bias=negmax[:, s:s + 1],
                                                 accum_out=sums[:, s:s + 1]).then_inc(prob_ready, 1)

                    def phase(ph, b):
                        kind = ph[0]
                        fl = att.fills(kind)
                        for s in range(steps):
                            if s + 1 < steps:
                                exps(ph, s + 1, s + 1)
                            elif kind != "last":
                                exps(ph, 0, steps)
                            for k, (fs, f) in enumerate(fl):
                                if fs == s and f[0] in ("K", "R0", "R1"):
                                    if f[0][0] == "R":
                                        if kind != "first":
                                            act.wait_ge(o_taken, count(ph, 2, 0 if f[0] == "R0" else -1))
                                    take(f, fills_before(att, ph, k + 1), 1 - b)
                            hf, h, q = s // half, s % nh, s // nh % 2
                            act.wait_ge(tr_ready, count(ph, 2 * steps, 2 * s + 1))
                            if s % half == 0 and kind != "first":
                                act.wait_ge(pv_ready, count(ph, 2, hf - 1))
                            nc.scalar.copy(probT[:, hf, h, 0:4, q * P:(q + 1) * P],
                                           TR[0][:, :].rearrange("p (k q) -> p k q", q=P)).then_inc(evac_act, 1)

                    def high_parts(dst, src, lo, hi):
                        for kt in range(KT):
                            nc.scalar.copy(dst[0][:, kt, lo:hi], src[:, kt, lo:hi]).then_inc(x_high, 1)

                    if att.parted:
                        high_parts(xs, xnT, 0, T)
                        act.wait_ge(ctx_loaded[0], 16)
                        high_parts(cs, ctxT, 0, SK)
                    for n, f in enumerate(att.projections):
                        if f[0] == "K":
                            take(f, n + 1, 0)
                    if att.parted:
                        act.wait_ge(ctx_loaded[1], 16)
                        high_parts(cs, ctxT, SK, 2 * SK)
                    exps(("first", None, 0), 0, 0)
                    phases(phase, act)
                    act.wait_ge(o_taken, 4 * G - 1)
                    take(("R1",), tail_fills + 1, 1)

                @block.vector
                def _(dve):
                    if att.twice:
                        dve.wait_ge(low_row_made, 1)
                        nc.vector.tensor_scalar(low_row_i[:], low_row_i[:], 4, 1, ALU.logical_shift_right,
                                                ALU.bitwise_and).then_inc(low_row_made, 1)
                        dve.wait_ge(low_row_made, 2)
                        nc.vector.tensor_copy(low_row[:], low_row_i[:]).then_inc(low_row_made, 1)
                        dve.wait_ge(low_row_made, 3)
                        nc.vector.memset(Q[:].bitcast(F32), 0.0).then_inc(q_zeroed, 1)
                        dve.wait_ge(q_zeroed, 1)
                    elif att.packed:
                        pass
                    elif ncc == 1:
                        nc.vector.memset(Q[:], 0.0).then_inc(q_zeroed, 1)
                        dve.wait_ge(q_zeroed, 1)
                    else:
                        nc.vector.memset(sums[:], 0.0).then_inc(q_zeroed, 1)
                        dve.wait_ge(q_zeroed, 1)
                    if att.mask == "add":
                        dve.wait_ge(mask_loaded, 16 * B)
                        for j in range(B * TTB):
                            nc.vector.tensor_scalar(mbias[:, j, :], mraw[:, j, :], 0.0, -1e15,
                                                    ALU.not_equal, ALU.mult).then_inc(mask_made, 1)
                        dve.wait_ge(mask_made, B * TTB)

                    def maxes(ph, s, off, b):
                        if att.mask == "select":
                            j = b * TTB + s
                            if j:
                                dve.wait_ge(max_ready, j)
                            else:
                                dve.wait_ge(mask_loaded, 16 * B)
                            nc.vector.tensor_scalar(keep[:], mraw[:, j, :], 0.0, None, ALU.not_equal).then_inc(mask_made, 1)
                            nc.vector.tensor_scalar(mbias[:], mraw[:, j, :], 0.0, -1e9,
                                                    ALU.is_equal, ALU.mult).then_inc(mask_made, 1)
                            dve.wait_ge(mask_made, 2 * j + 2)
                        dve.wait_ge(scores_ready, count(ph, steps, off + 1))
                        if not att.mask:
                            nc.vector.tensor_reduce(negmax[:, s:s + 1], SPAN[s % 2], AX_X, ALU.max,
                                                    negate=True).then_inc(max_ready, 1)
                            return
                        if not (ph[0] == "first" and off < 2):
                            if att.twice:
                                dve.wait_ge(tr_ready, count(ph, 2 * steps, 2 * off - 2))
                            else:
                                dve.wait_ge(prob_ready, count(ph, steps, off - 1))
                        src, mb = SPAN[s % 2], None
                        if att.mask == "select":
                            nc.vector.tensor_tensor(masked[:, s % 2, :], src, keep[:], ALU.mult).then_inc(dve_chain, 1)
                            dve.wait_ge(dve_chain, count(ph, 2 * steps, 2 * off + 1))
                            src, mb = masked[:, s % 2, :], mbias[:]
                        else:
                            mb = mbias[:, b * TTB + s // nh, :]
                        dve.sem_inc(spare, 1)
                        nc.vector.tensor_tensor_reduce(masked[:, s % 2, :], src, mb, 1.0, -3e38, ALU.add, ALU.max,
                                                       top[:, s:s + 1]).then_inc(dve_chain, 1)
                        per = 2 if att.mask == "select" else 1
                        dve.wait_ge(dve_chain, count(ph, per * steps, per * (off + 1)))
                        nc.vector.tensor_scalar(negmax[:, s:s + 1], top[:, s:s + 1], -1.0, None,
                                                ALU.mult).then_inc(max_ready, 1)

                    dve_takes = ("Q", "V", "O0", "O1")

                    def take_q(n, b, n_near):
                        if att.bias:
                            nc.vector.tensor_scalar(q_raw[:], FB[:, :], bqk[:, 0:1], att.scale,
                                                    ALU.add, ALU.mult).then_inc(fill_taken, 1)
                        else:
                            nc.vector.tensor_scalar(q_raw[:], FB[:, :], att.scale, None, ALU.mult).then_inc(fill_taken, 1)
                        dve.wait_ge(fill_taken, n)
                        if att.twice:
                            nc.vector.tensor_copy(q_near[:], q_raw[:]).then_inc(near_ready, 1)
                            dve.wait_ge(near_ready, n_near)
                            last = nc.vector.tensor_scalar(q_off[:], q_near[:], low_row[:, 0:1], None, ALU.mult)
                        for h, r in enumerate([] if att.twice else own_rows):
                            last = nc.vector.tensor_copy(Q[r, b, h, :], q_raw[r, :])
                        last.then_inc(q_high, 1)

                    def take(f, n, b, ph=None):
                        dve.wait_ge(fill_ready, n)
                        if f[0] == "Q" and att.packed:
                            take_q(n, b, 1 if ph is None else count(ph, 1, 2))
                        elif f[0] == "Q":
                            for h in range(nh):
                                r = slice(h * rows, (h + 1) * rows)
                                dst = Q[r, b, h if ncc == 1 else f[1], :]
                                if att.bias:
                                    last = nc.vector.tensor_scalar(dst, FB[r, :], bqk[r, f[1]:f[1] + 1], att.scale,
                                                                   ALU.add, ALU.mult)
                                else:
                                    last = nc.vector.tensor_scalar(dst, FB[r, :], att.scale, None, ALU.mult)
                            last.then_inc(fill_taken, 1)
                        elif f[0] == "V":
                            dst = V[:, b, f[1] * kpb:(f[1] + 1) * kpb, :]
                            src = FB[:, :].rearrange("p (k c) -> p k c", c=cols)
                            if att.bias:
                                nc.vector.tensor_tensor(dst, src, bv[:].unsqueeze(1).to_broadcast([P, kpb, cols]),
                                                        ALU.add).then_inc(fill_taken, 1)
                            else:
                                nc.vector.tensor_copy(dst, src).then_inc(fill_taken, 1)
                        else:
                            j = b * TTB + 2 * int(f[0][1])
                            nc.vector.tensor_tensor(x[:, j:j + 2, :], x[:, j:j + 2, :],
                                                    FB[:, :].rearrange("p (q d) -> p q d", d=D),
                                                    ALU.add).then_inc(fill_taken, 1)

                    def reciprocals(ph, hf, done):
                        dve.wait_ge(prob_ready, done)
                        s0 = hf * half
                        src = sums[:, s0:s0 + half].rearrange("p (q h) -> p q h", h=nh)
                        nc.vector.reciprocal(recip[:], src).then_inc(recip_ready, 1)

                    def normalise(n_pv, n_fill):
                        dve.wait_ge(pv_ready, n_pv)
                        dve.wait_ge(fill_taken, n_fill)
                        if ncc == 1:
                            nc.vector.tensor_tensor(OT[:, 0, :], OB[:, 0:2 * P], rall[:], ALU.mult).then_inc(o_taken, 1)
                        else:
                            nc.vector.tensor_tensor(OT[:], OB[:, :].rearrange("p (c q) -> p c q", c=ncc),
                                                    rall[:].unsqueeze(1).to_broadcast([P, ncc, 2 * P]),
                                                    ALU.mult).then_inc(o_taken, 1)

                    def phase(ph, b):
                        kind = ph[0]
                        fl = att.fills(kind)
                        names = [f for _, f in fl]
                        for s in range(steps):
                            if s == 0 and kind != "first":
                                reciprocals(ph, 1, count(ph, steps, 0))
                            if s == half:
                                reciprocals(ph, 0, count(ph, steps, half))
                            if s + 1 < steps:
                                maxes(ph, s + 1, s + 1, b)
                            elif kind != "last":
                                maxes(ph, 0, steps, 1 - b)
                            for k, (fs, f) in enumerate(fl):
                                if fs == s and f[0] in dve_takes:
                                    take(f, fills_before(att, ph, k + 1), 1 - b, ph)
                            if s == half - 1 and kind != "first":
                                normalise(count(ph, 2, 0), fills_before(att, ph, names.index(("R1",)) + 1))
                            if s == steps - 1:
                                normalise(count(ph, 2, 1), fills_before(att, ph, names.index(("R0",)) + 1))
                            hf, h, q = s // half, s % nh, s // nh % 2
                            dve.wait_ge(tr_ready, count(ph, 2 * steps, 2 * s + 2))
                            if s % half == 0 and kind != "first":
                                dve.wait_ge(pv_ready, count(ph, 2, hf - 1))
                            nc.vector.tensor_copy(probT[:, hf, h, 4:8, q * P:(q + 1) * P],
                                                  TR[1][:, :].rearrange("p (k q) -> p k q", q=P)).then_inc(evac_dve, 1)

                    def low_parts(done, parts, src, lo, hi):
                        for kt in range(KT):
                            dve.wait_ge(x_high, done + kt + 1)
                            nc.vector.tensor_tensor(parts[1][:, kt, lo:hi], src[:, kt, lo:hi], parts[0][:, kt, lo:hi],
                                                    ALU.subtract).then_inc(x_split, 1)

                    if att.parted:
                        low_parts(0, xs, xnT, 0, T)
                        low_parts(KT, cs, ctxT, 0, SK)
                    for n, f in enumerate(att.projections):
                        if f[0] in dve_takes:
                            take(f, n + 1, 0)
                    if att.parted:
                        low_parts(2 * KT, cs, ctxT, SK, 2 * SK)
                    maxes(("first", None, 0), 0, 0, 0)
                    phases(phase, dve)
                    reciprocals(("last", None, 2 * G), 1, 2 * G * steps)
                    take(("O0",), tail_fills + 2, 1)
                    normalise(4 * G, tail_fills + 1)
                    take(("O1",), tail_fills + 3, 1)

                @block.gpsimd
                def _(pool):
                    def spread(n):
                        pool.wait_ge(recip_ready, n)
                        pool.sem_inc(spare, 1)
                        nc.gpsimd.tensor_copy(rexp[:], recip[:].unsqueeze(3).to_broadcast([P, 2, nh, rows])
                                              ).then_inc(rsum_ready, 1)

                    def lows(b, n):
                        for i in range(1 + SK // N):
                            if i == 0:
                                pool.wait_ge(q_high, n(1, 1))
                            else:
                                pool.wait_ge(k_high, n(2, i))
                            cut = slice((i - 1) * N, i * N)
                            for h, r in enumerate([slice(0, P)] if att.twice and i else own_rows):
                                if i == 0:
                                    dst, high = (Q[r, b, h, :], q_off[r, :]) if att.twice else (q_low[r, :], Q[r, b, h, :])
                                    last = nc.gpsimd.tensor_tensor(dst, q_raw[r, :], high, ALU.subtract)
                                else:
                                    last = nc.gpsimd.tensor_tensor(K[r, b, h, 1, cut], k_raw[r, cut],
                                                                   K[r, b, h, 0, cut], ALU.subtract)
                                if att.twice and i == 0 and h + 1 < nh:
                                    last.then_inc(low_chain, 1)
                                    pool.wait_ge(low_chain, n(3, h + 1))
                                elif not att.twice and h == 0:
                                    last.then_inc(low_chain, 1)
                                    pool.wait_ge(low_chain, n(3, i + 1))
                            last.then_inc(qk_split, 1)
                            pool.wait_ge(qk_split, n(3, i + 1))

                    def split_w(g):
                        pool.wait_ge(wqk_loaded, g * 16 + 16)
                        pool.sem_inc(spare, 1)
                        nc.gpsimd.tensor_copy(ws[0][:], wqkv[:, :, qk_cols]).then_inc(w_high, 1)
                        pool.wait_ge(w_high, g + 1)
                        nc.gpsimd.tensor_tensor(ws[1][:], wqkv[:, :, qk_cols], ws[0][:], ALU.subtract).then_inc(w_split, 1)

                    def phase(ph, b):
                        if ph[0] != "first":
                            spread(count(ph, 2, 0))
                        if att.packed and ph[0] != "last":
                            lows(1 - b, lambda per, off: count(ph, per, per + off))
                        spread(count(ph, 2, 1))
                        if att.parted and ph[0] == "first":
                            split_w(1)
                        elif att.parted and ph[0] == "mid" and ph[2] == 2:
                            split_w(ph[1] + 2)

                    if att.parted:
                        split_w(0)
                    if att.twice:
                        nc.gpsimd.iota(low_row_i[:], pattern=[[1, 1]], base=0, channel_multiplier=1).then_inc(low_row_made, 1)
                    if att.packed:
                        lows(0, lambda per, off: off)
                    phases(phase, pool)
                    spread(4 * G)

        def route(name, norm, mode, eps=0.0, bias=False, b2=None, early=None, beside=None):
            choices = 2 if mode == "top2" else 1
            with ExitStack() as own:
                wg = sb(name + "_wg_sb", [P, KT, E], F32, own)
                gb = sb(name + "_gb", [P, E], F32, own)
                b2_sb = sb(name + "_b2", [E, D], F32, own)
                loaded = shared("route_loaded")

                def load_gates(sp):
                    sp.dma_start(wg[:], a[name + "_wg"]).then_inc(loaded, 16)
                    if bias:
                        sp.dma_start(gb[:], a[name + "_gb"].partition_broadcast(P)).then_inc(loaded, 16)
                    if b2:
                        sp.dma_start(b2_sb[:], a[b2]).then_inc(loaded, 16)
                    if early:
                        early(sp)

                layer_norm(norm, early=load_gates)
                lg = sb(name + "_lg", [P, TT, E], F32, own)
                top = sb(name + "_top", [P, TT, 8], F32, own)
                place = sb(name + "_place", [P, TT, 8], U32, own)
                placef = sb(name + "_placef", [P, TT, 8], F32, own)
                ex = sb(name + "_ex", [P, TT, E], F32, own)
                total = sb(name + "_total", [P, TT], F32, own)
                diff = sb(name + "_diff", [P, TT], F32, own)
                second = sb(name + "_second", [P, TT], F32, own)
                w0, w1 = weights[:, 0, :], weights[:, 1, :]
                hot = sb(name + "_hot", [P, choices, TT, E], F32, own)
                both = sb(name + "_both", [P, TT, E], F32, own)
                tile_sum = sb(name + "_tile_sum", [P, TT, E], F32, own)
                ahead = sb(name + "_ahead", [P, TT, E], F32, own)
                place_of = sb(name + "_place_of", [P, TT, E], F32, own)
                expert_sum = sb(name + "_expert_sum", [P, E], F32, own)
                more = sb(name + "_more", [P, E, E - 1], F32, own)
                bounds = sb(name + "_bounds", [P, E - 1], F32, own)
                tiles_of = sb(name + "_tiles_of", [P, E], F32, own)
                first_tile = sb(name + "_first_tile", [P, E + 1], F32, own)
                first_slot = sb(name + "_first_slot", [P, E], F32, own)
                slot = sb(name + "_slot", [P, TT], F32, own)
                if mode == "argmax":
                    start_of = sb(name + "_start_of", [P, E + 1], F32, own)
                    beyond = sb(name + "_beyond", [P, TT, E + 1], F32, own)
                    comb = sb(name + "_comb", [P, TT, E], F32, own)
                    combT = sb(name + "_combT", [E, T], F32, own)
                logits_ready = shared("route_logits")
                chain = shared("route_chain")
                shifted = shared("route_shifted")
                exps_ready = shared("route_exps")
                hot_ready = shared("route_hot_ready")
                counted = shared("route_counted")
                comb_ready = shared("route_comb")
                combT_ready = shared("route_combT_ready")
                combT_taken = shared("route_combT_taken")
                row_ready = shared("route_row_ready")
                row_taken = shared("route_row_taken")
                with nc.Block() as block:
                    @block.vector
                    def _(dve):
                        done = [0]

                        def link(ins):
                            done[0] += 1
                            ins.then_inc(chain, 1)
                            dve.wait_ge(chain, done[0])

                        def per_token(v):
                            return v.unsqueeze(2).to_broadcast([P, TT, E])

                        def per_expert(v):
                            return v.unsqueeze(1).to_broadcast([P, TT, E])

                        dve.wait_ge(logits_ready, 1)
                        src = bank[0][:, 0:TT * E].rearrange("p (j e) -> p j e", e=E)
                        if bias:
                            link(nc.vector.tensor_tensor(lg[:], src, per_expert(gb[:]), ALU.add))
                        else:
                            link(nc.vector.tensor_copy(lg[:], src))
                        for j in range(TT):
                            last = nc.vector.max(top[:, j, :], lg[:, j, :])
                        link(last)
                        for j in range(TT):
                            last = nc.vector.max_index(place[:, j, :], top[:, j, :], lg[:, j, :])
                        link(last)
                        nc.vector.tensor_tensor(lg[:], lg[:], per_token(top[:, :, 0]), ALU.subtract).then_inc(shifted, 1)
                        nc.vector.tensor_tensor(diff[:], top[:, :, 1], top[:, :, 0], ALU.subtract).then_inc(shifted, 1)
                        link(nc.vector.tensor_copy(placef[:], place[:]))
                        for c in range(choices):
                            link(nc.vector.tensor_tensor(hot[:, c], per_expert(iota[:]), per_token(placef[:, :, c]),
                                                         ALU.is_equal))
                        if choices == 2:
                            nc.vector.tensor_tensor(both[:], hot[:, 0], hot[:, 1], ALU.add).then_inc(hot_ready, 1)
                        else:
                            nc.vector.tensor_copy(both[:], hot[:, 0]).then_inc(hot_ready, 1)
                        dve.wait_ge(exps_ready, 2)
                        link(nc.vector.tensor_reduce(total[:], ex[:], AX_X, ALU.add))
                        if mode == "top2":
                            link(nc.vector.scalar_tensor_tensor(out=w1, in0=total[:], scalar=eps, in1=second[:],
                                                                op0=ALU.mult, op1=ALU.add))
                            link(nc.vector.tensor_scalar(w1, w1, 1.0, None, ALU.add))
                            link(nc.vector.reciprocal(w0, w1))
                            link(nc.vector.tensor_tensor(w1, w0, second[:], ALU.mult))
                            nc.vector.tensor_tensor(weights[:, 2, :], w0, w1, ALU.add)
                        else:
                            link(nc.vector.reciprocal(w0, total[:]))
                            for j in range(TT):
                                nc.vector.tensor_scalar(xn[:, j, :], xn[:, j, :], w0[:, j:j + 1], None, ALU.mult)
                        link(nc.vector.tensor_scalar(bounds[:], iota[:, 1:E], float(P), None, ALU.mult))
                        dve.wait_ge(counted, 1)
                        link(nc.vector.tensor_copy(tile_sum[:], bank[2][:, 0:TT * E].rearrange("p (j e) -> p j e", e=E)))
                        link(nc.vector.tensor_copy(ahead[:], bank[1][:, 0:TT * E].rearrange("p (j e) -> p j e", e=E)))
                        link(nc.vector.tensor_reduce(expert_sum[:], tile_sum[:].rearrange("p j e -> p e j"),
                                                     AX_X, ALU.add))
                        link(nc.vector.tensor_tensor(more[:], expert_sum[:].unsqueeze(2).to_broadcast([P, E, E - 1]),
                                                     bounds[:].unsqueeze(1).to_broadcast([P, E, E - 1]), ALU.is_gt))
                        link(nc.vector.tensor_reduce(tiles_of[:], more[:], AX_X, ALU.add))
                        link(nc.vector.tensor_scalar(tiles_of[:], tiles_of[:], 1.0, None, ALU.add))
                        link(nc.vector.memset(first_tile[:, 0:1], 0.0))
                        for e in range(E):
                            link(nc.vector.tensor_tensor(first_tile[:, e + 1:e + 2], first_tile[:, e:e + 1],
                                                         tiles_of[:, e:e + 1], ALU.add))
                        link(nc.vector.tensor_copy(tile_start[:], first_tile[:]))
                        link(nc.vector.tensor_scalar(first_slot[:], first_tile[:, 0:E], float(P), None, ALU.mult))
                        for j in range(2, TT):
                            link(nc.vector.tensor_tensor(tile_sum[:, j - 1, :], tile_sum[:, j - 1, :],
                                                         tile_sum[:, j - 2, :], ALU.add))
                        link(nc.vector.tensor_tensor(ahead[:, 1:, :], ahead[:, 1:, :], tile_sum[:, 0:TT - 1, :],
                                                     ALU.add))
                        link(nc.vector.tensor_tensor(ahead[:], ahead[:], per_expert(first_slot[:]), ALU.add))
                        for c in range(choices):
                            link(nc.vector.tensor_tensor(place_of[:], ahead[:], hot[:, c], ALU.mult))
                            link(nc.vector.tensor_reduce(slot[:], place_of[:], AX_X, ALU.add))
                            link(nc.vector.tensor_copy(put[:, c, :], slot[:]))
                            if mode == "top2":
                                link(nc.vector.tensor_copy(take[:, c, :], slot[:]))
                        if mode == "argmax":
                            link(nc.vector.memset(start_of[:, 0:1], 0.0))
                            for e in range(E):
                                link(nc.vector.tensor_tensor(start_of[:, e + 1:e + 2], start_of[:, e:e + 1],
                                                             expert_sum[:, e:e + 1], ALU.add))
                            link(nc.vector.tensor_tensor(beyond[:], token_no[:].unsqueeze(2).to_broadcast([P, TT, E + 1]),
                                                         start_of[:].unsqueeze(1).to_broadcast([P, TT, E + 1]),
                                                         ALU.is_ge))
                            nc.vector.tensor_tensor(comb[:], beyond[:, :, 0:E], beyond[:, :, 1:],
                                                    ALU.subtract).then_inc(comb_ready, 1)
                            link(nc.vector.tensor_tensor(first_slot[:], first_slot[:], start_of[:, 0:E], ALU.subtract))
                            dve.wait_ge(comb_ready, 1)
                            link(nc.vector.tensor_tensor(place_of[:], comb[:], per_expert(first_slot[:]), ALU.mult))
                            link(nc.vector.tensor_reduce(slot[:], place_of[:], AX_X, ALU.add))
                            link(nc.vector.tensor_tensor(slot[:], slot[:], token_no[:], ALU.add))
                            link(nc.vector.tensor_copy(take[:, 0, :], slot[:]))
                            for h in range(2):
                                dve.wait_ge(combT_ready, h + 1)
                                nc.vector.tensor_copy(combT[:, h * N:(h + 1) * N], bank[1 + h][0:E, :]
                                                      ).then_inc(combT_taken, 1)
                            for n in range(TT):
                                dve.wait_ge(row_ready, n + 1)
                                nc.vector.tensor_tensor(x[:, n, :], x[:, n, :], bank[5 + n % 3][:, 0:D],
                                                        ALU.add).then_inc(row_taken, 1)

                    @block.scalar
                    def _(act):
                        if beside:
                            beside[0](act)
                        act.wait_ge(shifted, 2)
                        nc.scalar.activation(ex[:], lg[:], ACT.Exp).then_inc(exps_ready, 1)
                        nc.scalar.activation(second[:], diff[:], ACT.Exp).then_inc(exps_ready, 1)

                    @block.gpsimd
                    def _(pool):
                        if beside:
                            beside[1](pool)

                    @block.tensor
                    def _(pe):
                        pe.wait_ge(loaded, 16 * (1 + bias + bool(b2)))
                        for j in range(TT):
                            for k in range(KT):
                                last = nc.tensor.matmul(bank[0][:, j * E:(j + 1) * E], xnT[:, k, j * P:(j + 1) * P],
                                                        wg[:, k, :], start=(k == 0), stop=(k == KT - 1))
                        last.then_inc(logits_ready, 1)
                        pe.wait_ge(hot_ready, 1)
                        hots = both[:].rearrange("p j e -> p (j e)")
                        nc.tensor.matmul(bank[1][:, 0:TT * E], below[:], hots, start=True, stop=True)
                        nc.tensor.matmul(bank[2][:, 0:TT * E], ones[:], hots, start=True, stop=True).then_inc(counted, 1)
                        if mode == "argmax":
                            pe.wait_ge(comb_ready, 1)
                            for j in range(TT):
                                last = nc.tensor.transpose(bank[1 + j // 4][0:E, (j % 4) * P:(j % 4 + 1) * P],
                                                           comb[:, j, :], ident[:])
                                if j % 4 == 3:
                                    last.then_inc(combT_ready, 1)
                            pe.wait_ge(combT_taken, 2)
                            for n in range(TT):
                                if n >= 3:
                                    pe.wait_ge(row_taken, n - 2)
                                nc.tensor.matmul(bank[5 + n % 3][:, 0:D], combT[:, n * P:(n + 1) * P], b2_sb[:],
                                                 start=True, stop=True).then_inc(row_ready, 1)

        def split_weights(name, tiles, hid, mats, own, until_split):
            up = [sb(name + "_up" + part, [P, tiles, KT, mats, hid], F32R, own) for part in ("_high", "_low")]
            down = [sb(name + "_down" + part, [hid, tiles, D], F32R, own) for part in ("_high", "_low")]
            up_raw = sb(name + "_up_raw", [P, tiles, KT, mats, hid], F32, until_split)
            down_raw = sb(name + "_down_raw", [hid, tiles, D], F32, until_split)
            loaded = [shared(f"ff_loaded{i}") for i in range(2)]
            w_high = shared("ff_w_high")
            w_split = shared("ff_w_split")

            def parts(n):
                raw, part, t = (up_raw, up, n) if n < tiles else (down_raw, down, n - tiles)
                return raw[:, t], part[0][:, t], part[1][:, t]

            def load(sp):
                sp.dma_start(up_raw[:], a[name + "_up"][0]).then_inc(loaded[0], 16)
                sp.dma_start(down_raw[:], a[name + "_down"][0]).then_inc(loaded[1], 16)

            def high(act):
                for n in range(2 * tiles):
                    if n % tiles == 0:
                        act.wait_ge(loaded[n // tiles], 16)
                    raw, part, _ = parts(n)
                    nc.scalar.copy(part, raw).then_inc(w_high, 1)

            def low(pool):
                for n in range(2 * tiles):
                    pool.wait_ge(w_high, n + 1)
                    raw, part, rest = parts(n)
                    nc.gpsimd.tensor_tensor(rest, raw, part, ALU.subtract).then_inc(w_split, 1)

            return up, down, load, high, low

        def feed_forward(name, tiles, hid, gated, func, up, down, bias=False, beside=None, making=None):
            mats = 2 if gated else 1
            NB = 2 if gated else 4
            pairs = [(0, 0), (0, 1)] + [(1, 0)] * (len(up) - 1)
            own = ExitStack()
            with own:
                b1 = sb(name + "_b1_sb", [hid, tiles], F32, own) if bias else None
                xs = [sb(name + "_x_high", [P, KT, N], F32R, own), sb(name + "_x_low", [P, KT, N], F32R, own)]
                gate_act = sb(name + "_gate_act", [hid, 2, N], F32, own) if gated else None
                value = sb(name + "_value", [hid, 2, N], F32, own)
                hidden = [sb(name + "_hidden_high", [hid, tiles, N], F32R, own),
                          sb(name + "_hidden_low", [hid, tiles, N], F32R, own)]
                b1_loaded = shared("ff_b1_loaded")
                x_high = shared("ff_x_high")
                x_split = shared("ff_x_split")
                up_ready = shared("ff_up_ready")
                gate_ready = shared("ff_gate_ready")
                value_ready = shared("ff_value_ready")
                hidden_high = shared("ff_hidden_high")
                hidden_ready = shared("ff_hidden_ready")
                down_ready = shared("ff_down_ready")
                down_taken = shared("ff_down_taken")
                block = own.enter_context(nc.Block())

                @block.sync
                def _(sp):
                    if bias:
                        sp.dma_start(b1[:], a[name + "_b1"][0]).then_inc(b1_loaded, 16)
                    if beside:
                        beside[1](sp)

                @block.gpsimd
                def _(pool):
                    if beside:
                        beside[0](pool)

                @block.tensor
                def _(pe):
                    for h in range(2):
                        pe.wait_ge(x_split, KT * (h + 1))
                        for t in range(tiles):
                            n = h * tiles + t
                            if making and h == 0:
                                pe.wait_ge(making[3], t * making[0] // tiles + 1)
                            if n >= NB:
                                pe.wait_ge(value_ready, n - NB + 1)
                            for m in range(mats):
                                for k in range(KT):
                                    for c, (i, j) in enumerate(pairs):
                                        last = nc.tensor.matmul(bank[(n % NB) * mats + m][0:hid, :],
                                                                up[i][:, t, k, m, :], xs[j][:, k, :],
                                                                start=(k == 0 and c == 0),
                                                                stop=(k == KT - 1 and c == len(pairs) - 1))
                            last.then_inc(up_ready, 1)
                        if making and h == 0:
                            pe.wait_ge(making[3], 2 * making[0])
                        pe.wait_ge(hidden_ready, (h + 1) * tiles)
                        for q in range(4):
                            n = h * 4 + q
                            if n >= 4:
                                pe.wait_ge(down_taken, n - 3)
                            for t in range(tiles):
                                for c, (i, j) in enumerate(pairs):
                                    last = nc.tensor.matmul(bank[4 + q][:, 0:D], hidden[j][:, t, q * P:(q + 1) * P],
                                                            down[i][:, t, :], start=(t == 0 and c == 0),
                                                            stop=(t == tiles - 1 and c == len(pairs) - 1))
                            last.then_inc(down_ready, 1)

                @block.scalar
                def _(act):
                    if bias:
                        act.wait_ge(b1_loaded, 16)
                    for h in range(2):
                        if h:
                            act.wait_ge(up_ready, tiles)
                        for k in range(KT):
                            nc.scalar.copy(xs[0][:, k, :], xnT[:, k, h * N:(h + 1) * N]).then_inc(x_high, 1)
                        for t in range(tiles):
                            n = h * tiles + t
                            act.wait_ge(up_ready, n + 1)
                            src = bank[(n % NB) * mats][0:hid, :]
                            if gated:
                                if n >= 2:
                                    act.wait_ge(value_ready, n - 1)
                                nc.scalar.activation(gate_act[:, n % 2, :], src, func).then_inc(gate_ready, 1)
                            else:
                                if n >= 2:
                                    act.wait_ge(hidden_ready, n - 1)
                                if h:
                                    act.wait_ge(down_ready, 4)
                                nc.scalar.activation(value[:, n % 2, :], src, func, bias=b1[:, t:t + 1])
                                nc.scalar.activation(hidden[0][:, t, :], src, func,
                                                     bias=b1[:, t:t + 1]).then_inc(value_ready, 1)

                @block.vector
                def _(dve):
                    if making:
                        pieces, bounds, make, _ = making
                        bounds(dve)
                        make(dve, 0, 0)
                    for h in range(2):
                        for k in range(KT):
                            dve.wait_ge(x_high, KT * h + k + 1)
                            nc.vector.tensor_tensor(xs[1][:, k, :], xnT[:, k, h * N:(h + 1) * N], xs[0][:, k, :],
                                                    ALU.subtract).then_inc(x_split, 1)
                        for piece in range(1, pieces) if making and h == 0 else ():
                            make(dve, 0, piece)
                        for t in range(tiles):
                            n = h * tiles + t
                            if making and h == 0 and t % (tiles // pieces) == 0:
                                make(dve, 1, t * pieces // tiles)
                            if gated:
                                dve.wait_ge(gate_ready, n + 1)
                                if n >= 2:
                                    dve.wait_ge(hidden_ready, n - 1)
                                nc.vector.tensor_tensor(value[:, n % 2, :], bank[(n % NB) * mats + 1][0:hid, :],
                                                        gate_act[:, n % 2, :], ALU.mult).then_inc(value_ready, 1)
                            dve.wait_ge(value_ready, n + 1)
                            if h:
                                dve.wait_ge(down_ready, 4)
                            if gated:
                                nc.vector.tensor_copy(hidden[0][:, t, :], value[:, n % 2, :]).then_inc(hidden_high, 1)
                                dve.wait_ge(hidden_high, n + 1)
                            nc.vector.tensor_tensor(hidden[1][:, t, :], value[:, n % 2, :], hidden[0][:, t, :],
                                                    ALU.subtract).then_inc(hidden_ready, 1)
                        for q in range(4):
                            n = h * 4 + q
                            dve.wait_ge(down_ready, n + 1)
                            nc.vector.tensor_tensor(x[:, n, :], x[:, n, :], bank[4 + q][:, 0:D],
                                                    ALU.add).then_inc(down_taken, 1)

        scattered = sem("ex_scattered")
        gathered = [[sem(f"ex_gathered{c}_{half}") for half in range(2)] for c in range(2)]
        moved = {"scattered": 0, "gathered": [0, 0]}

        def routed_experts(name, kind, tiles, hid, choices, own_down=True, bo=False, shared_expert=None):
            mats = 1 if kind == "relu" else 2
            up_order = {"silu": (0, 1), "glu": (1, 0), "relu": (0,)}[kind]
            half = tiles // 2
            NT = choices * TT + E
            parts = NT // TT
            biased = kind != "silu"
            loads = 1 + own_down + biased
            outer = ExitStack()
            with outer:
                up = sb(name + "_up_sb", [P, 2, tiles, KT, mats, hid], F32, outer)
                down = sb(name + "_down_sb", [hid, 2 if own_down else 1, tiles, D], F32, outer)
                b1 = sb(name + "_b1_sb", [hid, 2, tiles, mats], F32, outer) if biased else None
                sorted_x = sb(name + "_sorted_x", [P, NT, D], F32, outer)
                y = sorted_x
                w_loaded = [shared(f"ex_w_loaded{c}") for c in range(2)]
                fixed_loaded = shared("ex_fixed_loaded")
                scattered_before, gathered_before = moved["scattered"], moved["gathered"][:]
                moved["scattered"] += 16 * choices * TT
                for c in range(choices):
                    moved["gathered"][c] += 16 * TT // 2
                sorted_loaded = [shared(f"ex_sorted_loaded{i}") for i in range(parts)]

                def load_weights(sp, e, c):
                    sp.dma_start(up[:, c], a[name + "_up"][e]).then_inc(w_loaded[c], 16)
                    if own_down:
                        sp.dma_start(down[:, c], a[name + "_down"][e]).then_inc(w_loaded[c], 16)
                    if biased:
                        sp.dma_start(b1[:, c], a[name + "_b1"][e]).then_inc(w_loaded[c], 16)

                def scatter(pool):
                    pool.wait_ge(slots_cleared, 32)
                    for c in range(choices):
                        for j in range(TT):
                            nc.gpsimd.indirect_dma_start(by_slot, bass.IndirectOffsetOnAxis(put[:, c, j:j + 1], 0),
                                                         xn[:, j, :], None).then_inc(scattered, 16)

                def load_sorted(sp):
                    for e in range(2):
                        load_weights(sp, e, e)
                    if bo:
                        sp.dma_start(bo_sb[:], a[name + "_bo"].partition_broadcast(P)).then_inc(fixed_loaded, 16)
                    if not own_down:
                        sp.dma_start(down[:, 0], a[name + "_wo"]).then_inc(fixed_loaded, 16)
                    sp.wait_ge(scattered, scattered_before + 16 * choices * TT)
                    for i in range(parts):
                        sp.dma_start(sorted_x[:, i * TT:(i + 1) * TT, :],
                                     by_slot[i * TT * P:(i + 1) * TT * P, :].rearrange("(j p) d -> p j d", p=P)
                                     ).then_inc(sorted_loaded[i], 16)

                bo_sb = sb(name + "_bo_sb", [P, D], F32, outer) if bo else None
                if shared_expert:
                    shared_expert(scatter, load_sorted)
                sortedT = sb(name + "_sortedT", [P, KT, NT * P], F32, outer)
                gathered_y = sb(name + "_gathered_y", [P, choices, TT, D], F32, outer)
                gate = sb(name + "_gate", [hid, 2, half, P], F32, outer) if mats == 2 else None
                hidden = sb(name + "_hidden", [hid, tiles, P], F32, outer)
                tr_ready = shared("ex_tr_ready")
                evac_act = shared("ex_evac_act")
                evac_dve = shared("ex_evac_dve")
                up_ready = shared("ex_up_ready")
                gate_ready = shared("ex_gate_ready")
                hidden_ready = shared("ex_hidden_ready")
                down_ready = shared("ex_down_ready")
                y_taken = shared("ex_y_taken")
                y_stored = shared("ex_y_stored")
                added = shared("ex_added")
                block = outer.enter_context(nc.Block())

                def over_group(eng, e, before, body, after=None):
                    starts = [eng.value_load(tile_start[0:1, bass.ds(e + c, 1)], min_val=0, max_val=NT)
                              for c in range(GROUP + 1)]
                    for c in range(GROUP):
                        if before:
                            before(c)
                        with eng.Fori(starts[c], starts[c + 1]) as g:
                            body(g, c % 2)
                        if after:
                            after(c)

                def weights_loaded(eng, i):
                    def wait(c):
                        eng.wait_ge(w_loaded[c % 2], i * (16 * loads * GROUP // 2) + 16 * loads * (c // 2 + 1))
                        eng.sem_inc(spare, 1)
                    return wait

                def up_banks(hf):
                    return [bank[2 * hf + m][0:hid, 0:half * P].rearrange("p (t q) -> p t q", q=P) for m in range(2)]

                @block.sync
                def _(sp):
                    def store(g, c):
                        sp.wait_ge(y_taken, g + 2)
                        sp.dma_start(result_by_slot[bass.ds(g * P, P), :],
                                     y[:, bass.ds(g, 1), :].rearrange("p a d -> p (a d)")).then_inc(y_stored, 16)

                    if not shared_expert:
                        load_sorted(sp)
                    with sp.Fori(0, E // GROUP - 1) as i:
                        over_group(sp, GROUP * i, None, store,
                                   lambda c: load_weights(sp, GROUP * i + (c + 2), c % 2))
                    over_group(sp, E - GROUP, None, store)

                @block.gpsimd
                def _(pool):
                    if not shared_expert:
                        scatter(pool)
                    end = pool.value_load(tile_start[0:1, E:E + 1], min_val=E, max_val=NT)
                    pool.wait_ge(y_stored, end * 16)
                    pool.sem_inc(spare, 1)
                    for c in range(choices):
                        for j in range(TT):
                            nc.gpsimd.indirect_dma_start(gathered_y[:, c, j, :], None, result_by_slot,
                                                         bass.IndirectOffsetOnAxis(take[:, c, j:j + 1], 0)
                                                         ).then_inc(gathered[c][j // 4], 16)

                @block.tensor
                def _(pe):
                    for n in range(NT // 4):
                        if n % 2 == 0:
                            pe.wait_ge(sorted_loaded[n // 2], 16)
                        if n >= 2:
                            pe.wait_ge(evac_act, n - 1)
                            pe.wait_ge(evac_dve, n - 1)
                        for k in range(KT):
                            for i in range(4):
                                last = nc.tensor.transpose(bank[2 * (n % 2) + k][:, i * P:(i + 1) * P],
                                                           sorted_x[:, 4 * n + i, k * P:(k + 1) * P], ident[:])
                        last.then_inc(tr_ready, 1)
                    pe.wait_ge(evac_act, NT // 4)
                    pe.wait_ge(evac_dve, NT // 4)
                    if not own_down:
                        pe.wait_ge(fixed_loaded, 16 * (bo + 1))

                    def tile(g, c):
                        for hf in range(2):
                            dst = up_banks(hf)
                            for m in up_order:
                                for t in range(half):
                                    for k in range(KT):
                                        last = nc.tensor.matmul(dst[m][:, t, :], up[:, c, hf * half + t, k, m, :],
                                                                sortedT[:, k, bass.ds(g * P, P)],
                                                                start=(k == 0), stop=(k == KT - 1))
                                last.then_inc(up_ready, 1)
                        pe.wait_ge(y_taken, g + 1)
                        for hf in range(2):
                            pe.wait_ge(hidden_ready, 2 * g + (hf + 1))
                            for t in range(hf * half, hf * half + half):
                                last = nc.tensor.matmul(bank[4][:, 0:D], hidden[:, t, :],
                                                        down[:, c if own_down else 0, t, :],
                                                        start=(t == 0), stop=(t == tiles - 1))
                        last.then_inc(down_ready, 1)

                    with pe.Fori(0, E // GROUP) as i:
                        over_group(pe, GROUP * i, weights_loaded(pe, i), tile)

                @block.scalar
                def _(act):
                    for n in range(NT // 4):
                        act.wait_ge(tr_ready, n + 1)
                        nc.scalar.copy(sortedT[:, 0, n * N:(n + 1) * N], bank[2 * (n % 2)][:, :]).then_inc(evac_act, 1)

                    def tile(g, c):
                        for hf in range(2):
                            act.wait_ge(up_ready, 2 * mats * g + (mats * hf + 1))
                            first, second = up_banks(hf)
                            ts = range(hf * half, hf * half + half)
                            if kind == "silu":
                                nc.scalar.activation(gate[:, hf], first, ACT.Silu).then_inc(gate_ready, 1)
                            for t in ts if kind == "glu" else ():
                                last = nc.scalar.activation(gate[:, hf, t % half, :], second[:, t % half, :],
                                                            ACT.Sigmoid, bias=b1[:, c, t, 1:2])
                            for t in ts if kind == "relu" else ():
                                last = nc.scalar.activation(hidden[:, t, :], first[:, t % half, :], ACT.Relu,
                                                            bias=b1[:, c, t, 0:1])
                            if kind != "silu":
                                last.then_inc(hidden_ready if kind == "relu" else gate_ready, 1)

                    with act.Fori(0, E // GROUP) as i:
                        over_group(act, GROUP * i, weights_loaded(act, i) if biased else None, tile)

                @block.vector
                def _(dve):
                    for n in range(NT // 4):
                        dve.wait_ge(tr_ready, n + 1)
                        nc.vector.tensor_copy(sortedT[:, 1, n * N:(n + 1) * N],
                                              bank[2 * (n % 2) + 1][:, :]).then_inc(evac_dve, 1)
                    dve.sem_inc(y_taken, 1)

                    def tile(g, c):
                        for hf in range(2) if mats == 2 else ():
                            dve.wait_ge(gate_ready, 2 * g + (hf + 1))
                            dve.wait_ge(up_ready, 4 * g + (2 * hf + 2))
                            first, second = up_banks(hf)
                            if kind == "silu":
                                nc.vector.tensor_tensor(hidden[:, hf * half:(hf + 1) * half, :], second, gate[:, hf],
                                                        ALU.mult).then_inc(hidden_ready, 1)
                                continue
                            for t in range(half):
                                last = nc.vector.scalar_tensor_tensor(out=hidden[:, hf * half + t, :],
                                                                      in0=first[:, t, :],
                                                                      scalar=b1[:, c, hf * half + t, 0:1],
                                                                      in1=gate[:, hf, t, :], op0=ALU.add, op1=ALU.mult)
                            last.then_inc(hidden_ready, 1)
                        dve.wait_ge(down_ready, g + 1)
                        nc.vector.tensor_copy(y[:, bass.ds(g, 1), :].rearrange("p a d -> p (a d)"),
                                              bank[4][:, 0:D]).then_inc(y_taken, 1)

                    with dve.Fori(0, E // GROUP) as i:
                        over_group(dve, GROUP * i, weights_loaded(dve, i) if biased else None, tile)
                    if bo:
                        dve.wait_ge(fixed_loaded, 32)
                        for j in range(TT):
                            nc.vector.scalar_tensor_tensor(out=x[:, j, :], in0=bo_sb[:], scalar=weights[:, 2, j:j + 1],
                                                           in1=x[:, j, :], op0=ALU.mult, op1=ALU.add).then_inc(added, 1)
                    n_added = TT if bo else 0
                    for c in range(choices):
                        if n_added:
                            dve.wait_ge(added, n_added)
                        for j in range(TT):
                            if j % 4 == 0:
                                dve.wait_ge(gathered[c][j // 4], gathered_before[c] + 16 * TT // 2)
                            if choices == 2:
                                nc.vector.scalar_tensor_tensor(out=x[:, j, :], in0=gathered_y[:, c, j, :],
                                                               scalar=weights[:, c, j:j + 1], in1=x[:, j, :],
                                                               op0=ALU.mult, op1=ALU.add).then_inc(added, 1)
                            else:
                                nc.vector.tensor_tensor(x[:, j, :], x[:, j, :], gathered_y[:, c, j, :],
                                                        ALU.add).then_inc(added, 1)
                        n_added += TT

        def ternary_weights(raw, loaded, own):
            W, PIECES = raw[0].shape[1], 4
            size = sb("tern_size", [P, W], F32, own)
            ternary = [sb(f"tern{m}", [P, W], F32R, own) for m in range(2)]
            below = sb("tern_below", [P, W // PIECES], F32, own)
            mags = sb("tern_mags", [P, 2], F32, own)
            bound = sb("tern_bound", [P, 2, 2], F32, own)
            chain = sem("tern_chain")
            mags_ready = sem("tern_mags_ready")
            mean_ready = sem("tern_mean_ready")
            made = sem("tern_made")
            done = [0]

            def link(dve, ins):
                done[0] += 1
                ins.then_inc(chain, 1)
                dve.wait_ge(chain, done[0])

            def magnitudes(act):
                act.wait_ge(loaded, 32)
                for m in range(2):
                    if m:
                        act.wait_ge(mags_ready, 1)
                    nc.scalar.activation(size[:], raw[m][:], ACT.Abs, accum_out=mags[:, m:m + 1]).then_inc(mags_ready, 1)

            def mean(pe):
                pe.wait_ge(mags_ready, 2)
                nc.tensor.matmul(bank[7][:, 0:2], ones[:], mags[:], start=True, stop=True).then_inc(mean_ready, 1)

            def bounds(dve):
                dve.wait_ge(mean_ready, 1)
                link(dve, nc.vector.tensor_scalar(bound[:, :, 0], bank[7][:, 0:2], 1.0 / (P * W), 1e-8,
                                                  ALU.mult, ALU.max))
                link(dve, nc.vector.tensor_scalar(bound[:, :, 1], bound[:, :, 0], -0.5, None, ALU.mult))
                link(dve, nc.vector.tensor_scalar(bound[:, :, 0], bound[:, :, 0], 0.5, None, ALU.mult))

            def make(dve, m, piece):
                cut = slice(piece * W // PIECES, (piece + 1) * W // PIECES)
                link(dve, nc.vector.tensor_scalar(below[:], raw[m][:, cut], bound[:, m, 1:2], None, ALU.is_lt))
                nc.vector.scalar_tensor_tensor(out=ternary[m][:, cut], in0=raw[m][:, cut], scalar=bound[:, m, 0:1],
                                               in1=below[:], op0=ALU.is_gt, op1=ALU.subtract).then_inc(made, 1)
                dve.wait_ge(made, m * PIECES + piece + 1)

            return ternary, magnitudes, mean, (PIECES, bounds, make, made)

        PAIRS = dict(nh=2, nc=1, groups=8, fills=PAIR, packed=True)
        attention(Attention("L0", scale=1.0, bias=True, mask=None, **PAIRS), "n0", bo="L0_bo", first=True)
        clear_shared()
        route("L0f", "n1", "top2", eps=1e-9)
        routed_experts("L0f", "glu", tiles=4, hid=P, choices=2, own_down=False, bo=True)
        clear_shared()
        with ExitStack() as l1:
            raw = [sb(name + "_raw", a[name].shape, F32, l1) for name in ("L1f_up", "L1f_down")]
            tern_loaded = sem("tern_loaded")

            def load(sp):
                for m, name in enumerate(("L1f_up", "L1f_down")):
                    sp.dma_start(raw[m][:], a[name]).then_inc(tern_loaded, 16)

            attention(Attention("L1", scale=1 / 16, bias=True, mask="select", nh=1, nc=2, groups=1, fills=SINGLE),
                      "n2", bo="L1_bo", early=load)
            clear_shared()
            (up, down), magnitudes, mean, making = ternary_weights(raw, tern_loaded, l1)
            layer_norm("n3", bo="L1f_b2", beside=(magnitudes, mean))
            feed_forward("L1f", 8, P, False, ACT.Gelu, [up[:].rearrange("p (t k m h) -> p t k m h", t=8, k=KT, m=1)],
                         [down[:].rearrange("p (t d) -> p t d", d=D)], bias=True, making=making)
            clear_shared()
        attention(Attention("L2", scale=1 / 4, bias=True, mask="add", nh=4, nc=1, groups=4, fills=QUAD,
                            packed=True, twice=True), "n4", bo="L2_bo")
        clear_shared()
        route("L2f", "n5", "argmax", bias=True, b2="L2f_b2")
        routed_experts("L2f", "relu", tiles=2, hid=P, choices=1)
        clear_shared()
        attention(Attention("L3", scale=1 / 8, bias=False, mask=None, **PAIRS), "n6")
        clear_shared()
        with ExitStack() as l3:
            with ExitStack() as until_split:
                up, down, load, high, low = split_weights("L3s", 8, 118, 2, l3, until_split)
                route("L3f", "n7", "top2", eps=1e-8, early=load, beside=(high, low))
            routed_experts("L3f", "silu", tiles=8, hid=118, choices=2, shared_expert=lambda *beside:
                           feed_forward("L3s", 8, 118, True, ACT.Silu, up, down, beside=beside))
        clear_shared()

        with nc.Block() as block:
            @block.sync
            def _(sp):
                sp.dma_start(out.rearrange("(j p) d -> p j d", p=P), x[:]).then_inc(x_stored, 16)
                sp.wait_ge(x_stored, 16)





def kernel(**inputs):
    import numpy as np
    import concourse.bacc as bacc
    from concourse.bass_utils import run_bass_kernel_spmd as run

    i = {k: np.asarray(v) for k, v in inputs.items()}

    def grouped(w, groups, heads, rows, head_rows, twice=False):
        per = heads // groups
        w = w.reshape(w.shape[0], groups, per, head_rows)
        if twice:
            w = np.concatenate([w, w], axis=3)
        elif rows != head_rows:
            padded = np.zeros(w.shape[:3] + (rows,), w.dtype)
            padded[..., :head_rows] = w
            w = padded
        return w.transpose(1, 0, 2, 3).reshape(groups, w.shape[0], per * rows)

    def attention_arrays(name, wq, wk, wv, wo, biases, groups, heads, rows):
        dh = wq.shape[1] // heads
        twice = rows == 2 * dh
        g = [grouped(wq, groups, heads, rows, dh, twice), grouped(wk, groups, heads, rows, dh, twice),
             grouped(wv, groups, heads, rows, dh)]
        cols = g[0].shape[2]
        w = np.concatenate(g, axis=2).reshape(groups, KT, P, 3 * cols).transpose(0, 2, 1, 3)
        o = grouped(wo.T, groups, heads, rows, dh).transpose(0, 2, 1).reshape(groups, cols // P, P, D)
        again = (lambda v: np.concatenate([v, v[:2]])) if groups == 8 else (lambda v: v)
        arrays[name + "_wqkv"] = again(w)
        arrays[name + "_wo"] = o.transpose(0, 2, 1, 3)
        if biases:
            q, k, v = (grouped(b[None], groups, heads, rows, dh, twice and n < 2)[:, 0] for n, b in enumerate(biases))
            qk = np.concatenate([q, k], axis=1).reshape(groups, 2 * cols // P, P)
            arrays[name + "_bqk"] = again(qk.transpose(0, 2, 1))
            arrays[name + "_bv"] = again(v)

    arrays = {"x": i["x"].reshape(T, D), "ctxT": i["ctx_1024"].reshape(B * SK, D).T}
    attention_arrays("L0", i["L0_xattn_Wq"].T, i["L0_xattn_Wk"].T, i["L0_xattn_Wv"].T, i["L0_xattn_Wo"].T,
                     [i["L0_xattn_b" + c] for c in "qkv"], 8, 16, 64)
    attention_arrays("L1", i["L1_xattn_Wq"].T, i["L1_xattn_Wk"].T, i["L1_xattn_Wv"].T, i["L1_xattn_Wo"].T,
                     [i["L1_xattn_b" + c] for c in "qkv"], 1, 1, 256)
    attention_arrays("L2", i["L2_xattn_Wq"], i["L2_xattn_Wk"], i["L2_xattn_Wv"], i["L2_xattn_Wo"],
                     [i["L2_xattn_b" + c] for c in "qkv"], 4, 16, 32)
    attention_arrays("L3", i["L3_xattn_Wq"], i["L3_xattn_Wk"], i["L3_xattn_Wv"], i["L3_xattn_Wo"], None, 8, 16, 64)
    for n in range(3):
        arrays[f"L{n}_bo"] = i[f"L{n}_xattn_bo"]
    arrays["L1_mask"] = i["mask_BxSxS2_if1"]
    arrays["L2_mask"] = i["mask_Bx1xSxS2_bk1"][:, 0]

    def columns(w, tiles, rows):
        e = w.shape[0]
        full = np.zeros((e, tiles * rows, D), w.dtype)
        full[:, :w.shape[1]] = w
        return full.reshape(e, tiles, rows, KT, P).transpose(0, 4, 1, 3, 2)

    def rows_first(w, tiles, rows):
        e = w.shape[0]
        full = np.zeros((e, D, tiles * rows), w.dtype)
        full[:, :, :w.shape[2]] = w
        return full.reshape(e, D, tiles, rows).transpose(0, 3, 2, 1)

    def gates(w):
        return w.reshape(E, KT, P).transpose(2, 1, 0)

    w1 = i["L0_ffn_W1"]
    arrays["L0f_wg"] = gates(i["L0_ffn_Wg"])
    arrays["L0f_up"] = np.stack([columns(w1[:, :512], 4, P), columns(w1[:, 512:], 4, P)], axis=4)
    arrays["L0f_b1"] = i["L0_ffn_b1"].reshape(E, 2, 4, P).transpose(0, 3, 2, 1)
    arrays["L0f_wo"] = rows_first(i["L0_ffn_Wo"][None], 4, P)[0]
    arrays["L0f_bo"] = i["L0_ffn_bo"]
    arrays["L1f_up"] = columns(i["L1_ffn_W1"][None], 8, P)[0].reshape(P, 2048)
    arrays["L1f_down"] = rows_first(i["L1_ffn_W2"][None], 8, P)[0].reshape(P, 2048)
    arrays["L1f_b1"] = i["L1_ffn_b1"].reshape(1, 8, P).transpose(0, 2, 1)
    arrays["L1f_b2"] = i["L1_ffn_b2"]
    arrays["L2f_wg"] = gates(i["L2_ffn_Ws"])
    arrays["L2f_gb"] = i["L2_ffn_bs"]
    arrays["L2f_up"] = columns(i["L2_ffn_W1"].transpose(0, 2, 1), 2, P)[:, :, :, :, None]
    arrays["L2f_down"] = rows_first(i["L2_ffn_W2"].transpose(0, 2, 1), 2, P)
    arrays["L2f_b1"] = i["L2_ffn_b1"].reshape(E, 2, P, 1).transpose(0, 2, 1, 3)
    arrays["L2f_b2"] = i["L2_ffn_b2"]
    for name, gu, dn in (("L3s", i["L3_ffn_shared_gate_up"][None], i["L3_ffn_shared_down"][None]),
                         ("L3f", i["L3_ffn_experts_gate_up"], i["L3_ffn_experts_down"])):
        width = dn.shape[2]
        arrays[name + "_up"] = np.stack([columns(gu[:, :width], 8, 118), columns(gu[:, width:], 8, 118)], axis=4)
        arrays[name + "_down"] = rows_first(dn, 8, 118)
    arrays["L3f_wg"] = gates(i["L3_ffn_gate_weight"])

    nc = bacc.Bacc("TRN2", target_bir_lowering=False, num_devices=1)
    feed, aps = {}, {}
    for name, v in arrays.items():
        v = np.ascontiguousarray(v)
        feed["in_" + name] = v
        aps[name] = nc.dram_tensor("in_" + name, v.shape, mybir.dt.from_np(v.dtype), kind="ExternalInput").ap()
    out = nc.dram_tensor("out_x", (T, D), F32, kind="ExternalOutput").ap()
    build(nc, aps, out)
    r = run(nc, [feed], core_ids=[0])
    return r.results[0]["out_x"].reshape(B, TB, D)
```
